# Optimizing a Trainium2 kernel written in Bass

```python
import numpy as np
import jax
import jax.numpy as jnp

def _softmax(x, axis=-1):
    return jax.nn.softmax(x, axis=axis)

def _gelu(x):
    return jax.nn.gelu(x, approximate=True)

def _silu(x):
    return jax.nn.silu(x)

def _sigmoid(x):
    return jax.nn.sigmoid(x)

def _layernorm(x, axis=-1, eps=1e-05):
    m = jnp.mean(x, axis=axis, keepdims=True)
    v = jnp.var(x, axis=axis, keepdims=True)
    return (x - m) / jnp.sqrt(v + eps)

def _scatter_add(tgt, idx, src, axis=0):
    return tgt.at[idx].add(src)

def _segment_sum(src, seg, n):
    return jax.ops.segment_sum(src, seg, n)
kernel_name = 'mk_gnn_ffn_d2_gnn_r16_cb4dab'

def setup_inputs(seed: int=0):
    np.random.seed(seed)
    _w = jnp.asarray

    def _rec_inputs():
        import jax
        import jax.numpy as jnp
        _gk = jax.random.key(seed)
        x = -0.0002117 + 1 * jax.random.normal(jax.random.fold_in(_gk, 1), (6250, 256), jnp.float32)
        _s = jax.random.randint(jax.random.fold_in(_gk, 2), (50000,), 0, 6250, jnp.int32)
        _d = jax.random.randint(jax.random.fold_in(_gk, 3), (50000,), 0, 6250, jnp.int32)
        _loop = jnp.arange(6250, dtype=jnp.int32)
        src = jnp.concatenate([_s, _d, _loop])
        dst = jnp.concatenate([_d, _s, _loop])
        _o = jnp.argsort(dst, stable=True)
        src = src[_o]
        dst = dst[_o]
        return (x, src, dst)
    x, src, dst = _rec_inputs()

    def _L0_gnn_setup():
        import jax, jax.numpy as jnp
        import numpy as np
        N_NODES = 6250
        N_EDGES = 100000
        NFEAT, NHID, NCLASS = (256, 512, 256)

        def _init_params(key):
            ks = jax.random.split(key, 8)
            s = 0.02
            p = {'W1a': jax.random.normal(ks[0], (NFEAT, NHID), jnp.float32) * s, 'b1a': jnp.zeros((NHID,), jnp.float32), 'W1b': jax.random.normal(ks[1], (NHID, NHID), jnp.float32) * s, 'b1b': jnp.zeros((NHID,), jnp.float32), 'W2a': jax.random.normal(ks[2], (NHID, NHID), jnp.float32) * s, 'b2a': jnp.zeros((NHID,), jnp.float32), 'W2b': jax.random.normal(ks[3], (NHID, NCLASS), jnp.float32) * s, 'b2b': jnp.zeros((NCLASS,), jnp.float32), 'eps1': jnp.zeros((), jnp.float32), 'eps2': jnp.zeros((), jnp.float32)}
            return p

        def _gin_agg(h, src, dst, eps, n_nodes):
            agg = jax.ops.segment_sum(h[src], dst, num_segments=n_nodes)
            return (1.0 + eps) * h + agg
        key = jax.random.key(seed)
        kx, ke, kp = jax.random.split(key, 3)
        x = jax.random.normal(kx, (N_NODES, NFEAT), jnp.float32)
        edge_index = jax.random.randint(ke, (2, N_EDGES), 0, N_NODES, jnp.int64)
        inp = {'x': x, 'edge_index': edge_index}
        inp.update(_init_params(kp))
        return inp
    _L0_gnn_all = _L0_gnn_setup()
    _L0_gnn_in = {k: v for k, v in _L0_gnn_all.items() if k in ('W1a', 'b1a', 'W1b', 'b1b', 'W2a', 'b2a', 'W2b', 'b2b', 'eps1', 'eps2')}
    del _L0_gnn_all

    def _L0_ffn_setup():
        import jax, jax.numpy as jnp
        import numpy as np
        DIM = 256
        H = 8
        D = 64
        G = 64
        INNER = H * D
        SCALE = D ** (-0.5)
        key = jax.random.key(seed)
        ks = jax.random.split(key, 12)
        B, N = (4, 1024)
        x = jax.random.normal(ks[0], (B, N, DIM), dtype=jnp.float32)
        s = lambda fan_in: 1.0 / np.sqrt(fan_in)
        W_fx = jax.random.normal(ks[1], (DIM, INNER), dtype=jnp.float32) * s(DIM)
        b_fx = jnp.zeros((INNER,), dtype=jnp.float32)
        W_x = jax.random.normal(ks[2], (DIM, INNER), dtype=jnp.float32) * s(DIM)
        b_x = jnp.zeros((INNER,), dtype=jnp.float32)
        A = jax.random.normal(ks[3], (G, D), dtype=jnp.float32)
        Q, _ = jnp.linalg.qr(A.T)
        W_slice = Q[:, :G].astype(jnp.float32)
        b_slice = jnp.zeros((G,), dtype=jnp.float32)
        W_q = jax.random.normal(ks[4], (D, D), dtype=jnp.float32) * s(D)
        W_k = jax.random.normal(ks[5], (D, D), dtype=jnp.float32) * s(D)
        W_v = jax.random.normal(ks[6], (D, D), dtype=jnp.float32) * s(D)
        W_out = jax.random.normal(ks[7], (INNER, DIM), dtype=jnp.float32) * s(INNER)
        b_out = jnp.zeros((DIM,), dtype=jnp.float32)
        temperature = jnp.ones((1, H, 1, 1), dtype=jnp.float32) * 0.5
        return {'x': x, 'W_fx': W_fx, 'b_fx': b_fx, 'W_x': W_x, 'b_x': b_x, 'W_slice': W_slice, 'b_slice': b_slice, 'W_q': W_q, 'W_k': W_k, 'W_v': W_v, 'W_out': W_out, 'b_out': b_out, 'temperature': temperature}
    _L0_ffn_all = _L0_ffn_setup()
    _L0_ffn_in = {k: v for k, v in _L0_ffn_all.items() if k in ('W_fx', 'b_fx', 'W_x', 'b_x', 'W_slice', 'b_slice', 'W_q', 'W_k', 'W_v', 'W_out', 'b_out', 'temperature')}
    del _L0_ffn_all

    def _L1_gnn_setup():
        import jax, jax.numpy as jnp
        import numpy as np
        BN_EPS = 1e-05
        key = jax.random.key(seed)
        ks = jax.random.split(key, 4)
        N, E, D_IN, D_OUT = (3125, 50000, 256, 256)
        x = jax.random.normal(ks[0], (N, D_IN), dtype=jnp.float32)
        edge_index = jax.random.randint(ks[1], (2, E), 0, N, dtype=jnp.int64)
        W = jax.random.normal(ks[2], (D_IN, D_OUT), dtype=jnp.float32) * (1.0 / np.sqrt(D_IN))
        b = jnp.zeros((D_OUT,), dtype=jnp.float32)
        gamma = jnp.ones((D_OUT,), dtype=jnp.float32)
        beta = jnp.zeros((D_OUT,), dtype=jnp.float32)
        running_mean = jnp.zeros((D_OUT,), dtype=jnp.float32)
        running_var = jnp.ones((D_OUT,), dtype=jnp.float32)
        return {'x': x, 'edge_index': edge_index, 'W': W, 'b': b, 'gamma': gamma, 'beta': beta, 'running_mean': running_mean, 'running_var': running_var}
    _L1_gnn_all = _L1_gnn_setup()
    _L1_gnn_in = {k: v for k, v in _L1_gnn_all.items() if k in ('W', 'b', 'gamma', 'beta', 'running_mean', 'running_var')}
    del _L1_gnn_all

    def _L1_ffn_setup():
        import jax, jax.numpy as jnp
        import numpy as np
        D_MODEL = 256
        EXPERT_DIM = 512
        NUM_EXPERTS = 8
        TOP_K = 2
        SEQ_LEN = 128
        BATCH = 2
        key = jax.random.key(seed)
        ks = jax.random.split(key, 8)
        s = 0.02
        x = jax.random.normal(ks[0], (SEQ_LEN, BATCH, D_MODEL), dtype=jnp.float32)
        Wg = jax.random.normal(ks[1], (D_MODEL, NUM_EXPERTS), dtype=jnp.float32) * s
        bg = jax.random.normal(ks[2], (NUM_EXPERTS,), dtype=jnp.float32) * s
        bias = jnp.zeros((NUM_EXPERTS,), dtype=jnp.float32)
        W1 = jax.random.normal(ks[3], (NUM_EXPERTS, D_MODEL, EXPERT_DIM), dtype=jnp.float32) * s
        b1 = jax.random.normal(ks[4], (NUM_EXPERTS, EXPERT_DIM), dtype=jnp.float32) * s
        W2 = jax.random.normal(ks[5], (NUM_EXPERTS, EXPERT_DIM, D_MODEL), dtype=jnp.float32) * s
        b2 = jax.random.normal(ks[6], (NUM_EXPERTS, D_MODEL), dtype=jnp.float32) * s
        return {'x': x, 'Wg': Wg, 'bg': bg, 'bias': bias, 'W1': W1, 'b1': b1, 'W2': W2, 'b2': b2}
    _L1_ffn_all = _L1_ffn_setup()
    _L1_ffn_in = {k: v for k, v in _L1_ffn_all.items() if k in ('Wg', 'bg', 'bias', 'W1', 'b1', 'W2', 'b2')}
    del _L1_ffn_all
    return {'x': x, 'src': src, 'dst': dst, 'L0_gnn_W1a': _L0_gnn_in['W1a'], 'L0_gnn_b1a': _L0_gnn_in['b1a'], 'L0_gnn_W1b': _L0_gnn_in['W1b'], 'L0_gnn_b1b': _L0_gnn_in['b1b'], 'L0_gnn_W2a': _L0_gnn_in['W2a'], 'L0_gnn_b2a': _L0_gnn_in['b2a'], 'L0_gnn_W2b': _L0_gnn_in['W2b'], 'L0_gnn_b2b': _L0_gnn_in['b2b'], 'L0_gnn_eps1': _L0_gnn_in['eps1'], 'L0_gnn_eps2': _L0_gnn_in['eps2'], 'L0_ffn_W_fx': _L0_ffn_in['W_fx'], 'L0_ffn_b_fx': _L0_ffn_in['b_fx'], 'L0_ffn_W_x': _L0_ffn_in['W_x'], 'L0_ffn_b_x': _L0_ffn_in['b_x'], 'L0_ffn_W_slice': _L0_ffn_in['W_slice'], 'L0_ffn_b_slice': _L0_ffn_in['b_slice'], 'L0_ffn_W_q': _L0_ffn_in['W_q'], 'L0_ffn_W_k': _L0_ffn_in['W_k'], 'L0_ffn_W_v': _L0_ffn_in['W_v'], 'L0_ffn_W_out': _L0_ffn_in['W_out'], 'L0_ffn_b_out': _L0_ffn_in['b_out'], 'L0_ffn_temperature': _L0_ffn_in['temperature'], 'L1_gnn_W': _L1_gnn_in['W'], 'L1_gnn_b': _L1_gnn_in['b'], 'L1_gnn_gamma': _L1_gnn_in['gamma'], 'L1_gnn_beta': _L1_gnn_in['beta'], 'L1_gnn_running_mean': _L1_gnn_in['running_mean'], 'L1_gnn_running_var': _L1_gnn_in['running_var'], 'L1_ffn_Wg': _L1_ffn_in['Wg'], 'L1_ffn_bg': _L1_ffn_in['bg'], 'L1_ffn_bias': _L1_ffn_in['bias'], 'L1_ffn_W1': _L1_ffn_in['W1'], 'L1_ffn_b1': _L1_ffn_in['b1'], 'L1_ffn_W2': _L1_ffn_in['W2'], 'L1_ffn_b2': _L1_ffn_in['b2']}

def reference(x, src, dst, L0_gnn_W1a, L0_gnn_b1a, L0_gnn_W1b, L0_gnn_b1b, L0_gnn_W2a, L0_gnn_b2a, L0_gnn_W2b, L0_gnn_b2b, L0_gnn_eps1, L0_gnn_eps2, L0_ffn_W_fx, L0_ffn_b_fx, L0_ffn_W_x, L0_ffn_b_x, L0_ffn_W_slice, L0_ffn_b_slice, L0_ffn_W_q, L0_ffn_W_k, L0_ffn_W_v, L0_ffn_W_out, L0_ffn_b_out, L0_ffn_temperature, L1_gnn_W, L1_gnn_b, L1_gnn_gamma, L1_gnn_beta, L1_gnn_running_mean, L1_gnn_running_var, L1_ffn_Wg, L1_ffn_bg, L1_ffn_bias, L1_ffn_W1, L1_ffn_b1, L1_ffn_W2, L1_ffn_b2):
    import jax
    import jax.numpy as jnp

    def _L0_gnn_ref(x, edge_index, W1a, b1a, W1b, b1b, W2a, b2a, W2b, b2b, eps1, eps2):
        import jax, jax.numpy as jnp
        import numpy as np
        N_NODES = 6250
        N_EDGES = 100000
        NFEAT, NHID, NCLASS = (256, 512, 256)

        def _init_params(key):
            ks = jax.random.split(key, 8)
            s = 0.02
            p = {'W1a': jax.random.normal(ks[0], (NFEAT, NHID), jnp.float32) * s, 'b1a': jnp.zeros((NHID,), jnp.float32), 'W1b': jax.random.normal(ks[1], (NHID, NHID), jnp.float32) * s, 'b1b': jnp.zeros((NHID,), jnp.float32), 'W2a': jax.random.normal(ks[2], (NHID, NHID), jnp.float32) * s, 'b2a': jnp.zeros((NHID,), jnp.float32), 'W2b': jax.random.normal(ks[3], (NHID, NCLASS), jnp.float32) * s, 'b2b': jnp.zeros((NCLASS,), jnp.float32), 'eps1': jnp.zeros((), jnp.float32), 'eps2': jnp.zeros((), jnp.float32)}
            return p

        def _gin_agg(h, src, dst, eps, n_nodes):
            agg = jax.ops.segment_sum(h[src], dst, num_segments=n_nodes)
            return (1.0 + eps) * h + agg
        src, dst = (edge_index[0], edge_index[1])
        n = x.shape[0]
        h = _gin_agg(x, src, dst, eps1, n)
        h = jax.nn.relu(h @ W1a + b1a)
        h = jax.nn.relu(h @ W1b + b1b)
        h = _gin_agg(h, src, dst, eps2, n)
        h = jax.nn.relu(h @ W2a + b2a)
        out = h @ W2b + b2b
        return out

    def _L0_ffn_ref(x, W_fx, b_fx, W_x, b_x, W_slice, b_slice, W_q, W_k, W_v, W_out, b_out, temperature):
        import jax, jax.numpy as jnp
        import numpy as np
        DIM = 256
        H = 8
        D = 64
        G = 64
        INNER = H * D
        SCALE = D ** (-0.5)
        B, N, _ = x.shape
        fx_mid = (x @ W_fx + b_fx).reshape(B, N, H, D).transpose(0, 2, 1, 3)
        x_mid = (x @ W_x + b_x).reshape(B, N, H, D).transpose(0, 2, 1, 3)
        temp = jnp.clip(temperature, 0.1, 5.0)
        slice_weights = jax.nn.softmax((x_mid @ W_slice + b_slice) / temp, axis=-1)
        slice_norm = slice_weights.sum(axis=2)
        slice_token = jnp.einsum('bhnc,bhng->bhgc', fx_mid, slice_weights)
        slice_token = slice_token / (slice_norm[..., None] + 1e-05)
        q = slice_token @ W_q
        k = slice_token @ W_k
        v = slice_token @ W_v
        attn = jax.nn.softmax(jnp.einsum('bhgc,bhkc->bhgk', q, k) * SCALE, axis=-1)
        out_slice = jnp.einsum('bhgk,bhkc->bhgc', attn, v)
        out_x = jnp.einsum('bhgc,bhng->bhnc', out_slice, slice_weights)
        out_x = out_x.transpose(0, 2, 1, 3).reshape(B, N, INNER)
        return out_x @ W_out + b_out

    def _L1_gnn_ref(x, edge_index, W, b, gamma, beta, running_mean, running_var):
        import jax, jax.numpy as jnp
        import numpy as np
        BN_EPS = 1e-05
        N = x.shape[0]
        loop = jnp.arange(N, dtype=edge_index.dtype)
        src = jnp.concatenate([edge_index[0], loop])
        dst = jnp.concatenate([edge_index[1], loop])
        h = x @ W
        ones = jnp.ones(src.shape[0], dtype=x.dtype)
        deg = jax.ops.segment_sum(ones, dst, num_segments=N)
        dinv = jnp.where(deg > 0, jax.lax.rsqrt(deg), 0.0)
        norm = dinv[src] * dinv[dst]
        msgs = h[src] * norm[:, None]
        out = jax.ops.segment_sum(msgs, dst, num_segments=N) + b
        y = (out - running_mean) * jax.lax.rsqrt(running_var + BN_EPS) * gamma + beta
        return jax.nn.relu(y)

    def _L1_ffn_ref(x, Wg, bg, bias, W1, b1, W2, b2):
        import jax, jax.numpy as jnp
        import numpy as np
        D_MODEL = 256
        EXPERT_DIM = 512
        NUM_EXPERTS = 8
        TOP_K = 2
        SEQ_LEN = 128
        BATCH = 2
        x_flat = x.reshape(-1, D_MODEL)
        gate_logits = x_flat @ Wg + bg + bias
        topk_vals, topk_idx = jax.lax.top_k(gate_logits, TOP_K)
        topk_w = jax.nn.softmax(topk_vals, axis=-1)
        combine = (jax.nn.one_hot(topk_idx, NUM_EXPERTS, dtype=x.dtype) * topk_w[..., None]).sum(axis=1)
        h = jax.nn.relu(jnp.einsum('td,edh->teh', x_flat, W1) + b1)
        y = jnp.einsum('teh,ehd->ted', h, W2) + b2
        out = jnp.einsum('ted,te->td', y, combine)
        return out.reshape(x.shape)
    edge_index = jnp.stack([src, dst])
    x = x + _L0_gnn_ref(_layernorm(x, axis=-1), edge_index, L0_gnn_W1a, L0_gnn_b1a, L0_gnn_W1b, L0_gnn_b1b, L0_gnn_W2a, L0_gnn_b2a, L0_gnn_W2b, L0_gnn_b2b, L0_gnn_eps1, L0_gnn_eps2)
    x = x + _L0_ffn_ref(_layernorm(x, axis=-1)[None], L0_ffn_W_fx, L0_ffn_b_fx, L0_ffn_W_x, L0_ffn_b_x, L0_ffn_W_slice, L0_ffn_b_slice, L0_ffn_W_q, L0_ffn_W_k, L0_ffn_W_v, L0_ffn_W_out, L0_ffn_b_out, L0_ffn_temperature)[0]
    x = x + _L1_gnn_ref(_layernorm(x, axis=-1), edge_index, L1_gnn_W, L1_gnn_b, L1_gnn_gamma, L1_gnn_beta, L1_gnn_running_mean, L1_gnn_running_var)
    x = x + _L1_ffn_ref(_layernorm(x, axis=-1)[None], L1_ffn_Wg, L1_ffn_bg, L1_ffn_bias, L1_ffn_W1, L1_ffn_b1, L1_ffn_W2, L1_ffn_b2)[0]
    return x

_drawn_inputs = setup_inputs


def setup_inputs(seed=0):
    import zlib

    import numpy as np

    out = dict(_drawn_inputs(seed))
    spreads = {'L0_gnn_b1a': (0.0, 0.1),
     'L0_gnn_b1b': (0.0, 0.1),
     'L0_gnn_b2a': (0.0, 0.1),
     'L0_gnn_b2b': (0.0, 0.1),
     'L0_ffn_b_fx': (0.0, 0.1),
     'L0_ffn_b_x': (0.0, 0.8),
     'L0_ffn_b_slice': (0.0, 0.8),
     'L0_ffn_b_out': (0.0, 0.1),
     'L0_ffn_temperature': (0.5, 0.6),
     'L1_gnn_b': (0.0, 0.1),
     'L1_gnn_gamma': (1.0, 0.2),
     'L1_gnn_beta': (0.0, 0.1),
     'L1_gnn_running_mean': (0.0, 0.1),
     'L1_gnn_running_var': (1.0, 0.2),
     'L1_ffn_bias': (0.0, 0.487)}
    factors = {'L0_ffn_W_x': 5.286,
     'L0_ffn_W_slice': 7.706,
     'L0_ffn_W_q': 8.0,
     'L0_ffn_W_k': 8.0,
     'L1_ffn_bg': 8.0,
     'L1_ffn_b1': 8.0,
     'L1_ffn_b2': 5.595}
    for name, (base, spread) in spreads.items():
        noise = np.random.default_rng([zlib.crc32(name.encode()), seed]).standard_normal(out[name].shape)
        drawn = base * np.exp(spread * noise) if base else spread * noise
        out[name] = jnp.asarray(drawn.astype(out[name].dtype))
    for name, factor in factors.items():
        out[name] = (out[name] * factor).astype(out[name].dtype)
    return out
```

```python
import concourse.bass as bass
from concourse import mybir
from contextlib import ExitStack

FP32 = mybir.dt.float32
BF16 = mybir.dt.bfloat16
I32 = mybir.dt.int32
ALU = mybir.AluOpType
ACT = mybir.ActivationFunctionType
AX = mybir.AxisListType.X

P = 128
N = 6250
E = 106250
D = 256
HID = 512
NB = -(-N // P)
NPAD = NB * P
TAIL = N - (NB - 1) * P
SB = NB // 4
HEADS, HD, G = 8, 64, 64
NE = 8
LN_EPS = 1e-5
KD, KH = D // P, HID // P

PAIR = 2 * P
RING = 8
SLOTS = 2 * RING
PAIRS_MAX = E // PAIR + NB + 1
TILES = -(-(2 * (PAIRS_MAX + RING + RING)) // P) * P
TC = TILES // P
E_LAST = -(-(E + P) // P) * P
E_PAD = E_LAST + P
DE, ER = 125, E // 125

T1_MID, T1_LO, T1_HI, T1_W = 0, D, 2 * D, 3 * D + 2
T2_W, T3_W = 3 * HID, 3 * D


def build(nc, a, out):
    with ExitStack() as whole:

        def dram(name, shape, dt):
            return nc.dram_tensor(name, shape, dt, kind="Internal").ap()

        def row_bc(ap, n):
            return ap.rearrange("(a n) -> a n", a=1).to_broadcast([P, n])

        src_pad = dram("src_pad", [E_PAD, 1], I32)
        dst_pad = dram("dst_pad", [E_PAD, 1], I32)
        xtail = dram("xtail", [P, D], FP32)
        xl_rows = dram("xl_rows", [NPAD, D], FP32)
        table1 = dram("table1", [NPAD, T1_W], BF16)
        h_rows = dram("h_rows", [NPAD, HID], FP32)
        table2 = dram("table2", [NPAD, T2_W], BF16)
        x1_rows = dram("x1_rows", [NPAD, D], FP32)
        swt_rows = dram("swt_rows", [NB, P, KH * P], FP32)
        x2_rows = dram("x2_rows", [NPAD, D], FP32)
        v_rows = dram("v_rows", [NPAD, D], FP32)
        table3 = dram("table3", [NPAD, T3_W], BF16)

        class Scope:

            def __init__(self, stack, tag):
                self.stack, self.tag, self.sems = stack, tag, []
                stack.callback(self.end)

            def end(self):
                if self.sems:
                    nc.clear_and_free_semaphores(self.sems)
                    nc.all_engine_barrier()

            def sb(self, name, shape, dt=FP32):
                return self.stack.enter_context(nc.sbuf_tensor(f"{self.tag}_{name}", shape, dt))

            def ps(self, name, shape=(P, 512), dt=FP32):
                return self.stack.enter_context(nc.psum_tensor(f"{self.tag}_{name}", list(shape), dt))

            def sem(self, name):
                self.sems.append(nc.alloc_semaphore(name=f"{self.tag}_{name}"))
                return self.sems[-1]

        class Chain:

            def __init__(self, eng, sem):
                self.eng, self.sem, self.n = eng, sem, 0

            def link(self, ins):
                self.n += 1
                ins.then_inc(self.sem, 1)
                self.eng.wait_ge(self.sem, self.n)

            def restart(self):
                self.eng.sem_clear(self.sem)
                self.n = 0

        def rsqrt(ch, out, x, tmp):
            v = nc.vector
            ch.link(v.tensor_scalar(tmp.bitcast(I32), x.bitcast(I32), 1, None, ALU.arith_shift_right))
            ch.link(v.tensor_scalar(out.bitcast(I32), tmp.bitcast(I32), -1.0, float(0x5F3759DF), ALU.mult, ALU.add))
            for _ in range(4):
                ch.link(v.tensor_tensor(tmp, out, out, ALU.mult))
                ch.link(v.tensor_tensor(tmp, tmp, x, ALU.mult))
                ch.link(v.tensor_scalar(tmp, tmp, -0.5, 1.5, ALU.mult, ALU.add))
                ch.link(v.tensor_tensor(out, out, tmp, ALU.mult))

        def pipeline(eng, items, close, pieces, begin=None):

            def run(sb, nb, before):
                for q in range(4):
                    if q < nb:
                        items(sb, q)
                    if q == 0 and before:
                        close(sb - 1, 3)
                    if q == 0 and begin:
                        begin(sb, nb)
                    if 0 < q < nb:
                        close(sb, q - 1)
                    if before:
                        pieces(sb - 1, 4, q)

            run(0, 4, False)
            with eng.Fori(1, SB) as sb:
                run(sb, 4, True)
            run(SB, 1, True)
            close(SB, 0)
            for q in range(4):
                pieces(SB, 1, q)

        def superblocks(eng, body):
            with eng.Fori(0, SB) as sb:
                body(sb, 4)
            body(SB, 1)

        W = Scope(whole, "w")
        iota_row = W.sb("iota_row", [P, P], BF16)
        ident = W.sb("ident", [P, P])
        zeros = W.sb("zeros", [P, 512], BF16)
        dst_rel = W.sb("dst_rel", [P, TILES])
        src_idx = W.sb("src_idx", [P, TILES], I32)
        bounds = W.sb("bounds", [1, NB + 1], I32)
        chunks = W.sb("chunks", [1, 1], I32)
        degree = W.sb("degree", [P, NB])
        dinv = W.sb("dinv", [P, NB])
        slice_w = W.sb("slice_w", [P, KD, HID])
        slice_b = W.sb("slice_b", [P, HID])
        tok = W.sb("tok", [P, KH, D + 1])

        with ExitStack() as stack:
            S = Scope(stack, "s0")
            dst_i = S.sb("dst_i", [DE, ER], I32)
            dst_f = S.sb("dst_f", [DE, ER])
            below = S.sb("below", [DE, ER], BF16)
            count = S.sb("count", [DE, NB + 1])
            ones = S.sb("ones", [P, P])
            diff_i = S.sb("diff_i", [P, P], I32)
            col_i = S.sb("col_i", [P, P], I32)
            tri = S.sb("tri", [NB, NB + 1])
            ends = S.sb("ends", [NB, 2])
            npairs = S.sb("npairs", [NB, 1])
            npairs_i = S.sb("npairs_i", [NB, 1], I32)
            span = S.sb("span", [NB, 2])
            part_i = S.sb("part_i", [NB, 1], I32)
            vals = S.sb("vals", [NB, 2])
            tile_i = S.sb("tile_i", [NB, TILES], I32)
            tile_f = S.sb("tile_f", [NB, TILES])
            inside = S.sb("inside", [NB, TILES])
            tpos_i = S.sb("tpos_i", [P, TC], I32)
            tpos = S.sb("tpos", [P, TC])
            start = S.sb("start", [P, TC])
            start_i = S.sb("start_i", [P, TC], I32)
            base = S.sb("base", [P, TC])
            srow = S.sb("srow", [P, TC, P], I32)
            drow = S.sb("drow", [P, TC, P], I32)
            srow_f = S.sb("srow_f", [P, TC, P])
            drow_f = S.sb("drow_f", [P, TC, P])
            pad0 = S.sb("pad0", [1, E_PAD - E], I32)
            pad1 = S.sb("pad1", [1, E_PAD - E], I32)
            chunk_i = S.sb("chunk_i", [1, 1], I32)
            wx = S.sb("wx", [P, KD, HID])
            wxT = S.sb("wxT", [P, KH, D])
            ws2 = S.sb("ws2", [P, G])
            wsbd = S.sb("wsbd", [P, KH, P])
            bx = S.sb("bx", [P, KH])
            bxr = S.sb("bxr", [P, KH, P])
            rtemp = S.sb("rtemp", [P, HEADS])
            bs = S.sb("bs", [P, G])
            xin = S.sb("xin", [P, 2, 4, D])
            stat = S.sb("stat", [P, 4, 6])
            mv = S.sb("mv", [P, 4, 2])
            var = S.sb("var", [P, 4])
            tmp4 = S.sb("tmp4", [P, 4])
            rstd = S.sb("rstd", [P, 4])
            xl = S.sb("xl", [P, 4, D])
            res = S.sb("res", [P, 4, D])
            trow = S.sb("trow", [P, 4, T1_W], BF16)

            psA = S.ps("psA")
            psB = S.ps("psB")
            psT = [S.ps(f"psT{i}") for i in range(2)]

            s_in = S.sem("inputs")
            s_wx = S.sem("slice_inputs")
            s_iota = S.sem("iotas")
            s_cst = S.sem("constants")
            s_pad = S.sem("padded_edges")
            s_padset = S.sem("pad_values")
            s_cnt = S.sem("counted")
            s_ends = S.sem("ends")
            s_np = S.sem("npairs")
            s_span = S.sem("span")
            s_ins = S.sem("inside")
            s_st = S.sem("starts_psum")
            s_sti = S.sem("starts")
            s_rows = S.sem("edge_rows")
            s_rowf = S.sem("edge_rows_float")
            s_tr = S.sem("edge_transposes")
            s_trc = S.sem("edge_transposes_copied")
            s_wt = S.sem("wx_transposed")
            s_wtc = S.sem("wx_transposes_copied")
            s_bd = S.sem("block_diagonal")
            s_sw = S.sem("slice_weights_psum")
            s_dve = S.sem("dve_chain")
            s_x = [S.sem(f"x_loaded{i}") for i in range(2)]
            s_xl = S.sem("normalised")
            s_hi = S.sem("high_parts")
            s_res = S.sem("residuals")
            s_mid = S.sem("middle_parts")
            s_lo = S.sem("low_parts")
            s_sto = S.sem("tables_stored")
            s_xt = S.sem("tail_cleared")
            s_xts = S.sem("tail_stored")

            block = stack.enter_context(nc.Block())

            def x_view(t, sb, nb, w):
                return t[bass.ds(sb * 4 * P, nb * P), :].rearrange("(q p) d -> p q d", p=P)

            @block.sync
            def _(sp):
                sp.dma_start(dst_i[:, :], a["dst"].rearrange("(p r) -> p r", p=DE)).then_inc(s_in, 16)
                sp.dma_start(src_pad[0:E, :].rearrange("(p r) a -> p (r a)", p=DE),
                             a["src"].rearrange("(p r) -> p r", p=DE)).then_inc(s_pad, 16)
                sp.dma_start(dst_pad[0:E, :].rearrange("(p r) a -> p (r a)", p=DE),
                             a["dst"].rearrange("(p r) -> p r", p=DE)).then_inc(s_pad, 16)
                sp.wait_ge(s_padset, 2)
                sp.dma_start(src_pad[E:E_PAD, :].rearrange("r a -> a r"), pad0[:, :]).then_inc(s_pad, 16)
                sp.dma_start(dst_pad[E:E_PAD, :].rearrange("r a -> a r"), pad1[:, :]).then_inc(s_pad, 16)
                with sp.Fori(0, SB // 2) as it:
                    for par in range(2):
                        sp.wait_ge(s_xl, it * 2 + par + 1)
                        sp.dma_start(xin[:, par], x_view(a["x"], it * 2 + par, 4, D)).then_inc(s_x[par], 16)
                sp.wait_ge(s_xt, 1)
                sp.dma_start(xin[0:TAIL, 0, 0], a["x"][SB * 4 * P:N, :]).then_inc(s_x[0], 16)
                sp.wait_ge(s_pad, 64)

            @block.gpsimd
            def _(pool):
                pool.iota(diff_i[:, :], [[1, P]], base=0, channel_multiplier=-1).then_inc(s_iota, 1)
                pool.iota(part_i[:, :], [[0, 1]], base=0, channel_multiplier=P).then_inc(s_iota, 1)
                pool.iota(tile_i[:, :], [[1, TILES]], base=0, channel_multiplier=0).then_inc(s_iota, 1)
                pool.iota(tpos_i[:, :], [[P * P, TC]], base=0, channel_multiplier=P).then_inc(s_iota, 1)
                pool.iota(col_i[:, :], [[1, P]], base=0, channel_multiplier=0).then_inc(s_iota, 1)
                pool.memset(pad0[:, :], 0).then_inc(s_padset, 1)
                pool.wait_ge(s_sti, 1)
                pool.wait_ge(s_pad, 64)
                for c in range(TC):
                    pool.indirect_dma_start(srow[:, c, :], None, src_pad,
                                            bass.IndirectOffsetOnAxis(ap=start_i[:, c:c + 1], axis=0)).then_inc(s_rows, 16)
                    pool.indirect_dma_start(drow[:, c, :], None, dst_pad,
                                            bass.IndirectOffsetOnAxis(ap=start_i[:, c:c + 1], axis=0)).then_inc(s_rows, 16)

            @block.vector
            def _(dve):
                ch = Chain(dve, s_dve)
                v = nc.vector
                v.memset(pad1[:, :], 1000000).then_inc(s_padset, 1)
                v.memset(zeros[:, :], 0.0)
                v.memset(ones[:, :], 1.0)
                v.memset(count[:, 0:1], 0.0)
                v.memset(count[:, NB:NB + 1], float(ER))
                v.memset(wsbd[:, :, :], 0.0)
                v.memset(trow[:, :, T1_HI + D:T1_W], 1.0)
                ch.link(v.memset(tok[:, :, :], 0.0))
                dve.wait_ge(s_iota, 5)
                v.tensor_copy(iota_row[:, :], col_i[:, :])
                v.tensor_scalar(ident[:, :], diff_i[:, :], 0.0, None, ALU.is_equal)
                v.tensor_scalar(tri[:, :], diff_i[0:NB, 0:NB + 1], 0.0, None, ALU.is_gt)
                v.tensor_copy(tile_f[:, :], tile_i[:, :])
                v.tensor_copy(tpos[:, :], tpos_i[:, :])
                ch.link(v.tensor_copy(vals[:, 1:2], part_i[:, :]))
                dve.wait_ge(s_in, 16)
                ch.link(v.tensor_copy(dst_f[:, :], dst_i[:, :]))
                for b in range(1, NB):
                    ch.link(v.tensor_scalar(below[:, :], dst_f[:, :], float(b * P), 0.0, ALU.is_lt, ALU.add,
                                            accum_out=count[:, b:b + 1]))
                v.memset(start_i[:, :], 0).then_inc(s_cnt, 1)
                dve.wait_ge(s_ends, 1)
                ch.link(v.tensor_copy(ends[:, :], psA[0:NB, 0:2]))
                ch.link(v.tensor_tensor(npairs[:, :], ends[:, 1:2], ends[:, 0:1], ALU.subtract))
                ch.link(v.tensor_scalar(npairs_i[:, :], npairs[:, :], float(PAIR - 1), None, ALU.add))
                ch.link(v.tensor_scalar(npairs_i[:, :], npairs_i[:, :], 8, None, ALU.arith_shift_right))
                v.tensor_scalar(npairs[:, :], npairs_i[:, :], 1.0, None, ALU.max).then_inc(s_np, 1)
                dve.wait_ge(s_span, 1)
                v.tensor_copy(bounds[:, :], psB[0:1, 0:NB + 1])
                v.tensor_scalar(chunk_i[:, :], psB[0:1, NB:NB + 1], float(RING - 1), None, ALU.add)
                ch.link(v.tensor_scalar(span[:, :], psB[0:NB, 64:66], 2.0, None, ALU.mult))
                v.tensor_scalar(chunks[:, :], chunk_i[:, :], 3, None, ALU.arith_shift_right)
                ch.link(v.scalar_tensor_tensor(vals[:, 0:1], span[:, 0:1], -float(P), ends[:, 0:1], ALU.mult, ALU.add))
                ch.link(v.tensor_scalar(inside[:, :], tile_f[:, :], span[:, 0:1], None, ALU.is_ge))
                v.scalar_tensor_tensor(inside[:, :], tile_f[:, :], span[:, 1:2], inside[:, :],
                                       ALU.is_lt, ALU.mult).then_inc(s_ins, 1)
                dve.wait_ge(s_st, 1)
                st = psA[:, 64:64 + 2 * TC].rearrange("p (c v) -> p c v", v=2)
                v.tensor_copy(base[:, :], st[:, :, 1])
                ch.link(v.tensor_tensor(start[:, :], st[:, :, 0], tpos[:, :], ALU.add))
                v.tensor_scalar(start_i[:, :], start[:, :], float(E_LAST), None, ALU.min).then_inc(s_sti, 1)
                dve.wait_ge(s_wx, 16 * 6)
                ch.link(v.tensor_scalar(rtemp[:, :], rtemp[:, :], 0.1, 5.0, ALU.max, ALU.min))
                ch.link(v.reciprocal(rtemp[:, :], rtemp[:, :]))
                for c in range(KH):
                    for k in range(2):
                        rows = slice(k * 64, k * 64 + 64)
                        v.tensor_scalar(wsbd[rows, c, rows], ws2[rows, :], rtemp[rows, 2 * c + k:2 * c + k + 1], None, ALU.mult)
                    v.tensor_scalar(bxr[:, c, :], ones[:, :], bx[:, c:c + 1], None, ALU.mult)
                for h in range(HEADS):
                    last = v.tensor_scalar(slice_b[:, h * G:(h + 1) * G], bs[:, :], rtemp[:, h:h + 1], None, ALU.mult)
                last.then_inc(s_bd, 1)
                dve.wait_ge(s_wt, 1)
                for k in range(KD):
                    last = v.tensor_copy(wxT[:, :, k * P:(k + 1) * P], psT[k][:, :].rearrange("p (c j) -> p c j", c=KH))
                last.then_inc(s_wtc, 1)
                dve.wait_ge(s_sw, 1)
                v.tensor_copy(slice_w[:, 0, :], psT[0][:, :])
                v.tensor_copy(slice_w[:, 1, :], psT[1][:, :])
                ch.link(v.tensor_tensor(slice_b[:, :], slice_b[:, :], psB[:, :], ALU.add))
                dve.wait_ge(s_rows, 16 * 2 * TC)
                v.tensor_copy(srow_f[:, :, :], srow[:, :, :])
                for c in range(TC):
                    last = v.tensor_scalar(drow_f[:, c, :], drow[:, c, :], base[:, c:c + 1], None, ALU.subtract)
                last.then_inc(s_rowf, 1)
                for k in range(TC // 2):
                    dve.wait_ge(s_tr, k + 1)
                    table = (src_idx, dst_rel)[k // 2]
                    v.tensor_copy(table[:, (k % 2) * 512:(k % 2) * 512 + 512], psT[k % 2][:, :]).then_inc(s_trc, 1)
                ch.restart()

                def norm(sb, nb, par, it):
                    dve.wait_ge(s_x[par], (it + 1) * 16)
                    for q in range(nb):
                        last = v.bn_stats(stat[:, q, :], xin[:, par, q, :])
                    ch.link(last)
                    for q in range(nb):
                        last = v.bn_aggr(mv[:, q, :], stat[:, q, :])
                    ch.link(last)
                    ch.link(v.tensor_scalar(var[:, 0:nb], mv[:, 0:nb, 1], LN_EPS, None, ALU.add))
                    rsqrt(ch, rstd[:, 0:nb], var[:, 0:nb], tmp4[:, 0:nb])
                    dve.wait_ge(s_sto, sb * 32 + 32)
                    for q in range(nb):
                        last = v.tensor_scalar(xl[:, q, :], xin[:, par, q, :], mv[:, q, 0:1], rstd[:, q:q + 1],
                                               ALU.subtract, ALU.mult)
                    last.then_inc(s_xl, 1)
                    dve.wait_ge(s_hi, sb + 1)
                    v.tensor_tensor(res[:, 0:nb, :], xl[:, 0:nb, :], trow[:, 0:nb, T1_HI:T1_HI + D], ALU.subtract).then_inc(s_res, 1)
                    dve.wait_ge(s_mid, sb + 1)
                    v.tensor_tensor(trow[:, 0:nb, T1_LO:T1_LO + D], res[:, 0:nb, :], trow[:, 0:nb, T1_MID:T1_MID + D],
                                    ALU.subtract).then_inc(s_lo, 1)
                    ch.restart()

                dve.sem_inc(s_xl, 2)
                with dve.Fori(0, SB // 2) as it:
                    for par in range(2):
                        norm(it * 2 + par, 4, par, it)
                v.memset(xin[:, 0, 0, :], 0.0).then_inc(s_xt, 1)
                norm(SB, 1, 0, SB // 2)

            @block.scalar
            def _(act):
                ac = nc.scalar
                act.dma_start(wx[:, :, :], a["L0_ffn_W_x"].rearrange("(k p) n -> p k n", p=P)).then_inc(s_wx, 16)
                act.dma_start(ws2[0:64, :], a["L0_ffn_W_slice"]).then_inc(s_wx, 16)
                act.dma_start(ws2[64:128, :], a["L0_ffn_W_slice"]).then_inc(s_wx, 16)
                act.dma_start(bx[:, :], a["L0_ffn_b_x"].rearrange("(c p) -> p c", p=P), allow_slow_non_contiguous=True).then_inc(s_wx, 16)
                act.dma_start(rtemp[:, :], row_bc(a["L0_ffn_temperature"].rearrange("a h b c -> (a h b c)"), HEADS)).then_inc(s_wx, 16)
                act.dma_start(bs[:, :], row_bc(a["L0_ffn_b_slice"], G)).then_inc(s_wx, 16)
                act.sem_inc(s_sto, 32)

                def parts(sb, nb):
                    act.wait_ge(s_xl, sb + 3)
                    ac.activation(trow[:, 0:nb, T1_HI:T1_HI + D], xl[:, 0:nb, :], ACT.Copy).then_inc(s_hi, 1)
                    act.wait_ge(s_res, sb + 1)
                    ac.activation(trow[:, 0:nb, T1_MID:T1_MID + D], res[:, 0:nb, :], ACT.Copy).then_inc(s_mid, 1)
                    act.wait_ge(s_lo, sb + 1)
                    act.dma_start(x_view(xl_rows, sb, nb, D), xl[:, 0:nb, :]).then_inc(s_sto, 16)
                    act.dma_start(x_view(table1, sb, nb, T1_W), trow[:, 0:nb, :]).then_inc(s_sto, 16)

                superblocks(act, parts)
                act.dma_start(xtail, xin[:, 0, 0, :]).then_inc(s_xts, 16)
                act.wait_ge(s_xts, 16)
                act.wait_ge(s_sto, 32 * (SB + 2))

            @block.tensor
            def _(pe):
                pe.wait_ge(s_cnt, 1)
                nc.tensor.matmul(psA[0:NB, 0:1], count[:, 0:NB], ones[0:DE, 0:1], start=True, stop=True)
                nc.tensor.matmul(psA[0:NB, 1:2], count[:, 1:NB + 1], ones[0:DE, 0:1], start=True, stop=True).then_inc(s_ends, 1)
                pe.wait_ge(s_np, 1)
                nc.tensor.matmul(psB[0:1, 0:NB + 1], npairs[:, :], tri[:, :], start=True, stop=True)
                nc.tensor.matmul(psB[0:NB, 64:65], tri[:, 0:NB], npairs[:, :], start=True, stop=True)
                nc.tensor.matmul(psB[0:NB, 65:66], tri[:, 1:NB + 1], npairs[:, :], start=True, stop=True).then_inc(s_span, 1)
                pe.wait_ge(s_ins, 1)
                for c in range(TC):
                    last = nc.tensor.matmul(psA[:, 64 + 2 * c:66 + 2 * c], inside[:, c * P:(c + 1) * P], vals[:, :], start=True, stop=True)
                last.then_inc(s_st, 1)
                pe.wait_ge(s_wx, 16 * 6)
                for k in range(KD):
                    for c in range(KH):
                        last = nc.tensor.transpose(psT[k][:, c * P:(c + 1) * P], wx[:, k, c * P:(c + 1) * P], ident[:, :])
                last.then_inc(s_wt, 1)
                pe.wait_ge(s_bd, 1)
                pe.wait_ge(s_wtc, 1)
                for c in range(KH):
                    cols = slice(c * P, (c + 1) * P)
                    for k in range(KD):
                        nc.tensor.matmul(psT[k][:, cols], wxT[:, c, k * P:(k + 1) * P], wsbd[:, c, :], start=True, stop=True)
                    last = nc.tensor.matmul(psB[:, cols], bxr[:, c, :], wsbd[:, c, :], start=True, stop=True)
                last.then_inc(s_sw, 1)
                pe.wait_ge(s_rowf, 1)
                for k in range(TC // 2):
                    if k >= 2:
                        pe.wait_ge(s_trc, k - 1)
                    rows = (srow_f, drow_f)[k // 2]
                    for j in range(4):
                        last = nc.tensor.transpose(psT[k % 2][:, j * P:(j + 1) * P], rows[:, (k % 2) * 4 + j, :], ident[:, :])
                    last.then_inc(s_tr, 1)

        class Edges:
            AHEAD = 32

            def __init__(self, S, table, width, parts, feats, ones_at=None):
                self.table, self.parts, self.feats, self.ones_at = table, parts, feats, ones_at
                self.rows = S.sb("edge_rows", [P, RING, 2, width], BF16)
                self.onehot = S.sb("onehot", [P, self.AHEAD, 2, P], BF16)
                self.idx = [S.sb(f"idx{h}", [P, SLOTS // 2], I32) for h in range(2)]
                self.s_idx = [S.sem(f"idx_loaded{h}") for h in range(2)]
                self.s_slot = [S.sem(f"slot_filled{j}") for j in range(SLOTS)]
                self.s_gathered = S.sem("pairs_gathered")
                self.s_onehot = S.sem("onehots_ready")
                self.s_used = S.sem("pairs_used")
                self.s_start = S.sem("pairs_started")
                self.s_agg = S.sem("block_summed")

            def gather(self, pool):
                n = pool.value_load(chunks[0:1, 0:1], min_val=1, max_val=TILES // SLOTS - 1)
                with pool.Fori(0, n) as c:
                    for h in range(2):
                        pool.wait_ge(self.s_idx[h], c * 16 + 16)
                        for j in range(SLOTS // 2):
                            slot = h * SLOTS // 2 + j
                            if j % 2 == 0:
                                pool.wait_ge(self.s_used, c * RING + (slot // 2 + 1 + self.AHEAD - RING))
                                pool.sem_inc(self.s_start, 1)
                            pool.indirect_dma_start(
                                self.rows[:, slot // 2, slot % 2, :], None, self.table,
                                bass.IndirectOffsetOnAxis(ap=self.idx[h][:, j:j + 1], axis=0)
                            ).then_inc(self.s_slot[slot], 16)

            def relay(self, sp):
                n = sp.value_load(chunks[0:1, 0:1], min_val=1, max_val=TILES // SLOTS - 1)
                half = SLOTS // 2
                for h in range(2):
                    sp.dma_start(self.idx[h][:, :], src_idx[:, h * half:(h + 1) * half]).then_inc(self.s_idx[h], 16)
                with sp.Fori(0, n) as c:
                    for h in range(2):
                        for pair in range(h * RING // 2, (h + 1) * RING // 2):
                            sp.wait_ge(self.s_slot[2 * pair], c * 16 + 16)
                            sp.wait_ge(self.s_slot[2 * pair + 1], c * 16 + 16)
                            sp.sem_inc(self.s_gathered, 1)
                        sp.dma_start(self.idx[h][:, :], src_idx[:, bass.ds(c * SLOTS + (SLOTS + h * half), half)]
                                     ).then_inc(self.s_idx[h], 16)
                for h in range(2):
                    sp.wait_ge(self.s_idx[h], n * 16 + 16)
                sp.sem_inc(self.s_gathered, 1)

            def range_of(self, eng, b):
                lo = eng.value_load(bounds[0:1, bass.ds(b, 1)], min_val=0, max_val=PAIRS_MAX)
                hi = eng.value_load(bounds[0:1, bass.ds(b + 1, 1)], min_val=1, max_val=PAIRS_MAX)
                return lo, hi

            def onehots(self, dve, b):
                lo, hi = self.range_of(dve, b)
                with dve.Fori(lo, hi) as i:
                    dve.wait_ge(self.s_used, i + 1)
                    r = dve.snap(i % self.AHEAD)
                    for t in range(2):
                        last = nc.vector.tensor_scalar(self.onehot[:, bass.ds(r, 1), t, :], iota_row[:, :],
                                                       dst_rel[:, bass.ds(i * 2 + t, 1)], None, ALU.is_equal)
                    last.then_inc(self.s_onehot, 1)

            def next_onehots(self, dve, sb, q):
                if not (isinstance(sb, int) and sb == SB):
                    self.onehots(dve, sb * 4 + (q + 1))

            def sums(self, pe, b, bank):
                w = self.feats + (self.ones_at is not None)
                nc.tensor.matmul(bank[:, 0:w], zeros[:, 0:P], zeros[:, 0:w], start=True, stop=False, skip_group_check=True)
                lo, hi = self.range_of(pe, b)
                with pe.Fori(lo, hi) as i:
                    pe.wait_ge(self.s_onehot, i + 1)
                    pe.wait_ge(self.s_gathered, i + 1)
                    r, o = pe.snap(i % RING), pe.snap(i % self.AHEAD)
                    for t in range(2):
                        for part in self.parts:
                            n = self.feats + (part + self.feats == self.ones_at)
                            last = nc.tensor.matmul(bank[:, 0:n], self.onehot[:, bass.ds(o, 1), t, :],
                                                    self.rows[:, bass.ds(r, 1), t, part:part + n],
                                                    start=False, stop=False, skip_group_check=True)
                    last.then_inc(self.s_used, 1)
                nc.tensor.matmul(bank[:, 0:w], zeros[:, 0:P], zeros[:, 0:w], start=False, stop=True,
                                 skip_group_check=True).then_inc(self.s_agg, 1)

        def rows_of(t, sb, nb):
            return t[bass.ds(sb * (4 * P), nb * P), :].rearrange("(q p) d -> p q d", p=P)

        with ExitStack() as stack:
            S = Scope(stack, "s1")
            edges = Edges(S, table1, T1_W, (T1_MID, T1_LO, T1_HI), D, ones_at=T1_HI + D)
            w1a = S.sb("w1a", [P, KD, HID])
            w1b = S.sb("w1b", [P, KH, HID])
            b1a = S.sb("b1a", [P, KH])
            b1b = S.sb("b1b", [P, HID])
            eps1 = S.sb("eps1", [P, 1])
            self_x = S.sb("self_x", [P, 4, D])
            agg = S.sb("agg", [P, 4, D])
            aggT = S.sb("aggT", [P, KD, 4 * P])
            h1T = S.sb("h1T", [P, KH, 4 * P])
            pre = S.sb("pre", [P, 4, HID])
            hid = S.sb("hid", [P, 4, HID])
            res = S.sb("res", [P, 4, HID])
            trow = S.sb("trow", [P, 4, T2_W], BF16)
            psA = [S.ps(f"psA{i}") for i in range(2)]
            psT = [S.ps(f"psT{i}") for i in range(2)]
            psM = [S.ps(f"psM{i}") for i in range(4)]

            s_w = S.sem("weights")
            s_eps = S.sem("one_plus_eps")
            s_self = S.sem("self_rows")
            s_evac = S.sem("sums_copied")
            s_tr = S.sem("sums_transposed")
            s_aggT = S.sem("transposes_copied")
            s_m1 = S.sem("first_product")
            s_h1T = S.sem("first_relu")
            s_m2 = S.sem("second_product")
            s_pre = S.sem("second_product_copied")
            s_hid = S.sem("hidden_rows")
            s_res = S.sem("residual")
            s_mid = S.sem("middle_part")
            s_lo = S.sem("low_part")
            s_sto = S.sem("rows_stored")
            block = stack.enter_context(nc.Block())

            @block.gpsimd
            def _(pool):
                edges.gather(pool)

            @block.sync
            def _(sp):
                edges.relay(sp)

            @block.scalar
            def _(act):
                ac = nc.scalar
                act.dma_start(w1a[:, :, :], a["L0_gnn_W1a"].rearrange("(k p) n -> p k n", p=P)).then_inc(s_w, 16)
                act.dma_start(w1b[:, :, :], a["L0_gnn_W1b"].rearrange("(k p) n -> p k n", p=P)).then_inc(s_w, 16)
                act.dma_start(b1a[:, :], a["L0_gnn_b1a"].rearrange("(m p) -> p m", p=P), allow_slow_non_contiguous=True).then_inc(s_w, 16)
                act.dma_start(b1b[:, :], row_bc(a["L0_gnn_b1b"], HID)).then_inc(s_w, 16)
                act.dma_start(eps1[:, :], row_bc(a["L0_gnn_eps1"], 1)).then_inc(s_w, 16)
                act.sem_inc(s_aggT, 2)
                act.sem_inc(s_sto, 32)
                act.wait_ge(s_w, 80)

                def begin(sb, nb):
                    act.wait_ge(s_evac, sb * 4 + 2)
                    act.dma_start(self_x[:, 0:nb, :], rows_of(xl_rows, sb, nb)).then_inc(s_self, 16)

                def close(sb, q):
                    act.wait_ge(s_tr, sb * 4 + (q + 1))
                    ac.activation(aggT[:, :, q * P:(q + 1) * P], psT[q % 2][:, 0:D].rearrange("p (k n) -> p k n", k=KD),
                                  ACT.Copy).then_inc(s_aggT, 1)

                def pieces(sb, nb, q):
                    if q == 0:
                        for m in range(KH):
                            act.wait_ge(s_m1, sb * 4 + (m + 1))
                            ac.activation(h1T[:, m, 0:nb * P], psM[m][:, 0:nb * P], ACT.Relu, bias=b1a[:, m:m + 1]).then_inc(s_h1T, 1)
                    if q == 3:
                        act.wait_ge(s_pre, sb * 4 + (4 + nb))
                        act.wait_ge(s_sto, sb * 32 + 32)
                        ac.activation(hid[:, 0:nb, :], pre[:, 0:nb, :], ACT.Relu).then_inc(s_hid, 1)
                        ac.activation(trow[:, 0:nb, 0:HID], pre[:, 0:nb, :], ACT.Relu).then_inc(s_hid, 1)
                        act.wait_ge(s_res, sb + 1)
                        ac.activation(trow[:, 0:nb, HID:2 * HID], res[:, 0:nb, :], ACT.Copy).then_inc(s_mid, 1)
                        act.wait_ge(s_lo, sb + 1)
                        act.dma_start(rows_of(h_rows, sb, nb), hid[:, 0:nb, :]).then_inc(s_sto, 16)
                        act.dma_start(rows_of(table2, sb, nb), trow[:, 0:nb, :]).then_inc(s_sto, 16)

                pipeline(act, lambda sb, q: None, close, pieces, begin)
                act.wait_ge(s_sto, 32 * (SB + 2))

            @block.vector
            def _(dve):
                v = nc.vector
                dve.sem_inc(s_evac, 2)
                dve.sem_inc(s_pre, 4)
                edges.onehots(dve, 0)
                dve.wait_ge(s_w, 80)
                v.tensor_scalar(eps1[:, :], eps1[:, :], 1.0, None, ALU.add).then_inc(s_eps, 1)
                dve.wait_ge(s_eps, 1)

                def close(sb, q):
                    bank = psA[q % 2]
                    dve.wait_ge(edges.s_agg, sb * 4 + (q + 1))
                    dve.wait_ge(s_self, sb * 16 + 16)
                    v.tensor_scalar(degree[:, bass.ds(sb * 4 + q, 1)], bank[:, D:D + 1], 1.0, None, ALU.add)
                    v.scalar_tensor_tensor(agg[:, q, :], self_x[:, q, :], eps1[:, 0:1], bank[:, 0:D],
                                           ALU.mult, ALU.add).then_inc(s_evac, 1)

                def pieces(sb, nb, q):
                    if q in (2, 3):
                        for j in (2 * q - 4, 2 * q - 3):
                            if j < nb:
                                dve.wait_ge(s_m2, sb * 4 + (j + 1))
                                v.tensor_tensor(pre[:, j, :], psM[j][:, :], b1b[:, :], ALU.add).then_inc(s_pre, 1)
                    if q == 3:
                        dve.wait_ge(s_hid, sb * 2 + 2)
                        v.tensor_tensor(res[:, 0:nb, :], hid[:, 0:nb, :], trow[:, 0:nb, 0:HID], ALU.subtract).then_inc(s_res, 1)
                        dve.wait_ge(s_mid, sb + 1)
                        v.tensor_tensor(trow[:, 0:nb, 2 * HID:3 * HID], res[:, 0:nb, :], trow[:, 0:nb, HID:2 * HID],
                                        ALU.subtract).then_inc(s_lo, 1)

                pipeline(dve, lambda sb, q: edges.next_onehots(dve, sb, q), close, pieces)

            @block.tensor
            def _(pe):
                mm = nc.tensor.matmul
                pe.sem_inc(edges.s_used, edges.AHEAD)
                pe.wait_ge(s_w, 80)

                def items(sb, q):
                    pe.wait_ge(s_evac, sb * 4 + (q + 1))
                    edges.sums(pe, sb * 4 + q, psA[q % 2])

                def close(sb, q):
                    pe.wait_ge(s_evac, sb * 4 + (q + 3))
                    pe.wait_ge(s_aggT, sb * 4 + (q + 1))
                    for k in range(KD):
                        last = nc.tensor.transpose(psT[q % 2][:, k * P:(k + 1) * P], agg[:, q, k * P:(k + 1) * P], ident[:, :])
                    last.then_inc(s_tr, 1)

                def pieces(sb, nb, q):
                    n = nb * P
                    if q == 0:
                        pe.wait_ge(s_aggT, sb * 4 + (nb + 2))
                        for m in range(KH):
                            pe.wait_ge(s_pre, sb * 4 + (m + 1))
                            for k in range(KD):
                                last = mm(psM[m][:, 0:n], w1a[:, k, m * P:(m + 1) * P], aggT[:, k, 0:n], start=k == 0, stop=k == KD - 1)
                            last.then_inc(s_m1, 1)
                    if q in (1, 2):
                        pe.wait_ge(s_h1T, sb * 4 + 4)
                        for j in (2 * q - 2, 2 * q - 1):
                            if j < nb:
                                for k in range(KH):
                                    last = mm(psM[j][:, :], h1T[:, k, j * P:(j + 1) * P], w1b[:, k, :], start=k == 0, stop=k == KH - 1)
                                last.then_inc(s_m2, 1)

                pipeline(pe, items, close, pieces)

        with ExitStack() as stack:
            S = Scope(stack, "s2")
            edges = Edges(S, table2, T2_W, (0, HID, 2 * HID), HID)
            w2a = S.sb("w2a", [P, KH, HID])
            w2b = S.sb("w2b", [P, KH, D])
            b2a = S.sb("b2a", [P, KH])
            b2b = S.sb("b2b", [P, D])
            eps2 = S.sb("eps2", [P, 1])
            self_h = S.sb("self_h", [P, 4, HID])
            agg = S.sb("agg", [P, 4, HID])
            aggT = S.sb("aggT", [P, KH, 4 * P])
            h3T = S.sb("h3T", [P, KH, 4 * P])
            xrow = S.sb("xrow", [P, 4, D])
            x1 = S.sb("x1", [P, 4, D])
            stat = S.sb("stat", [P, 4, 6])
            mv = S.sb("mv", [P, 4, 2])
            var = S.sb("var", [P, 4])
            tmp4 = S.sb("tmp4", [P, 4])
            rstd = S.sb("rstd", [P, 4])
            xl1 = S.sb("xl1", [P, 4, D + 1])
            xl1T = S.sb("xl1T", [P, KD, 4 * P])
            prob = S.sb("prob", [P, 4, HID])
            sw = S.sb("sw", [P, 4, HID])
            gmax = S.sb("gmax", [P, 4 * HEADS])
            gsum = S.sb("gsum", [P, 4 * HEADS])
            swT = S.sb("swT", [P, 4, HID])
            psA = [S.ps(f"psA{i}") for i in range(2)]
            psT = [S.ps(f"psT{i}") for i in range(2)]
            psM = [S.ps(f"psM{i}") for i in range(4)]

            s_w = S.sem("weights")
            s_dve = S.sem("dve_chain")
            s_self = S.sem("self_rows")
            s_x = S.sem("x_rows")
            s_evac = S.sem("sums_copied")
            s_tr = S.sem("sums_transposed")
            s_aggT = S.sem("transposes_copied")
            s_m1 = S.sem("first_product")
            s_h3T = S.sem("first_relu")
            s_m2 = S.sem("second_product")
            s_xl = S.sem("x1_normalised")
            s_t1 = S.sem("second_bank_transposed")
            s_t1c = S.sem("second_bank_copied")
            s_lg = S.sem("logits")
            s_sh = S.sem("logits_less_max")
            s_exp = S.sem("exponentials")
            s_sw = S.sem("slice_weights")
            s_tokp = S.sem("token_products")
            s_tok = S.sem("token_sums")
            s_x1s = S.sem("x1_stored")
            s_sws = S.sem("slice_weights_stored")
            block = stack.enter_context(nc.Block())

            @block.gpsimd
            def _(pool):
                edges.gather(pool)

            @block.sync
            def _(sp):
                edges.relay(sp)

            @block.scalar
            def _(act):
                ac = nc.scalar
                act.dma_start(w2a[:, :, :], a["L0_gnn_W2a"].rearrange("(k p) n -> p k n", p=P)).then_inc(s_w, 16)
                act.dma_start(w2b[:, :, :], a["L0_gnn_W2b"].rearrange("(k p) n -> p k n", p=P)).then_inc(s_w, 16)
                act.dma_start(b2a[:, :], a["L0_gnn_b2a"].rearrange("(m p) -> p m", p=P), allow_slow_non_contiguous=True).then_inc(s_w, 16)
                act.dma_start(b2b[:, :], row_bc(a["L0_gnn_b2b"], D)).then_inc(s_w, 16)
                act.dma_start(eps2[:, :], row_bc(a["L0_gnn_eps2"], 1)).then_inc(s_w, 16)
                act.sem_inc(s_aggT, 1)
                act.sem_inc(s_t1c, 1)
                act.sem_inc(s_x1s, 16)
                act.sem_inc(s_sws, 16)
                act.wait_ge(s_w, 80)

                def begin(sb, nb):
                    act.wait_ge(s_evac, sb * 4 + 2)
                    act.dma_start(self_h[:, 0:nb, :], rows_of(h_rows, sb, nb)).then_inc(s_self, 16)

                def close(sb, q):
                    act.wait_ge(s_tr, sb * 4 + (q + 1))
                    ac.activation(aggT[:, :, q * P:(q + 1) * P], psT[0][:, :].rearrange("p (k n) -> p k n", k=KH),
                                  ACT.Copy).then_inc(s_aggT, 1)

                def pieces(sb, nb, q):
                    if q == 0:
                        act.wait_ge(s_xl, sb * 4 + 4)
                        if nb == 4:
                            act.dma_start(xrow[:, :, :], rows_of(a["x"], sb, 4)).then_inc(s_x, 16)
                        else:
                            act.dma_start(xrow[:, 0, :], xtail).then_inc(s_x, 16)
                        for m in range(KH):
                            act.wait_ge(s_m1, sb * 4 + (m + 1))
                            ac.activation(h3T[:, m, 0:nb * P], psM[m][:, 0:nb * P], ACT.Relu, bias=b2a[:, m:m + 1]).then_inc(s_h3T, 1)
                    if q == 2:
                        act.wait_ge(s_xl, sb * 4 + (nb + 4))
                        act.dma_start(rows_of(x1_rows, sb, nb), x1[:, 0:nb, :]).then_inc(s_x1s, 16)
                        for j in range(nb):
                            act.wait_ge(s_t1, sb * 8 + (j + 1))
                            ac.activation(xl1T[:, :, j * P:(j + 1) * P], psT[1][:, 0:D].rearrange("p (k n) -> p k n", k=KD),
                                          ACT.Copy).then_inc(s_t1c, 1)
                        act.wait_ge(s_sh, sb + 1)
                        ac.activation(prob[:, 0:nb, :], prob[:, 0:nb, :], ACT.Exp).then_inc(s_exp, 1)
                    if q == 3:
                        act.wait_ge(s_sws, sb * 16 + 16)
                        for j in range(nb):
                            act.wait_ge(s_t1, sb * 8 + (nb + j + 1))
                            last = ac.activation(swT[:, j, :], psT[1][:, :], ACT.Copy)
                            last.then_inc(s_t1c, 1)
                        act.wait_ge(s_t1c, sb * 8 + (2 * nb + 1))
                        act.dma_start(swt_rows[bass.ds(sb * 4, nb), :, :].rearrange("q p d -> p q d"), swT[:, 0:nb, :]).then_inc(s_sws, 16)

                pipeline(act, lambda sb, q: None, close, pieces, begin)
                act.wait_ge(s_x1s, 16 * (SB + 2))
                act.wait_ge(s_sws, 16 * (SB + 2))

            @block.vector
            def _(dve):
                v = nc.vector
                ch = Chain(dve, s_dve)
                dve.sem_inc(s_evac, 2)
                dve.sem_inc(s_xl, 4)
                dve.sem_inc(s_tok, 4)
                edges.onehots(dve, 0)
                dve.wait_ge(s_w, 80)
                v.memset(xl1[:, :, D:D + 1], 1.0)
                ch.link(v.tensor_scalar(eps2[:, :], eps2[:, :], 1.0, None, ALU.add))
                ch.restart()

                def close(sb, q):
                    dve.wait_ge(edges.s_agg, sb * 4 + (q + 1))
                    dve.wait_ge(s_self, sb * 16 + 16)
                    v.scalar_tensor_tensor(agg[:, q, :], self_h[:, q, :], eps2[:, 0:1], psA[q % 2][:, :],
                                           ALU.mult, ALU.add).then_inc(s_evac, 1)

                def pieces(sb, nb, q):
                    groups = prob[:, 0:nb, :].rearrange("p q (h g) -> p (q h) g", g=G)
                    if q == 1:
                        dve.wait_ge(s_x, sb * 16 + 16)
                        dve.wait_ge(s_x1s, sb * 16 + 16)
                        for j in range(nb):
                            dve.wait_ge(s_m2, sb * 4 + (j + 1))
                            last = v.tensor_tensor(x1[:, j, :], psM[j][:, 0:D], b2b[:, :], ALU.add)
                        ch.link(last)
                        ch.link(v.tensor_tensor(x1[:, 0:nb, :], x1[:, 0:nb, :], xrow[:, 0:nb, :], ALU.add))
                        for j in range(nb):
                            last = v.bn_stats(stat[:, j, :], x1[:, j, :])
                        ch.link(last)
                        for j in range(nb):
                            last = v.bn_aggr(mv[:, j, :], stat[:, j, :])
                        ch.link(last)
                        ch.link(v.tensor_scalar(var[:, 0:nb], mv[:, 0:nb, 1], LN_EPS, None, ALU.add))
                        rsqrt(ch, rstd[:, 0:nb], var[:, 0:nb], tmp4[:, 0:nb])
                        for j in range(nb):
                            v.tensor_scalar(xl1[:, j, 0:D], x1[:, j, :], mv[:, j, 0:1], rstd[:, j:j + 1],
                                            ALU.subtract, ALU.mult).then_inc(s_xl, 1)
                        ch.restart()
                    if q == 2:
                        for j in range(nb):
                            dve.wait_ge(s_lg, sb * 4 + (j + 1))
                            last = v.tensor_tensor(prob[:, j, :], psM[j][:, :], slice_b[:, :], ALU.add)
                        ch.link(last)
                        ch.link(v.tensor_reduce(gmax[:, 0:nb * HEADS], groups, AX, ALU.max))
                        v.tensor_tensor(groups, groups, gmax[:, 0:nb * HEADS].unsqueeze(2).to_broadcast([P, nb * HEADS, G]),
                                        ALU.subtract).then_inc(s_sh, 1)
                        dve.wait_ge(s_exp, sb + 1)
                        ch.link(v.tensor_reduce(gsum[:, 0:nb * HEADS], groups, AX, ALU.add))
                        ch.link(v.reciprocal(gsum[:, 0:nb * HEADS], gsum[:, 0:nb * HEADS]))
                        v.tensor_tensor(sw[:, 0:nb, :].rearrange("p q (h g) -> p (q h) g", g=G), groups,
                                        gsum[:, 0:nb * HEADS].unsqueeze(2).to_broadcast([P, nb * HEADS, G]),
                                        ALU.mult).then_inc(s_sw, 1)
                        ch.restart()
                    if q == 3:
                        for c in range(KH):
                            dve.wait_ge(s_tokp, sb * 4 + (c + 1))
                            v.tensor_tensor(tok[:, c, :], tok[:, c, :], psM[c][:, 0:D + 1], ALU.add).then_inc(s_tok, 1)

                pipeline(dve, lambda sb, q: edges.next_onehots(dve, sb, q), close, pieces)

            @block.tensor
            def _(pe):
                mm = nc.tensor.matmul
                pe.sem_inc(edges.s_used, edges.AHEAD)
                pe.wait_ge(s_w, 80)

                def items(sb, q):
                    pe.wait_ge(s_evac, sb * 4 + (q + 1))
                    edges.sums(pe, sb * 4 + q, psA[q % 2])

                def close(sb, q):
                    pe.wait_ge(s_evac, sb * 4 + (q + 3))
                    pe.wait_ge(s_aggT, sb * 4 + (q + 1))
                    for k in range(KH):
                        last = nc.tensor.transpose(psT[0][:, k * P:(k + 1) * P], agg[:, q, k * P:(k + 1) * P], ident[:, :])
                    last.then_inc(s_tr, 1)

                def logits(sb, j):
                    pe.wait_ge(s_t1c, sb * 8 + (j + 2))
                    for k in range(KD):
                        last = mm(psM[j][:, :], xl1T[:, k, j * P:(j + 1) * P], slice_w[:, k, :], start=k == 0, stop=k == KD - 1)
                    last.then_inc(s_lg, 1)

                def pieces(sb, nb, q):
                    n = nb * P
                    if q == 0:
                        pe.wait_ge(s_aggT, sb * 4 + (nb + 1))
                        for m in range(KH):
                            pe.wait_ge(s_tok, sb * 4 + (m + 1))
                            for k in range(KH):
                                last = mm(psM[m][:, 0:n], w2a[:, k, m * P:(m + 1) * P], aggT[:, k, 0:n], start=k == 0, stop=k == KH - 1)
                            last.then_inc(s_m1, 1)
                    if q == 1:
                        pe.wait_ge(s_h3T, sb * 4 + 4)
                        for j in range(nb):
                            for k in range(KH):
                                last = mm(psM[j][:, 0:D], h3T[:, k, j * P:(j + 1) * P], w2b[:, k, :], start=k == 0, stop=k == KH - 1)
                            last.then_inc(s_m2, 1)
                    if q == 2:
                        for j in range(nb):
                            pe.wait_ge(s_xl, sb * 4 + (j + 5))
                            pe.wait_ge(s_t1c, sb * 8 + (j + 1))
                            for k in range(KD):
                                last = nc.tensor.transpose(psT[1][:, k * P:(k + 1) * P], xl1[:, j, k * P:(k + 1) * P], ident[:, :])
                            last.then_inc(s_t1, 1)
                            if j >= 1:
                                logits(sb, j - 1)
                        logits(sb, nb - 1)
                    if q == 3:
                        pe.wait_ge(s_sw, sb + 1)
                        for j in range(nb):
                            pe.wait_ge(s_t1c, sb * 8 + (nb + j + 1))
                            for c in range(KH):
                                last = nc.tensor.transpose(psT[1][:, c * P:(c + 1) * P], sw[:, j, c * P:(c + 1) * P], ident[:, :])
                            last.then_inc(s_t1, 1)
                            k = P if nb == 4 else TAIL
                            for c in range(KH):
                                last = mm(psM[c][:, 0:D + 1], sw[0:k, j, c * P:(c + 1) * P], xl1[0:k, j, :],
                                          start=j == 0, stop=j == nb - 1)
                                if j == nb - 1:
                                    last.then_inc(s_tokp, 1)

                pipeline(pe, items, close, pieces)

        with ExitStack() as stack:
            S = Scope(stack, "s3")
            wfx = S.sb("wfx", [P, KD, HID])
            bfx = S.sb("bfx", [P, HID])
            wqkv = S.sb("wqkv", [P, 3, HD])
            wbd = S.sb("wbd", [P, 3, P])
            wout = S.sb("wout", [P, KH, D])
            bout = S.sb("bout", [P, D])
            tokT = S.sb("tokT", [P, KD, HID])
            rnorm = S.sb("rnorm", [P, KH])
            stok = S.sb("stok", [P, KH, P])
            stokT = S.sb("stokT", [P, KH, P])
            qT = S.sb("qT", [P, KH, P])
            kT = S.sb("kT", [P, KH, P])
            val = S.sb("val", [P, KH, P])
            score = S.sb("score", [P, KH, HD])
            smax = S.sb("smax", [P, KH])
            ssum = S.sb("ssum", [P, KH])
            pbd = S.sb("pbd", [P, KH, P])
            pbdT = S.sb("pbdT", [P, KH, P])
            osT = S.sb("osT", [P, KH, P])
            mix = S.sb("mix", [P, KH, D])
            dtmp = S.sb("dtmp", [P, NB])
            swT = S.sb("swT", [P, 2, 4, HID])
            x1 = S.sb("x1", [P, 2, 4, D])
            x2 = S.sb("x2", [P, 4, D])
            stat = S.sb("stat", [P, 4, 6])
            mv = S.sb("mv", [P, 4, 2])
            var = S.sb("var", [P, 4])
            tmp4 = S.sb("tmp4", [P, 4])
            rstd = S.sb("rstd", [P, 4])
            vrow = S.sb("vrow", [P, 4, D])
            res = S.sb("res", [P, 4, D])
            trow = S.sb("trow", [P, 4, T3_W], BF16)
            psM = [S.ps(f"psM{i}") for i in range(4)]
            psX = [S.ps(f"psX{i}") for i in range(3)]

            s_w = S.sem("weights")
            s_dve = S.sem("dve_chain")
            s_pe = S.sem("attention_products")
            s_at = S.sem("attention_operands")
            s_ex = S.sem("attention_exponentials")
            s_in = [S.sem(f"rows_loaded{i}") for i in range(2)]
            s_mm = S.sem("products")
            s_x2 = S.sem("x2_rows")
            s_v = S.sem("scaled_rows")
            s_hi = S.sem("high_part")
            s_res = S.sem("residual")
            s_mid = S.sem("middle_part")
            s_lo = S.sem("low_part")
            s_sto = S.sem("rows_stored")
            block = stack.enter_context(nc.Block())

            @block.sync
            def _(sp):
                sp.dma_start(wfx[:, :, :], a["L0_ffn_W_fx"].rearrange("(k p) n -> p k n", p=P)).then_inc(s_w, 16)
                sp.dma_start(bfx[:, :], row_bc(a["L0_ffn_b_fx"], HID)).then_inc(s_w, 16)
                for i, name in enumerate(("L0_ffn_W_q", "L0_ffn_W_k", "L0_ffn_W_v")):
                    for h in range(2):
                        sp.dma_start(wqkv[h * HD:(h + 1) * HD, i, :], a[name]).then_inc(s_w, 16)
                sp.dma_start(wout[:, :, :], a["L0_ffn_W_out"].rearrange("(c p) n -> p c n", p=P)).then_inc(s_w, 16)
                sp.dma_start(bout[:, :], row_bc(a["L0_ffn_b_out"], D)).then_inc(s_w, 16)

                def load(sb, nb, par):
                    sp.wait_ge(s_v, sb + 1)
                    sp.dma_start(swT[:, par, 0:nb, :], swt_rows[bass.ds(sb * 4, nb), :, :].rearrange("q p d -> p q d")).then_inc(s_in[par], 16)
                    sp.dma_start(x1[:, par, 0:nb, :], rows_of(x1_rows, sb, nb)).then_inc(s_in[par], 16)

                with sp.Fori(0, SB // 2) as it:
                    for par in range(2):
                        load(it * 2 + par, 4, par)
                load(SB, 1, 0)
                sp.wait_ge(s_in[0], 32 * (SB // 2 + 1))
                sp.wait_ge(s_in[1], 32 * (SB // 2))

            @block.vector
            def _(dve):
                v = nc.vector
                ch = Chain(dve, s_dve)
                dve.sem_inc(s_x2, 8)
                dve.sem_inc(s_v, 2)
                for t in (wbd, stok, pbd):
                    last = v.memset(t[:, :, :], 0.0)
                ch.link(last)
                dve.wait_ge(s_w, 16 * 10)
                for i in range(3):
                    for h in range(2):
                        rows = slice(h * HD, (h + 1) * HD)
                        last = v.tensor_copy(wbd[rows, i, rows], wqkv[rows, i, :])
                ch.link(v.tensor_scalar(rnorm[:, :], tok[:, :, D], 1e-5, None, ALU.add))
                ch.link(v.reciprocal(rnorm[:, :], rnorm[:, :]))
                for k in range(KD):
                    dve.wait_ge(s_pe, 1)
                    last = v.tensor_copy(tokT[:, k, :], psX[k][:, :])
                last.then_inc(s_at, 1)
                dve.wait_ge(s_pe, 2)
                for c in range(KH):
                    for h in range(2):
                        rows = slice(h * HD, (h + 1) * HD)
                        cols = slice(c * P + h * HD, c * P + (h + 1) * HD)
                        last = v.scalar_tensor_tensor(stok[rows, c, rows], bfx[rows, cols], tok[rows, c, D:D + 1], psX[2][rows, cols],
                                                      ALU.mult, ALU.add)
                ch.link(last)
                for c in range(KH):
                    last = v.tensor_scalar(stok[:, c, :], stok[:, c, :], rnorm[:, c:c + 1], None, ALU.mult)
                last.then_inc(s_at, 1)
                dve.wait_ge(s_pe, 3)
                v.tensor_copy(stokT[:, :, :], psX[0][:, :].rearrange("p (c j) -> p c j", c=KH)).then_inc(s_at, 1)
                dve.wait_ge(s_pe, 4)
                for t, ps in ((qT, psX[0]), (kT, psX[1]), (val, psX[2])):
                    last = v.tensor_copy(t[:, :, :], ps[:, :].rearrange("p (c j) -> p c j", c=KH))
                last.then_inc(s_at, 1)
                dve.wait_ge(s_pe, 5)
                for h in range(2):
                    rows = slice(h * HD, (h + 1) * HD)
                    last = v.tensor_scalar(score[rows, :, :], psX[0][rows, :].rearrange("p (c j) -> p c j", c=KH)[:, :, rows],
                                           float(HD) ** -0.5, None, ALU.mult)
                ch.link(last)
                ch.link(v.tensor_reduce(smax[:, :], score[:, :, :], AX, ALU.max))
                v.tensor_tensor(score[:, :, :], score[:, :, :], smax[:, :].unsqueeze(2).to_broadcast([P, KH, HD]),
                                ALU.subtract).then_inc(s_at, 1)
                dve.wait_ge(s_ex, 1)
                ch.link(v.tensor_reduce(ssum[:, :], score[:, :, :], AX, ALU.add))
                ch.link(v.reciprocal(ssum[:, :], ssum[:, :]))
                for h in range(2):
                    rows = slice(h * HD, (h + 1) * HD)
                    last = v.tensor_tensor(pbd[rows, :, rows], score[rows, :, :], ssum[rows, :].unsqueeze(2).to_broadcast([HD, KH, HD]), ALU.mult)
                last.then_inc(s_at, 1)
                dve.wait_ge(s_pe, 6)
                v.tensor_copy(pbdT[:, :, :], psX[1][:, :].rearrange("p (c j) -> p c j", c=KH)).then_inc(s_at, 1)
                dve.wait_ge(s_pe, 7)
                v.tensor_copy(osT[:, :, :], psX[0][:, :].rearrange("p (c j) -> p c j", c=KH)).then_inc(s_at, 1)
                dve.wait_ge(s_pe, 8)
                v.tensor_copy(mix[:, 0:2, :], psX[1][:, :].rearrange("p (c j) -> p c j", c=2))
                v.tensor_copy(mix[:, 2:4, :], psX[2][:, :].rearrange("p (c j) -> p c j", c=2)).then_inc(s_at, 1)
                rsqrt(ch, dinv[:, :], degree[:, :], dtmp[:, :])
                ch.restart()

                def body(sb, nb, par, it):
                    dve.wait_ge(s_in[par], it * 32 + 32)
                    dve.wait_ge(s_sto, sb * 48 + 48)
                    for j in range(nb):
                        dve.wait_ge(s_mm, sb * 4 + (j + 1))
                        last = v.tensor_tensor(x2[:, j, :], psM[j][:, 0:D], bout[:, :], ALU.add)
                        last.then_inc(s_x2, 1)
                    dve.wait_ge(s_x2, sb * 4 + (nb + 8))
                    ch.link(v.tensor_tensor(x2[:, 0:nb, :], x2[:, 0:nb, :], x1[:, par, 0:nb, :], ALU.add))
                    for j in range(nb):
                        last = v.bn_stats(stat[:, j, :], x2[:, j, :])
                    ch.link(last)
                    for j in range(nb):
                        last = v.bn_aggr(mv[:, j, :], stat[:, j, :])
                    ch.link(last)
                    ch.link(v.tensor_scalar(var[:, 0:nb], mv[:, 0:nb, 1], LN_EPS, None, ALU.add))
                    rsqrt(ch, rstd[:, 0:nb], var[:, 0:nb], tmp4[:, 0:nb])
                    ch.link(v.tensor_tensor(rstd[:, 0:nb], rstd[:, 0:nb], dinv[:, bass.ds(sb * 4, nb)], ALU.mult))
                    for j in range(nb):
                        last = v.tensor_scalar(vrow[:, j, :], x2[:, j, :], mv[:, j, 0:1], rstd[:, j:j + 1], ALU.subtract, ALU.mult)
                    last.then_inc(s_v, 1)
                    dve.wait_ge(s_hi, sb + 1)
                    v.tensor_tensor(res[:, 0:nb, :], vrow[:, 0:nb, :], trow[:, 0:nb, 0:D], ALU.subtract).then_inc(s_res, 1)
                    dve.wait_ge(s_mid, sb + 1)
                    v.tensor_tensor(trow[:, 0:nb, 2 * D:3 * D], res[:, 0:nb, :], trow[:, 0:nb, D:2 * D], ALU.subtract).then_inc(s_lo, 1)
                    ch.restart()

                with dve.Fori(0, SB // 2) as it:
                    for par in range(2):
                        body(it * 2 + par, 4, par, it)
                body(SB, 1, 0, SB // 2)

            @block.scalar
            def _(act):
                ac = nc.scalar
                act.sem_inc(s_sto, 48)
                act.wait_ge(s_at, 5)
                ac.activation(score[:, :, :], score[:, :, :], ACT.Exp).then_inc(s_ex, 1)

                def body(sb, nb):
                    act.wait_ge(s_v, sb + 3)
                    ac.activation(trow[:, 0:nb, 0:D], vrow[:, 0:nb, :], ACT.Copy).then_inc(s_hi, 1)
                    act.dma_start(rows_of(x2_rows, sb, nb), x2[:, 0:nb, :]).then_inc(s_sto, 16)
                    act.dma_start(rows_of(v_rows, sb, nb), vrow[:, 0:nb, :]).then_inc(s_sto, 16)
                    act.wait_ge(s_res, sb + 1)
                    ac.activation(trow[:, 0:nb, D:2 * D], res[:, 0:nb, :], ACT.Copy).then_inc(s_mid, 1)
                    act.wait_ge(s_lo, sb + 1)
                    act.dma_start(rows_of(table3, sb, nb), trow[:, 0:nb, :]).then_inc(s_sto, 16)

                superblocks(act, body)
                act.wait_ge(s_sto, 48 * (SB + 2))

            @block.tensor
            def _(pe):
                mm = nc.tensor.matmul
                pairs = [slice(c * P, (c + 1) * P) for c in range(KH)]
                for k in range(KD):
                    for c in range(KH):
                        last = nc.tensor.transpose(psX[k][:, pairs[c]], tok[:, c, k * P:(k + 1) * P], ident[:, :])
                last.then_inc(s_pe, 1)
                pe.wait_ge(s_at, 1)
                for c in range(KH):
                    for k in range(KD):
                        last = mm(psX[2][:, pairs[c]], tokT[:, k, pairs[c]], wfx[:, k, pairs[c]], start=k == 0, stop=k == KD - 1)
                last.then_inc(s_pe, 1)
                pe.wait_ge(s_at, 2)
                for c in range(KH):
                    last = nc.tensor.transpose(psX[0][:, pairs[c]], stok[:, c, :], ident[:, :])
                last.then_inc(s_pe, 1)
                pe.wait_ge(s_at, 3)
                for c in range(KH):
                    mm(psX[0][:, pairs[c]], wbd[:, 0, :], stokT[:, c, :], start=True, stop=True)
                    mm(psX[1][:, pairs[c]], wbd[:, 1, :], stokT[:, c, :], start=True, stop=True)
                    last = mm(psX[2][:, pairs[c]], stokT[:, c, :], wbd[:, 2, :], start=True, stop=True)
                last.then_inc(s_pe, 1)
                pe.wait_ge(s_at, 4)
                for c in range(KH):
                    last = mm(psX[0][:, pairs[c]], qT[:, c, :], kT[:, c, :], start=True, stop=True)
                last.then_inc(s_pe, 1)
                pe.wait_ge(s_at, 6)
                for c in range(KH):
                    last = nc.tensor.transpose(psX[1][:, pairs[c]], pbd[:, c, :], ident[:, :])
                last.then_inc(s_pe, 1)
                pe.wait_ge(s_at, 7)
                for c in range(KH):
                    last = mm(psX[0][:, pairs[c]], val[:, c, :], pbdT[:, c, :], start=True, stop=True)
                last.then_inc(s_pe, 1)
                pe.wait_ge(s_at, 8)
                for c in range(KH):
                    last = mm(psX[1 + c // 2][:, (c % 2) * D:(c % 2 + 1) * D], osT[:, c, :], wout[:, c, :], start=True, stop=True)
                last.then_inc(s_pe, 1)
                pe.wait_ge(s_at, 9)

                def body(sb, nb, par, it):
                    pe.wait_ge(s_in[par], it * 32 + 32)
                    for j in range(nb):
                        pe.wait_ge(s_x2, sb * 4 + (j + 5))
                        for c in range(KH):
                            last = mm(psM[j][:, 0:D], swT[:, par, j, pairs[c]], mix[:, c, :], start=c == 0, stop=c == KH - 1)
                        last.then_inc(s_mm, 1)

                with pe.Fori(0, SB // 2) as it:
                    for par in range(2):
                        body(it * 2 + par, 4, par, it)
                body(SB, 1, 0, SB // 2)

        with ExitStack() as stack:
            S = Scope(stack, "s4")
            edges = Edges(S, table3, T3_W, (0, D, 2 * D), D)
            w = S.sb("w", [P, KD, D])
            bias = S.sb("bias", [P, D])
            bmean = S.sb("bmean", [P, D])
            bvar = S.sb("bvar", [P, D])
            gamma = S.sb("gamma", [P, D])
            beta = S.sb("beta", [P, D])
            factor = S.sb("factor", [P, D])
            w1 = S.sb("w1", [P, NE, KD, HID])
            w2 = S.sb("w2", [P, NE, KH, D])
            b1 = S.sb("b1", [P, NE, KH])
            b2 = S.sb("b2", [NE, D])
            wg = S.sb("wg", [P, KD, NE])
            bg = S.sb("bg", [P, NE])
            gbias = S.sb("gbias", [P, NE])
            erow = S.sb("erow", [P, 4, NE])
            self_v = S.sb("self_v", [P, 4, D])
            agg = S.sb("agg", [P, 4, D])
            aggT = S.sb("aggT", [P, KD, 4 * P])
            xrow = S.sb("xrow", [P, 4, D])
            acc = S.sb("acc", [P, 4, D])
            stat = S.sb("stat", [P, 4, 6])
            mv = S.sb("mv", [P, 4, 2])
            var = S.sb("var", [P, 4])
            tmp4 = S.sb("tmp4", [P, 4])
            rstd = S.sb("rstd", [P, 4])
            xl3 = S.sb("xl3", [P, 4, D])
            xl3T = S.sb("xl3T", [P, KD, 4 * P])
            gate = S.sb("gate", [P, 4, NE])
            equal = S.sb("equal", [P, 4, NE])
            top = [S.sb(f"top{i}", [P, 4]) for i in range(2)]
            first = S.sb("first", [P, 4])
            pick = [S.sb(f"pick{i}", [P, 4, NE]) for i in range(2)]
            share = [S.sb(f"share{i}", [P, 4]) for i in range(2)]
            ratio = S.sb("ratio", [P, 4])
            comb = S.sb("comb", [P, 4, NE])
            combT = S.sb("combT", [NE, 4 * P])
            hT = S.sb("hT", [P, 2, KH, 4 * P])
            psA = [S.ps(f"psA{i}") for i in range(2)]
            psM = [S.ps(f"psM{i}") for i in range(2)]
            psO = [S.ps(f"psO{i}") for i in range(2)]
            psT = [S.ps(f"psT{i}") for i in range(2)]

            s_wg = S.sem("graph_weights")
            s_we = S.sem("expert_weights")
            s_w = S.sem("scaled_weights")
            s_dve = S.sem("dve_chain")
            s_self = S.sem("self_rows")
            s_x = S.sem("x2_rows")
            s_evac = S.sem("sums_copied")
            s_tr = S.sem("sums_transposed")
            s_aggT = S.sem("transposes_copied")
            s_o = S.sem("row_products")
            s_acc = S.sem("row_products_used")
            s_xl = S.sem("x3_normalised")
            s_t1 = S.sem("second_bank_transposed")
            s_t1c = S.sem("second_bank_copied")
            s_gate = S.sem("gates")
            s_diff = S.sem("gate_differences")
            s_exp = S.sem("gate_exponentials")
            s_comb = S.sem("gate_shares")
            s_up = S.sem("up_products")
            s_h = S.sem("expert_hidden")
            s_sto = S.sem("output_stored")
            block = stack.enter_context(nc.Block())

            MOE = {0: (),
                   1: (("up", 0), ("up", 1), ("down", 0), ("up", 2), ("down", 1)),
                   2: (("up", 3), ("down", 2), ("up", 4), ("down", 3), ("up", 5), ("down", 4)),
                   3: (("up", 6), ("down", 5), ("up", 7), ("down", 6), ("down", 7), ("down", NE))}

            @block.gpsimd
            def _(pool):
                edges.gather(pool)

            @block.sync
            def _(sp):
                edges.relay(sp)

            @block.scalar
            def _(act):
                ac = nc.scalar
                act.dma_start(w[:, :, :], a["L1_gnn_W"].rearrange("(k p) n -> p k n", p=P)).then_inc(s_wg, 16)
                for t, name in ((bias, "L1_gnn_b"), (bmean, "L1_gnn_running_mean"), (bvar, "L1_gnn_running_var"),
                                (gamma, "L1_gnn_gamma"), (beta, "L1_gnn_beta")):
                    act.dma_start(t[:, :], row_bc(a[name], D)).then_inc(s_wg, 16)
                act.dma_start(bg[:, :], row_bc(a["L1_ffn_bg"], NE)).then_inc(s_wg, 16)
                act.dma_start(gbias[:, :], row_bc(a["L1_ffn_bias"], NE)).then_inc(s_wg, 16)
                act.dma_start(wg[:, :, :], a["L1_ffn_Wg"].rearrange("(k p) n -> p k n", p=P)).then_inc(s_we, 16)
                act.dma_start(b2[:, :], a["L1_ffn_b2"]).then_inc(s_we, 16)
                act.dma_start(b1[:, :, :], a["L1_ffn_b1"].rearrange("e (m p) -> p e m", p=P), allow_slow_non_contiguous=True).then_inc(s_we, 16)
                act.dma_start(w1[:, :, :, :], a["L1_ffn_W1"].rearrange("e (k p) n -> p e k n", p=P)).then_inc(s_we, 16)
                act.dma_start(w2[:, :, :, :], a["L1_ffn_W2"].rearrange("e (k p) n -> p e k n", p=P)).then_inc(s_we, 16)
                act.sem_inc(s_aggT, 1)
                act.sem_inc(s_t1c, 1)
                act.sem_inc(s_h, 2)
                act.sem_inc(s_sto, 16)

                def begin(sb, nb):
                    act.wait_ge(s_evac, sb * 4 + 2)
                    act.dma_start(self_v[:, 0:nb, :], rows_of(v_rows, sb, nb)).then_inc(s_self, 16)

                def close(sb, q):
                    act.wait_ge(s_tr, sb * 4 + (q + 1))
                    ac.activation(aggT[:, :, q * P:(q + 1) * P], psT[0][:, 0:D].rearrange("p (k n) -> p k n", k=KD),
                                  ACT.Copy).then_inc(s_aggT, 1)

                def up(sb, nb, e):
                    act.wait_ge(s_o, sb * 40 + nb * max(e, 1))
                    for m in range(KH):
                        act.wait_ge(s_up, sb * 32 + (e * KH + m + 1))
                        ac.activation(hT[:, e % 2, m, 0:nb * P], psM[m % 2][:, 0:nb * P], ACT.Relu,
                                      bias=b1[:, e, m:m + 1]).then_inc(s_h, 1)

                def pieces(sb, nb, q):
                    if q == 0:
                        act.wait_ge(s_xl, sb * 4 + 4)
                        act.dma_start(xrow[:, 0:nb, :], rows_of(x2_rows, sb, nb)).then_inc(s_x, 16)
                        act.wait_ge(s_we, 16 * 5)
                        act.wait_ge(s_o, sb * 40 + nb)
                    if q == 1:
                        for j in range(nb):
                            act.wait_ge(s_t1, sb * 5 + (j + 1))
                            ac.activation(xl3T[:, :, j * P:(j + 1) * P], psT[1][:, 0:D].rearrange("p (k n) -> p k n", k=KD),
                                          ACT.Copy).then_inc(s_t1c, 1)
                        act.wait_ge(s_diff, sb + 1)
                        ac.activation(ratio[:, 0:nb], ratio[:, 0:nb], ACT.Exp).then_inc(s_exp, 1)
                    for kind, e in MOE[q]:
                        if kind == "up":
                            up(sb, nb, e)
                    if q == 3:
                        act.wait_ge(s_t1, sb * 5 + (nb + 1))
                        ac.activation(combT[:, 0:nb * P], psT[1][0:NE, 0:nb * P], ACT.Copy).then_inc(s_t1c, 1)
                        act.wait_ge(s_acc, sb * 40 + (10 * nb + 2))
                        if nb == 4:
                            act.dma_start(rows_of(out, sb, 4), acc[:, :, :]).then_inc(s_sto, 16)
                        else:
                            act.dma_start(out[N - TAIL:N, :], acc[0:TAIL, 0, :]).then_inc(s_sto, 16)

                pipeline(act, lambda sb, q: None, close, pieces, begin)
                act.wait_ge(s_sto, 16 * (SB + 2))

            @block.vector
            def _(dve):
                v = nc.vector
                ch = Chain(dve, s_dve)
                dve.sem_inc(s_evac, 2)
                dve.sem_inc(s_acc, 2)
                dve.sem_inc(s_xl, 4)
                edges.onehots(dve, 0)
                dve.wait_ge(s_wg, 16 * 8)
                for e in range(NE):
                    last = v.memset(erow[:, :, e:e + 1], float(e - NE))
                ch.link(v.tensor_scalar(bvar[:, :], bvar[:, :], LN_EPS, None, ALU.add))
                rsqrt(ch, factor[:, :], bvar[:, :], xrow[:, 0, :])
                v.tensor_tensor(gbias[:, :], gbias[:, :], bg[:, :], ALU.add)
                v.tensor_tensor(bias[:, :], bias[:, :], bmean[:, :], ALU.subtract)
                ch.link(v.tensor_tensor(factor[:, :], factor[:, :], gamma[:, :], ALU.mult))
                ch.link(v.tensor_tensor(bias[:, :], bias[:, :], factor[:, :], ALU.mult))
                v.tensor_tensor(bias[:, :], bias[:, :], beta[:, :], ALU.add)
                for k in range(KD):
                    last = v.tensor_tensor(w[:, k, :], w[:, k, :], factor[:, :], ALU.mult)
                ch.link(last)
                ch.restart()
                dve.sem_inc(s_w, 1)

                def close(sb, q):
                    dve.wait_ge(edges.s_agg, sb * 4 + (q + 1))
                    dve.wait_ge(s_self, sb * 16 + 16)
                    v.tensor_tensor(agg[:, q, :], self_v[:, q, :], psA[q % 2][:, 0:D], ALU.add).then_inc(s_evac, 1)

                def largest(nb, i):
                    ch.link(v.tensor_reduce(top[i][:, 0:nb], gate[:, 0:nb, :], AX, ALU.max))
                    ch.link(v.tensor_tensor(equal[:, 0:nb, :], gate[:, 0:nb, :],
                                            top[i][:, 0:nb].unsqueeze(2).to_broadcast([P, nb, NE]), ALU.is_equal))
                    ch.link(v.tensor_tensor(equal[:, 0:nb, :], equal[:, 0:nb, :], erow[:, 0:nb, :], ALU.mult))
                    ch.link(v.tensor_reduce(first[:, 0:nb], equal[:, 0:nb, :], AX, ALU.min))
                    ch.link(v.tensor_tensor(pick[i][:, 0:nb, :], erow[:, 0:nb, :],
                                            first[:, 0:nb].unsqueeze(2).to_broadcast([P, nb, NE]), ALU.is_equal))

                def down(sb, nb, e):
                    for j in range(nb):
                        i = (e + 1) * nb + j
                        dve.wait_ge(s_o, sb * 40 + (i + 1))
                        if e < NE:
                            v.scalar_tensor_tensor(acc[:, j, :], psO[j % 2][:, 0:D], comb[:, j, e:e + 1], acc[:, j, :],
                                                   ALU.mult, ALU.add).then_inc(s_acc, 1)
                        else:
                            v.tensor_tensor(acc[:, j, :], acc[:, j, :], psO[j % 2][:, 0:D], ALU.add).then_inc(s_acc, 1)

                def pieces(sb, nb, q):
                    if q == 0:
                        dve.wait_ge(s_sto, sb * 16 + 16)
                        dve.wait_ge(s_x, sb * 16 + 16)
                        for j in range(nb):
                            dve.wait_ge(s_o, sb * 40 + (j + 1))
                            v.scalar_tensor_tensor(acc[:, j, :], psO[j % 2][:, 0:D], dinv[:, bass.ds(sb * 4 + j, 1)], bias[:, :],
                                                   ALU.mult, ALU.add).then_inc(s_acc, 1)
                        dve.wait_ge(s_acc, sb * 40 + (nb + 2))
                        ch.link(v.scalar_tensor_tensor(acc[:, 0:nb, :], acc[:, 0:nb, :], 0.0, xrow[:, 0:nb, :], ALU.max, ALU.add))
                        for j in range(nb):
                            last = v.bn_stats(stat[:, j, :], acc[:, j, :])
                        ch.link(last)
                        for j in range(nb):
                            last = v.bn_aggr(mv[:, j, :], stat[:, j, :])
                        ch.link(last)
                        ch.link(v.tensor_scalar(var[:, 0:nb], mv[:, 0:nb, 1], LN_EPS, None, ALU.add))
                        rsqrt(ch, rstd[:, 0:nb], var[:, 0:nb], tmp4[:, 0:nb])
                        for j in range(nb):
                            v.tensor_scalar(xl3[:, j, :], acc[:, j, :], mv[:, j, 0:1], rstd[:, j:j + 1],
                                            ALU.subtract, ALU.mult).then_inc(s_xl, 1)
                        ch.restart()
                    if q == 1:
                        dve.wait_ge(s_gate, sb * 4 + nb)
                        for j in range(nb):
                            last = v.tensor_tensor(gate[:, j, :], psT[1][:, D + j * NE:D + (j + 1) * NE], gbias[:, :], ALU.add)
                        ch.link(last)
                        largest(nb, 0)
                        ch.link(v.scalar_tensor_tensor(gate[:, 0:nb, :], pick[0][:, 0:nb, :], -3e38, gate[:, 0:nb, :], ALU.mult, ALU.add))
                        largest(nb, 1)
                        v.tensor_tensor(ratio[:, 0:nb], top[1][:, 0:nb], top[0][:, 0:nb], ALU.subtract).then_inc(s_diff, 1)
                        dve.wait_ge(s_exp, sb + 1)
                        ch.link(v.tensor_scalar(share[0][:, 0:nb], ratio[:, 0:nb], 1.0, None, ALU.add))
                        ch.link(v.reciprocal(share[0][:, 0:nb], share[0][:, 0:nb]))
                        ch.link(v.tensor_tensor(share[1][:, 0:nb], ratio[:, 0:nb], share[0][:, 0:nb], ALU.mult))
                        for i in range(2):
                            last = v.tensor_tensor(pick[i][:, 0:nb, :], pick[i][:, 0:nb, :],
                                                   share[i][:, 0:nb].unsqueeze(2).to_broadcast([P, nb, NE]), ALU.mult)
                        ch.link(last)
                        ch.link(v.tensor_tensor(comb[:, 0:nb, :], pick[0][:, 0:nb, :], pick[1][:, 0:nb, :], ALU.add))
                        ch.restart()
                        dve.sem_inc(s_comb, 1)
                    for kind, e in MOE[q]:
                        if kind == "down":
                            down(sb, nb, e)

                pipeline(dve, lambda sb, q: edges.next_onehots(dve, sb, q), close, pieces)

            @block.tensor
            def _(pe):
                mm = nc.tensor.matmul
                pe.sem_inc(edges.s_used, edges.AHEAD)

                def items(sb, q):
                    pe.wait_ge(s_evac, sb * 4 + (q + 1))
                    edges.sums(pe, sb * 4 + q, psA[q % 2])

                def close(sb, q):
                    pe.wait_ge(s_evac, sb * 4 + (q + 3))
                    pe.wait_ge(s_aggT, sb * 4 + (q + 1))
                    for k in range(KD):
                        last = nc.tensor.transpose(psT[0][:, k * P:(k + 1) * P], agg[:, q, k * P:(k + 1) * P], ident[:, :])
                    last.then_inc(s_tr, 1)

                def bank_free(sb, nb, i):
                    pe.wait_ge(s_acc, sb * 40 + (i + (1 if nb > 1 else 2)))

                def gates(sb, j):
                    for k in range(KD):
                        last = mm(psT[1][:, D + j * NE:D + (j + 1) * NE], xl3T[:, k, j * P:(j + 1) * P], wg[:, k, :],
                                  start=k == 0, stop=k == KD - 1)
                    last.then_inc(s_gate, 1)

                def up(sb, nb, e):
                    for m in range(KH):
                        pe.wait_ge(s_h, sb * 32 + (e * KH + m + 1))
                        for k in range(KD):
                            last = mm(psM[m % 2][:, 0:nb * P], w1[:, e, k, m * P:(m + 1) * P], xl3T[:, k, 0:nb * P],
                                      start=k == 0, stop=k == KD - 1)
                        last.then_inc(s_up, 1)

                def down(sb, nb, e):
                    pe.wait_ge(s_h, sb * 32 + (e * KH + KH + 2))
                    for j in range(nb):
                        bank_free(sb, nb, (e + 1) * nb + j)
                        for k in range(KH):
                            last = mm(psO[j % 2][:, 0:D], hT[:, e % 2, k, j * P:(j + 1) * P], w2[:, e, k, :],
                                      start=k == 0, stop=k == KH - 1)
                        last.then_inc(s_o, 1)

                def shares_transposed(sb, nb):
                    pe.wait_ge(s_t1c, sb * 5 + (nb + 1))
                    pe.wait_ge(s_comb, sb + 1)
                    for j in range(nb):
                        last = nc.tensor.transpose(psT[1][0:NE, j * P:(j + 1) * P], comb[:, j, :], ident[:, :])
                    last.then_inc(s_t1, 1)

                def bias_term(sb, nb):
                    pe.wait_ge(s_t1c, sb * 5 + (nb + 2))
                    for j in range(nb):
                        bank_free(sb, nb, 9 * nb + j)
                        mm(psO[j % 2][:, 0:D], combT[:, j * P:(j + 1) * P], b2[:, :], start=True, stop=True).then_inc(s_o, 1)

                def pieces(sb, nb, q):
                    if q == 0:
                        pe.wait_ge(s_w, 1)
                        pe.wait_ge(s_we, 16 * 5)
                        pe.wait_ge(s_aggT, sb * 4 + (nb + 1))
                        for j in range(nb):
                            bank_free(sb, nb, j)
                            for k in range(KD):
                                last = mm(psO[j % 2][:, 0:D], aggT[:, k, j * P:(j + 1) * P], w[:, k, :], start=k == 0, stop=k == KD - 1)
                            last.then_inc(s_o, 1)
                    if q == 1:
                        for j in range(nb):
                            pe.wait_ge(s_xl, sb * 4 + (j + 5))
                            pe.wait_ge(s_t1c, sb * 5 + (j + 1))
                            for k in range(KD):
                                last = nc.tensor.transpose(psT[1][:, k * P:(k + 1) * P], xl3[:, j, k * P:(k + 1) * P], ident[:, :])
                            last.then_inc(s_t1, 1)
                        pe.wait_ge(s_t1c, sb * 5 + (nb + 1))
                        for j in range(nb):
                            gates(sb, j)
                    for kind, e in MOE[q]:
                        if kind == "up":
                            up(sb, nb, e)
                        elif e < NE:
                            if e == NE - 1:
                                shares_transposed(sb, nb)
                            down(sb, nb, e)
                        else:
                            bias_term(sb, nb)

                pipeline(pe, items, close, pieces)


def kernel(**inputs):
    import numpy as _np
    import concourse.bacc as _bacc
    from concourse import mybir as _mybir
    from concourse.bass_utils import run_bass_kernel_spmd as _run

    nc = _bacc.Bacc("TRN2", target_bir_lowering=False, num_devices=1)
    arrays, args = {}, {}
    for name, value in inputs.items():
        array = _np.ascontiguousarray(_np.atleast_1d(_np.asarray(value)))
        arrays[f"in_{name}_dram"] = array
        args[name] = nc.dram_tensor(f"in_{name}_dram", array.shape, _mybir.dt.from_np(array.dtype), kind="ExternalInput").ap()
    out = nc.dram_tensor("out_0_dram", (N, D), FP32, kind="ExternalOutput").ap()
    build(nc, args, out)
    result = _run(nc, [arrays], core_ids=[0])
    return result.results[0]["out_0_dram"]
```

```python
import concourse.bass as bass
from concourse import mybir
from contextlib import ExitStack

FP32 = mybir.dt.float32
BF16 = mybir.dt.bfloat16
I32 = mybir.dt.int32
ALU = mybir.AluOpType
ACT = mybir.ActivationFunctionType
AX = mybir.AxisListType.X

P = 128
N = 6250
E = 106250
D = 256
HID = 512
NB = -(-N // P)
NPAD = NB * P
TAIL = N - (NB - 1) * P
SB = NB // 4
HEADS, HD, G = 8, 64, 64
NE = 8
LN_EPS = 1e-5
KD, KH = D // P, HID // P

PAIR = 2 * P
RING = 8
SLOTS = 2 * RING
PAIRS_MAX = E // PAIR + NB + 1
TILES = -(-(2 * (PAIRS_MAX + RING + RING)) // P) * P
TC = TILES // P
E_LAST = -(-(E + P) // P) * P
E_PAD = E_LAST + P
DE, ER = 125, E // 125

TM = -(-(2 * NPAD // P + NE) // 4) * 4
SCAT = 7
T1_MID, T1_LO, T1_HI, T1_W = 0, D, 2 * D, 3 * D + 2
T2_W, T3_W = 3 * HID, 3 * D


def build(nc, a, out):
    with ExitStack() as whole:

        def dram(name, shape, dt):
            return nc.dram_tensor(name, shape, dt, kind="Internal").ap()

        def row_bc(ap, n):
            return ap.rearrange("(a n) -> a n", a=1).to_broadcast([P, n])

        src_pad = dram("src_pad", [E_PAD, 1], I32)
        dst_pad = dram("dst_pad", [E_PAD, 1], I32)
        xtail = dram("xtail", [P, D], FP32)
        xl_rows = dram("xl_rows", [NPAD, D], FP32)
        table1 = dram("table1", [NPAD, T1_W], BF16)
        h_rows = dram("h_rows", [NPAD, HID], FP32)
        table2 = dram("table2", [NPAD, T2_W], BF16)
        x1_rows = dram("x1_rows", [NPAD, D], FP32)
        swt_rows = dram("swt_rows", [NB, P, KH * P], FP32)
        x2_rows = dram("x2_rows", [NPAD, D], FP32)
        v_rows = dram("v_rows", [NPAD, D], FP32)
        table3 = dram("table3", [NPAD, T3_W], BF16)

        x3_rows = dram("x3_rows", [NPAD, D], FP32)
        xl3_rows = dram("xl3_rows", [NPAD, D], FP32)
        slot_node = dram("slot_node", [TM * P, 1], I32)
        y_slots = dram("y_slots", [TM * P, D], FP32)

        class Scope:

            def __init__(self, stack, tag):
                self.stack, self.tag, self.sems = stack, tag, []
                stack.callback(self.end)

            def end(self):
                if self.sems:
                    nc.clear_and_free_semaphores(self.sems)
                    nc.all_engine_barrier()

            def sb(self, name, shape, dt=FP32):
                return self.stack.enter_context(nc.sbuf_tensor(f"{self.tag}_{name}", shape, dt))

            def ps(self, name, shape=(P, 512), dt=FP32):
                return self.stack.enter_context(nc.psum_tensor(f"{self.tag}_{name}", list(shape), dt))

            def sem(self, name):
                self.sems.append(nc.alloc_semaphore(name=f"{self.tag}_{name}"))
                return self.sems[-1]

        class Chain:

            def __init__(self, eng, sem):
                self.eng, self.sem, self.n = eng, sem, 0

            def link(self, ins):
                self.n += 1
                ins.then_inc(self.sem, 1)
                self.eng.wait_ge(self.sem, self.n)

            def restart(self):
                self.eng.sem_clear(self.sem)
                self.n = 0

        def rsqrt(ch, out, x, tmp):
            v = nc.vector
            ch.link(v.tensor_scalar(tmp.bitcast(I32), x.bitcast(I32), 1, None, ALU.arith_shift_right))
            ch.link(v.tensor_scalar(out.bitcast(I32), tmp.bitcast(I32), -1.0, float(0x5F3759DF), ALU.mult, ALU.add))
            for _ in range(3):
                ch.link(v.tensor_tensor(tmp, out, out, ALU.mult))
                ch.link(v.tensor_tensor(tmp, tmp, x, ALU.mult))
                ch.link(v.tensor_scalar(tmp, tmp, -0.5, 1.5, ALU.mult, ALU.add))
                ch.link(v.tensor_tensor(out, out, tmp, ALU.mult))

        def pipeline(eng, items, close, pieces, begin=None, close_first=False):

            def run(sb, nb, before):
                for q in range(4):
                    if q < nb and not close_first:
                        items(sb, q)
                    if q == 0 and before:
                        close(sb - 1, 3)
                    if q == 0 and begin:
                        begin(sb, nb)
                    if 0 < q < nb:
                        close(sb, q - 1)
                    if q < nb and close_first:
                        items(sb, q)
                    if before:
                        pieces(sb - 1, 4, q)

            run(0, 4, False)
            with eng.Fori(1, SB) as sb:
                run(sb, 4, True)
            run(SB, 1, True)
            close(SB, 0)
            for q in range(4):
                pieces(SB, 1, q)

        def halves(eng, body):
            with eng.Fori(0, SB // 2) as it:
                for par in range(2):
                    body(it * 2 + par, 4, par, it)
            body(SB, 1, 0, SB // 2)

        def delayed(body, then, eng):
            nothing = lambda: None
            body(0, 4, 0, 0, nothing)
            with eng.Fori(0, SB // 2 - 1) as it:
                body(it * 2 + 1, 4, 1, it, lambda: then(it * 2, 4, 0))
                body(it * 2 + 2, 4, 0, it + 1, lambda: then(it * 2 + 1, 4, 1))
            body(SB - 1, 4, 1, SB // 2 - 1, lambda: then(SB - 2, 4, 0))
            body(SB, 1, 0, SB // 2, lambda: then(SB - 1, 4, 1))
            then(SB, 1, 0)

        W = Scope(whole, "w")
        iota_row = W.sb("iota_row", [P, P], BF16)
        ident = W.sb("ident", [P, P])
        zeros = W.sb("zeros", [P, 512], BF16)
        dst_rel = W.sb("dst_rel", [P, TILES])
        src_idx = W.sb("src_idx", [P, TILES], I32)
        bounds = W.sb("bounds", [1, NB + 1], I32)
        chunks = W.sb("chunks", [1, 1], I32)
        degree = W.sb("degree", [P, NB])
        dinv = W.sb("dinv", [P, NB])
        slice_w = W.sb("slice_w", [P, KD, HID])
        slice_b = W.sb("slice_b", [P, HID])
        tok = W.sb("tok", [P, KH, D + 1])

        pick = [W.sb(f"pick{i}", [P, NB, NE]) for i in range(2)]
        share = [W.sb(f"share{i}", [P, NB]) for i in range(2)]

        with ExitStack() as stack:
            S = Scope(stack, "s0")
            dst_i = S.sb("dst_i", [DE, ER], I32)
            dst_b = S.sb("dst_b", [DE, ER], BF16)
            below = S.sb("below", [DE, ER], BF16)
            count = S.sb("count", [DE, NB + 1])
            ones = S.sb("ones", [P, P])
            diff_i = S.sb("diff_i", [P, P], I32)
            col_i = S.sb("col_i", [P, P], I32)
            tri = S.sb("tri", [NB, NB + 1])
            ends = S.sb("ends", [NB, 2])
            npairs = S.sb("npairs", [NB, 1])
            npairs_i = S.sb("npairs_i", [NB, 1], I32)
            span = S.sb("span", [NB, 2])
            part_i = S.sb("part_i", [NB, 1], I32)
            vals = S.sb("vals", [NB, 2])
            tile_i = S.sb("tile_i", [NB, TILES], I32)
            tile_f = S.sb("tile_f", [NB, TILES])
            inside = S.sb("inside", [NB, TILES])
            tpos_i = S.sb("tpos_i", [P, TC], I32)
            tpos = S.sb("tpos", [P, TC])
            start = S.sb("start", [P, TC])
            start_i = S.sb("start_i", [P, TC], I32)
            base = S.sb("base", [P, TC])
            srow = S.sb("srow", [P, TC, P], I32)
            drow = S.sb("drow", [P, TC, P], I32)
            srow_f = S.sb("srow_f", [P, TC, P])
            drow_f = S.sb("drow_f", [P, TC, P])
            pad0 = S.sb("pad0", [1, E_PAD - E], I32)
            pad1 = S.sb("pad1", [1, E_PAD - E], I32)
            chunk_i = S.sb("chunk_i", [1, 1], I32)
            wx = S.sb("wx", [P, KD, HID])
            wxT = S.sb("wxT", [P, KH, D])
            ws2 = S.sb("ws2", [P, G])
            wsbd = S.sb("wsbd", [P, KH, P])
            bx = S.sb("bx", [P, KH])
            bxr = S.sb("bxr", [P, KH, P])
            rtemp = S.sb("rtemp", [P, HEADS])
            bs = S.sb("bs", [P, G])
            xin = S.sb("xin", [P, 2, 4, D])
            stat = S.sb("stat", [P, 4, 6])
            mv = S.sb("mv", [P, 4, 2])
            var = S.sb("var", [P, 4])
            tmp4 = S.sb("tmp4", [P, 4])
            rstd = S.sb("rstd", [P, 4])
            xl = S.sb("xl", [P, 2, 4, D])
            res = S.sb("res", [P, 4, D])
            trow = S.sb("trow", [P, 2, 4, T1_W], BF16)

            psA = S.ps("psA")
            psB = S.ps("psB")
            psT = [S.ps(f"psT{i}") for i in range(2)]

            s_in = S.sem("inputs")
            s_wx = S.sem("slice_inputs")
            s_iota = S.sem("iotas")
            s_cst = S.sem("constants")
            s_pad = S.sem("padded_edges")
            s_padset = S.sem("pad_values")
            s_cnt = S.sem("counted")
            s_ends = S.sem("ends")
            s_np = S.sem("npairs")
            s_span = S.sem("span")
            s_ins = S.sem("inside")
            s_st = S.sem("starts_psum")
            s_sti = S.sem("starts")
            s_rows = S.sem("edge_rows")
            s_rowf = S.sem("edge_rows_float")
            s_tr = S.sem("edge_transposes")
            s_trc = S.sem("edge_transposes_copied")
            s_wt = S.sem("wx_transposed")
            s_wtc = S.sem("wx_transposes_copied")
            s_bd = S.sem("block_diagonal")
            s_sw = S.sem("slice_weights_psum")
            s_dve = S.sem("dve_chain")
            s_x = [S.sem(f"x_loaded{i}") for i in range(2)]
            s_xl = S.sem("normalised")
            s_hi = S.sem("high_parts")
            s_res = S.sem("residuals")
            s_mid = S.sem("middle_parts")
            s_lo = S.sem("low_parts")
            s_rows_st = [S.sem(f"rows_stored{i}") for i in range(2)]
            s_sto = [S.sem(f"tables_stored{i}") for i in range(2)]
            s_xt = S.sem("tail_cleared")
            s_xts = S.sem("tail_stored")

            block = stack.enter_context(nc.Block())

            def x_view(t, sb, nb, w):
                return t[bass.ds(sb * 4 * P, nb * P), :].rearrange("(q p) d -> p q d", p=P)

            @block.sync
            def _(sp):
                sp.dma_start(dst_i[:, :], a["dst"].rearrange("(p r) -> p r", p=DE)).then_inc(s_in, 16)
                sp.dma_start(src_pad[0:E, :].rearrange("(p r) a -> p (r a)", p=DE),
                             a["src"].rearrange("(p r) -> p r", p=DE)).then_inc(s_pad, 16)
                sp.dma_start(dst_pad[0:E, :].rearrange("(p r) a -> p (r a)", p=DE),
                             a["dst"].rearrange("(p r) -> p r", p=DE)).then_inc(s_pad, 16)
                sp.wait_ge(s_padset, 2)
                sp.dma_start(src_pad[E:E_PAD, :].rearrange("r a -> a r"), pad0[:, :]).then_inc(s_pad, 16)
                sp.dma_start(dst_pad[E:E_PAD, :].rearrange("r a -> a r"), pad1[:, :]).then_inc(s_pad, 16)
                with sp.Fori(0, SB // 2) as it:
                    for par in range(2):
                        sp.wait_ge(s_xl, it * 2 + par + 1)
                        sp.dma_start(xin[:, par], x_view(a["x"], it * 2 + par, 4, D)).then_inc(s_x[par], 16)
                sp.wait_ge(s_xt, 1)
                sp.dma_start(xin[0:TAIL, 0, 0], a["x"][SB * 4 * P:N, :]).then_inc(s_x[0], 16)
                sp.wait_ge(s_pad, 64)

            @block.gpsimd
            def _(pool):
                pool.iota(diff_i[:, :], [[1, P]], base=0, channel_multiplier=-1).then_inc(s_iota, 1)
                pool.iota(part_i[:, :], [[0, 1]], base=0, channel_multiplier=P).then_inc(s_iota, 1)
                pool.iota(tile_i[:, :], [[1, TILES]], base=0, channel_multiplier=0).then_inc(s_iota, 1)
                pool.iota(tpos_i[:, :], [[P * P, TC]], base=0, channel_multiplier=P).then_inc(s_iota, 1)
                pool.iota(col_i[:, :], [[1, P]], base=0, channel_multiplier=0).then_inc(s_iota, 1)
                pool.memset(pad0[:, :], 0).then_inc(s_padset, 1)
                pool.wait_ge(s_sti, 1)
                pool.wait_ge(s_pad, 64)
                for c in range(TC):
                    pool.indirect_dma_start(srow[:, c, :], None, src_pad,
                                            bass.IndirectOffsetOnAxis(ap=start_i[:, c:c + 1], axis=0)).then_inc(s_rows, 16)
                    pool.indirect_dma_start(drow[:, c, :], None, dst_pad,
                                            bass.IndirectOffsetOnAxis(ap=start_i[:, c:c + 1], axis=0)).then_inc(s_rows, 16)

                pool.sem_inc(s_lo, 2)

                def residuals(sb, nb, par, it):
                    hi, mid, lo = (trow[:, par, 0:nb, col:col + D] for col in (T1_HI, T1_MID, T1_LO))
                    pool.wait_ge(s_hi, sb + 1)
                    pool.wait_ge(s_lo, sb + 2)
                    nc.gpsimd.tensor_tensor(res[:, 0:nb, :], xl[:, par, 0:nb, :], hi, ALU.subtract).then_inc(s_res, 1)
                    pool.wait_ge(s_mid, sb + 1)
                    nc.gpsimd.tensor_tensor(lo, res[:, 0:nb, :], mid, ALU.subtract).then_inc(s_lo, 1)

                halves(pool, residuals)

            @block.vector
            def _(dve):
                ch = Chain(dve, s_dve)
                v = nc.vector
                v.memset(pad1[:, :], 1000000).then_inc(s_padset, 1)
                v.memset(zeros[:, :], 0.0)
                v.memset(ones[:, :], 1.0)
                v.memset(count[:, 0:1], 0.0)
                v.memset(count[:, NB:NB + 1], float(ER))
                v.memset(wsbd[:, :, :], 0.0)
                v.memset(trow[:, :, :, T1_HI + D:T1_W], 1.0)
                ch.link(v.memset(tok[:, :, :], 0.0))
                dve.wait_ge(s_iota, 5)
                v.tensor_copy(iota_row[:, :], col_i[:, :])
                v.tensor_scalar(ident[:, :], diff_i[:, :], 0.0, None, ALU.is_equal)
                v.tensor_scalar(tri[:, :], diff_i[0:NB, 0:NB + 1], 0.0, None, ALU.is_gt)
                v.tensor_copy(tile_f[:, :], tile_i[:, :])
                v.tensor_copy(tpos[:, :], tpos_i[:, :])
                ch.link(v.tensor_copy(vals[:, 1:2], part_i[:, :]))
                dve.wait_ge(s_in, 16)
                ch.link(v.tensor_scalar(dst_i[:, :], dst_i[:, :], 7, None, ALU.arith_shift_right))
                ch.link(v.tensor_copy(dst_b[:, :], dst_i[:, :]))
                for b in range(1, NB):
                    ch.link(v.tensor_scalar(below[:, :], dst_b[:, :], float(b), 0.0, ALU.is_lt, ALU.add,
                                            accum_out=count[:, b:b + 1]))
                v.memset(start_i[:, :], 0).then_inc(s_cnt, 1)
                dve.wait_ge(s_ends, 1)
                ch.link(v.tensor_copy(ends[:, :], psA[0:NB, 0:2]))
                ch.link(v.tensor_tensor(npairs[:, :], ends[:, 1:2], ends[:, 0:1], ALU.subtract))
                ch.link(v.tensor_scalar(npairs_i[:, :], npairs[:, :], float(PAIR - 1), None, ALU.add))
                ch.link(v.tensor_scalar(npairs_i[:, :], npairs_i[:, :], 8, None, ALU.arith_shift_right))
                v.tensor_scalar(npairs[:, :], npairs_i[:, :], 1.0, None, ALU.max).then_inc(s_np, 1)
                dve.wait_ge(s_span, 1)
                v.tensor_copy(bounds[:, :], psB[0:1, 0:NB + 1])
                v.tensor_scalar(chunk_i[:, :], psB[0:1, NB:NB + 1], float(RING - 1), None, ALU.add)
                ch.link(v.tensor_scalar(span[:, :], psB[0:NB, 64:66], 2.0, None, ALU.mult))
                v.tensor_scalar(chunks[:, :], chunk_i[:, :], 3, None, ALU.arith_shift_right)
                ch.link(v.scalar_tensor_tensor(vals[:, 0:1], span[:, 0:1], -float(P), ends[:, 0:1], ALU.mult, ALU.add))
                ch.link(v.tensor_scalar(inside[:, :], tile_f[:, :], span[:, 0:1], None, ALU.is_ge))
                v.scalar_tensor_tensor(inside[:, :], tile_f[:, :], span[:, 1:2], inside[:, :],
                                       ALU.is_lt, ALU.mult).then_inc(s_ins, 1)
                dve.wait_ge(s_st, 1)
                st = psA[:, 64:64 + 2 * TC].rearrange("p (c v) -> p c v", v=2)
                v.tensor_copy(base[:, :], st[:, :, 1])
                ch.link(v.tensor_tensor(start[:, :], st[:, :, 0], tpos[:, :], ALU.add))
                v.tensor_scalar(start_i[:, :], start[:, :], float(E_LAST), None, ALU.min).then_inc(s_sti, 1)
                dve.wait_ge(s_wx, 16 * 6)
                ch.link(v.tensor_scalar(rtemp[:, :], rtemp[:, :], 0.1, 5.0, ALU.max, ALU.min))
                ch.link(v.reciprocal(rtemp[:, :], rtemp[:, :]))
                for c in range(KH):
                    for k in range(2):
                        rows = slice(k * 64, k * 64 + 64)
                        v.tensor_scalar(wsbd[rows, c, rows], ws2[rows, :], rtemp[rows, 2 * c + k:2 * c + k + 1], None, ALU.mult)
                    v.tensor_scalar(bxr[:, c, :], ones[:, :], bx[:, c:c + 1], None, ALU.mult)
                for h in range(HEADS):
                    last = v.tensor_scalar(slice_b[:, h * G:(h + 1) * G], bs[:, :], rtemp[:, h:h + 1], None, ALU.mult)
                last.then_inc(s_bd, 1)
                dve.wait_ge(s_wt, 1)
                for k in range(KD):
                    last = v.tensor_copy(wxT[:, :, k * P:(k + 1) * P], psT[k][:, :].rearrange("p (c j) -> p c j", c=KH))
                last.then_inc(s_wtc, 1)
                dve.wait_ge(s_sw, 1)
                v.tensor_copy(slice_w[:, 0, :], psT[0][:, :])
                v.tensor_copy(slice_w[:, 1, :], psT[1][:, :])
                ch.link(v.tensor_tensor(slice_b[:, :], slice_b[:, :], psB[:, :], ALU.add))
                dve.wait_ge(s_rows, 16 * 2 * TC)
                v.tensor_copy(srow_f[:, :, :], srow[:, :, :])
                for c in range(TC):
                    last = v.tensor_scalar(drow_f[:, c, :], drow[:, c, :], base[:, c:c + 1], None, ALU.subtract)
                last.then_inc(s_rowf, 1)
                for k in range(TC // 2):
                    dve.wait_ge(s_tr, k + 1)
                    table = (src_idx, dst_rel)[k // 2]
                    v.tensor_copy(table[:, (k % 2) * 512:(k % 2) * 512 + 512], psT[k % 2][:, :]).then_inc(s_trc, 1)
                ch.restart()

                def norm(sb, nb, par, it):
                    if nb == 1:
                        v.memset(xin[:, 0, 0, :], 0.0).then_inc(s_xt, 1)
                    dve.wait_ge(s_x[par], (it + 1) * 16)
                    for q in range(nb):
                        last = v.bn_stats(stat[:, q, :], xin[:, par, q, :])
                    ch.link(last)
                    for q in range(nb):
                        last = v.bn_aggr(mv[:, q, :], stat[:, q, :])
                    ch.link(last)
                    ch.link(v.tensor_scalar(var[:, 0:nb], mv[:, 0:nb, 1], LN_EPS, None, ALU.add))
                    rsqrt(ch, rstd[:, 0:nb], var[:, 0:nb], tmp4[:, 0:nb])
                    dve.wait_ge(s_rows_st[par], it * 16 + 16)
                    dve.wait_ge(s_lo, sb + 1)
                    for q in range(nb):
                        last = v.tensor_scalar(xl[:, par, q, :], xin[:, par, q, :], mv[:, q, 0:1], rstd[:, q:q + 1],
                                               ALU.subtract, ALU.mult)
                    last.then_inc(s_xl, 1)
                    ch.restart()

                dve.sem_inc(s_xl, 2)
                halves(dve, norm)

            @block.scalar
            def _(act):
                ac = nc.scalar
                act.dma_start(wx[:, :, :], a["L0_ffn_W_x"].rearrange("(k p) n -> p k n", p=P)).then_inc(s_wx, 16)
                act.dma_start(ws2[0:64, :], a["L0_ffn_W_slice"]).then_inc(s_wx, 16)
                act.dma_start(ws2[64:128, :], a["L0_ffn_W_slice"]).then_inc(s_wx, 16)
                act.dma_start(bx[:, :], a["L0_ffn_b_x"].rearrange("(c p) -> p c", p=P), allow_slow_non_contiguous=True).then_inc(s_wx, 16)
                act.dma_start(rtemp[:, :], row_bc(a["L0_ffn_temperature"].rearrange("a h b c -> (a h b c)"), HEADS)).then_inc(s_wx, 16)
                act.dma_start(bs[:, :], row_bc(a["L0_ffn_b_slice"], G)).then_inc(s_wx, 16)
                act.sem_inc(s_rows_st[0], 16)
                act.sem_inc(s_rows_st[1], 16)
                act.sem_inc(s_sto[0], 16)
                act.sem_inc(s_sto[1], 16)

                def parts(sb, nb, par, it, later):
                    act.wait_ge(s_xl, sb + 3)
                    act.dma_start(x_view(xl_rows, sb, nb, D), xl[:, par, 0:nb, :]).then_inc(s_rows_st[par], 16)
                    act.wait_ge(s_sto[par], it * 16 + 16)
                    ac.activation(trow[:, par, 0:nb, T1_HI:T1_HI + D], xl[:, par, 0:nb, :], ACT.Copy).then_inc(s_hi, 1)
                    later()
                    act.wait_ge(s_res, sb + 1)
                    ac.activation(trow[:, par, 0:nb, T1_MID:T1_MID + D], res[:, 0:nb, :], ACT.Copy).then_inc(s_mid, 1)

                def store(sb, nb, par):
                    act.wait_ge(s_lo, sb + 3)
                    act.dma_start(x_view(table1, sb, nb, T1_W), trow[:, par, 0:nb, :]).then_inc(s_sto[par], 16)

                delayed(parts, store, act)
                act.dma_start(xtail, xin[:, 0, 0, :]).then_inc(s_xts, 16)
                act.wait_ge(s_xts, 16)
                act.wait_ge(s_rows_st[0], 16 * (SB // 2 + 2))
                act.wait_ge(s_rows_st[1], 16 * (SB // 2 + 1))
                act.wait_ge(s_sto[0], 16 * (SB // 2 + 2))
                act.wait_ge(s_sto[1], 16 * (SB // 2 + 1))

            @block.tensor
            def _(pe):
                pe.wait_ge(s_cnt, 1)
                nc.tensor.matmul(psA[0:NB, 0:1], count[:, 0:NB], ones[0:DE, 0:1], start=True, stop=True)
                nc.tensor.matmul(psA[0:NB, 1:2], count[:, 1:NB + 1], ones[0:DE, 0:1], start=True, stop=True).then_inc(s_ends, 1)
                pe.wait_ge(s_np, 1)
                nc.tensor.matmul(psB[0:1, 0:NB + 1], npairs[:, :], tri[:, :], start=True, stop=True)
                nc.tensor.matmul(psB[0:NB, 64:65], tri[:, 0:NB], npairs[:, :], start=True, stop=True)
                nc.tensor.matmul(psB[0:NB, 65:66], tri[:, 1:NB + 1], npairs[:, :], start=True, stop=True).then_inc(s_span, 1)
                pe.wait_ge(s_ins, 1)
                for c in range(TC):
                    last = nc.tensor.matmul(psA[:, 64 + 2 * c:66 + 2 * c], inside[:, c * P:(c + 1) * P], vals[:, :], start=True, stop=True)
                last.then_inc(s_st, 1)
                pe.wait_ge(s_wx, 16 * 6)
                for k in range(KD):
                    for c in range(KH):
                        last = nc.tensor.transpose(psT[k][:, c * P:(c + 1) * P], wx[:, k, c * P:(c + 1) * P], ident[:, :])
                last.then_inc(s_wt, 1)
                pe.wait_ge(s_bd, 1)
                pe.wait_ge(s_wtc, 1)
                for c in range(KH):
                    cols = slice(c * P, (c + 1) * P)
                    for k in range(KD):
                        nc.tensor.matmul(psT[k][:, cols], wxT[:, c, k * P:(k + 1) * P], wsbd[:, c, :], start=True, stop=True)
                    last = nc.tensor.matmul(psB[:, cols], bxr[:, c, :], wsbd[:, c, :], start=True, stop=True)
                last.then_inc(s_sw, 1)
                pe.wait_ge(s_rowf, 1)
                for k in range(TC // 2):
                    if k >= 2:
                        pe.wait_ge(s_trc, k - 1)
                    rows = (srow_f, drow_f)[k // 2]
                    for j in range(4):
                        last = nc.tensor.transpose(psT[k % 2][:, j * P:(j + 1) * P], rows[:, (k % 2) * 4 + j, :], ident[:, :])
                    last.then_inc(s_tr, 1)

        class Edges:
            AHEAD = 32

            def __init__(self, S, table, width, parts, bank_width):
                self.table, self.parts, self.bank_width = table, parts, bank_width
                self.rows = S.sb("edge_rows", [P, RING, 2, width], BF16)
                self.onehot = S.sb("onehot", [P, self.AHEAD, 2, P], BF16)
                self.idx = [S.sb(f"idx{h}", [P, SLOTS // 2], I32) for h in range(2)]
                self.s_idx = [S.sem(f"idx_loaded{h}") for h in range(2)]
                self.s_slot = [S.sem(f"slot_filled{j}") for j in range(SLOTS)]
                self.s_gathered = S.sem("pairs_gathered")
                self.s_onehot = S.sem("onehots_ready")
                self.s_used = S.sem("pairs_used")
                self.s_start = S.sem("pairs_started")
                self.s_agg = S.sem("block_summed")

            def gather(self, pool):
                n = pool.value_load(chunks[0:1, 0:1], min_val=1, max_val=TILES // SLOTS - 1)
                with pool.Fori(0, n) as c:
                    for h in range(2):
                        pool.wait_ge(self.s_idx[h], c * 16 + 16)
                        for j in range(SLOTS // 2):
                            slot = h * SLOTS // 2 + j
                            if j % 2 == 0:
                                pool.wait_ge(self.s_used, c * RING + (slot // 2 + 1 + self.AHEAD - RING))
                                pool.sem_inc(self.s_start, 1)
                            pool.indirect_dma_start(
                                self.rows[:, slot // 2, slot % 2, :], None, self.table,
                                bass.IndirectOffsetOnAxis(ap=self.idx[h][:, j:j + 1], axis=0)
                            ).then_inc(self.s_slot[slot], 16)

            def relay(self, sp):
                n = sp.value_load(chunks[0:1, 0:1], min_val=1, max_val=TILES // SLOTS - 1)
                half = SLOTS // 2
                for h in range(2):
                    sp.dma_start(self.idx[h][:, :], src_idx[:, h * half:(h + 1) * half]).then_inc(self.s_idx[h], 16)
                with sp.Fori(0, n) as c:
                    for h in range(2):
                        for pair in range(h * RING // 2, (h + 1) * RING // 2):
                            sp.wait_ge(self.s_slot[2 * pair], c * 16 + 16)
                            sp.wait_ge(self.s_slot[2 * pair + 1], c * 16 + 16)
                            sp.sem_inc(self.s_gathered, 1)
                        sp.dma_start(self.idx[h][:, :], src_idx[:, bass.ds(c * SLOTS + (SLOTS + h * half), half)]
                                     ).then_inc(self.s_idx[h], 16)
                for h in range(2):
                    sp.wait_ge(self.s_idx[h], n * 16 + 16)
                sp.sem_inc(self.s_gathered, 1)

            def range_of(self, eng, b):
                lo = eng.value_load(bounds[0:1, bass.ds(b, 1)], min_val=0, max_val=PAIRS_MAX)
                hi = eng.value_load(bounds[0:1, bass.ds(b + 1, 1)], min_val=1, max_val=PAIRS_MAX)
                return lo, hi

            def onehots(self, dve, b):
                lo, hi = self.range_of(dve, b)
                with dve.Fori(lo, hi) as i:
                    dve.wait_ge(self.s_used, i + 1)
                    r = dve.snap(i % self.AHEAD)
                    for t in range(2):
                        last = nc.vector.tensor_scalar(self.onehot[:, bass.ds(r, 1), t, :], iota_row[:, :],
                                                       dst_rel[:, bass.ds(i * 2 + t, 1)], None, ALU.is_equal)
                    last.then_inc(self.s_onehot, 1)

            def next_onehots(self, dve, sb, q):
                if not (isinstance(sb, int) and sb == SB):
                    self.onehots(dve, sb * 4 + (q + 1))

            def sums(self, pe, b, bank):
                w = self.bank_width
                nc.tensor.matmul(bank[:, 0:w], zeros[:, 0:P], zeros[:, 0:w], start=True, stop=False, skip_group_check=True)
                lo, hi = self.range_of(pe, b)
                with pe.Fori(lo, hi) as i:
                    pe.wait_ge(self.s_onehot, i + 1)
                    pe.wait_ge(self.s_gathered, i + 1)
                    rows = self.rows[:, bass.ds(i % RING, 1), :, :]
                    onehot = self.onehot[:, bass.ds(i % self.AHEAD, 1), :, :]
                    for t in range(2):
                        for col, n, to in self.parts:
                            last = nc.tensor.matmul(bank[:, to:to + n], onehot[:, 0, t, :], rows[:, 0, t, col:col + n],
                                                    start=False, stop=False, skip_group_check=True)
                    last.then_inc(self.s_used, 1)
                nc.tensor.matmul(bank[:, 0:w], zeros[:, 0:P], zeros[:, 0:w], start=False, stop=True,
                                 skip_group_check=True).then_inc(self.s_agg, 1)

        def rows_of(t, sb, nb):
            return t[bass.ds(sb * (4 * P), nb * P), :].rearrange("(q p) d -> p q d", p=P)

        with ExitStack() as stack:
            S = Scope(stack, "s1")
            edges = Edges(S, table1, T1_W, ((T1_MID, D, 0), (T1_LO, D, 0), (T1_HI, D + 1, 0)), D + 1)
            w1a = S.sb("w1a", [P, KD, HID])
            w1b = S.sb("w1b", [P, KH, HID])
            b1a = S.sb("b1a", [P, KH])
            b1b = S.sb("b1b", [P, HID])
            eps1 = S.sb("eps1", [P, 1])
            self_x = S.sb("self_x", [P, 4, D])
            agg = S.sb("agg", [P, 4, D])
            aggT = S.sb("aggT", [P, KD, 4 * P])
            h1T = S.sb("h1T", [P, KH, 4 * P])
            pre = S.sb("pre", [P, 4, HID])
            hid = S.sb("hid", [P, 4, HID])
            res = S.sb("res", [P, 4, HID])
            trow = S.sb("trow", [P, 4, T2_W], BF16)
            psA = [S.ps(f"psA{i}") for i in range(2)]
            psT = [S.ps(f"psT{i}") for i in range(2)]
            psM = [S.ps(f"psM{i}") for i in range(4)]

            s_w = S.sem("weights")
            s_eps = S.sem("one_plus_eps")
            s_self = S.sem("self_rows")
            s_evac = S.sem("sums_copied")
            s_tr = S.sem("sums_transposed")
            s_aggT = S.sem("transposes_copied")
            s_m1 = S.sem("first_product")
            s_h1T = S.sem("first_relu")
            s_m2 = S.sem("second_product")
            s_pre = S.sem("second_product_copied")
            s_hid = S.sem("hidden_rows")
            s_res = S.sem("residual")
            s_mid = S.sem("middle_part")
            s_lo = S.sem("low_part")
            s_sto = S.sem("rows_stored")
            block = stack.enter_context(nc.Block())

            @block.gpsimd
            def _(pool):
                edges.gather(pool)

            @block.sync
            def _(sp):
                edges.relay(sp)

            @block.scalar
            def _(act):
                ac = nc.scalar
                act.dma_start(w1a[:, :, :], a["L0_gnn_W1a"].rearrange("(k p) n -> p k n", p=P)).then_inc(s_w, 16)
                act.dma_start(w1b[:, :, :], a["L0_gnn_W1b"].rearrange("(k p) n -> p k n", p=P)).then_inc(s_w, 16)
                act.dma_start(b1a[:, :], a["L0_gnn_b1a"].rearrange("(m p) -> p m", p=P), allow_slow_non_contiguous=True).then_inc(s_w, 16)
                act.dma_start(b1b[:, :], row_bc(a["L0_gnn_b1b"], HID)).then_inc(s_w, 16)
                act.dma_start(eps1[:, :], row_bc(a["L0_gnn_eps1"], 1)).then_inc(s_w, 16)
                act.sem_inc(s_aggT, 2)
                act.sem_inc(s_sto, 32)
                act.wait_ge(s_w, 80)

                def begin(sb, nb):
                    act.wait_ge(s_evac, sb * 4 + 2)
                    act.dma_start(self_x[:, 0:nb, :], rows_of(xl_rows, sb, nb)).then_inc(s_self, 16)

                def close(sb, q):
                    act.wait_ge(s_tr, sb * 4 + (q + 1))
                    ac.activation(aggT[:, :, q * P:(q + 1) * P], psT[q % 2][:, 0:D].rearrange("p (k n) -> p k n", k=KD),
                                  ACT.Copy).then_inc(s_aggT, 1)

                def pieces(sb, nb, q):
                    if q == 0:
                        for m in range(KH):
                            act.wait_ge(s_m1, sb * 4 + (m + 1))
                            ac.activation(h1T[:, m, 0:nb * P], psM[m][:, 0:nb * P], ACT.Relu, bias=b1a[:, m:m + 1]).then_inc(s_h1T, 1)
                    if q == 3:
                        act.wait_ge(s_pre, sb * 4 + (4 + nb))
                        act.wait_ge(s_sto, sb * 32 + 32)
                        ac.activation(hid[:, 0:nb, :], pre[:, 0:nb, :], ACT.Relu).then_inc(s_hid, 1)
                        ac.activation(trow[:, 0:nb, 0:HID], pre[:, 0:nb, :], ACT.Relu).then_inc(s_hid, 1)
                        act.wait_ge(s_res, sb + 1)
                        ac.activation(trow[:, 0:nb, HID:2 * HID], res[:, 0:nb, :], ACT.Copy).then_inc(s_mid, 1)
                        act.wait_ge(s_lo, sb + 1)
                        act.dma_start(rows_of(h_rows, sb, nb), hid[:, 0:nb, :]).then_inc(s_sto, 16)
                        act.dma_start(rows_of(table2, sb, nb), trow[:, 0:nb, :]).then_inc(s_sto, 16)

                pipeline(act, lambda sb, q: None, close, pieces, begin)
                act.wait_ge(s_sto, 32 * (SB + 2))

            @block.vector
            def _(dve):
                v = nc.vector
                dve.sem_inc(s_evac, 2)
                dve.sem_inc(s_pre, 4)
                edges.onehots(dve, 0)
                dve.wait_ge(s_w, 80)
                v.tensor_scalar(eps1[:, :], eps1[:, :], 1.0, None, ALU.add).then_inc(s_eps, 1)
                dve.wait_ge(s_eps, 1)

                def close(sb, q):
                    bank = psA[q % 2]
                    dve.wait_ge(edges.s_agg, sb * 4 + (q + 1))
                    dve.wait_ge(s_self, sb * 16 + 16)
                    v.tensor_scalar(degree[:, bass.ds(sb * 4 + q, 1)], bank[:, D:D + 1], 1.0, None, ALU.add)
                    v.scalar_tensor_tensor(agg[:, q, :], self_x[:, q, :], eps1[:, 0:1], bank[:, 0:D],
                                           ALU.mult, ALU.add).then_inc(s_evac, 1)

                def pieces(sb, nb, q):
                    if q in (2, 3):
                        for j in (2 * q - 4, 2 * q - 3):
                            if j < nb:
                                dve.wait_ge(s_m2, sb * 4 + (j + 1))
                                v.tensor_tensor(pre[:, j, :], psM[j][:, :], b1b[:, :], ALU.add).then_inc(s_pre, 1)
                    if q == 3:
                        dve.wait_ge(s_hid, sb * 2 + 2)
                        v.tensor_tensor(res[:, 0:nb, :], hid[:, 0:nb, :], trow[:, 0:nb, 0:HID], ALU.subtract).then_inc(s_res, 1)
                        dve.wait_ge(s_mid, sb + 1)
                        v.tensor_tensor(trow[:, 0:nb, 2 * HID:3 * HID], res[:, 0:nb, :], trow[:, 0:nb, HID:2 * HID],
                                        ALU.subtract).then_inc(s_lo, 1)

                pipeline(dve, lambda sb, q: edges.next_onehots(dve, sb, q), close, pieces, close_first=True)

            @block.tensor
            def _(pe):
                mm = nc.tensor.matmul
                pe.sem_inc(edges.s_used, edges.AHEAD)
                pe.wait_ge(s_w, 80)

                def items(sb, q):
                    pe.wait_ge(s_evac, sb * 4 + (q + 1))
                    edges.sums(pe, sb * 4 + q, psA[q % 2])

                def close(sb, q):
                    pe.wait_ge(s_evac, sb * 4 + (q + 3))
                    pe.wait_ge(s_aggT, sb * 4 + (q + 1))
                    for k in range(KD):
                        last = nc.tensor.transpose(psT[q % 2][:, k * P:(k + 1) * P], agg[:, q, k * P:(k + 1) * P], ident[:, :])
                    last.then_inc(s_tr, 1)

                def pieces(sb, nb, q):
                    n = nb * P
                    if q == 0:
                        pe.wait_ge(s_aggT, sb * 4 + (nb + 2))
                        for m in range(KH):
                            pe.wait_ge(s_pre, sb * 4 + (m + 1))
                            for k in range(KD):
                                last = mm(psM[m][:, 0:n], w1a[:, k, m * P:(m + 1) * P], aggT[:, k, 0:n], start=k == 0, stop=k == KD - 1)
                            last.then_inc(s_m1, 1)
                    if q in (1, 2):
                        pe.wait_ge(s_h1T, sb * 4 + 4)
                        for j in (2 * q - 2, 2 * q - 1):
                            if j < nb:
                                for k in range(KH):
                                    last = mm(psM[j][:, :], h1T[:, k, j * P:(j + 1) * P], w1b[:, k, :], start=k == 0, stop=k == KH - 1)
                                last.then_inc(s_m2, 1)

                pipeline(pe, items, close, pieces)

        with ExitStack() as stack:
            S = Scope(stack, "s2")
            edges = Edges(S, table2, T2_W, [(part * HID, HID, 0) for part in range(3)], HID)
            w2a = S.sb("w2a", [P, KH, HID])
            w2b = S.sb("w2b", [P, KH, D])
            b2a = S.sb("b2a", [P, KH])
            b2b = S.sb("b2b", [P, D])
            eps2 = S.sb("eps2", [P, 1])
            self_h = S.sb("self_h", [P, 4, HID])
            agg = S.sb("agg", [P, 4, HID])
            aggT = S.sb("aggT", [P, KH, 4 * P])
            h3T = S.sb("h3T", [P, KH, 4 * P])
            xrow = S.sb("xrow", [P, 4, D])
            x1 = S.sb("x1", [P, 4, D])
            stat = S.sb("stat", [P, 4, 6])
            mv = S.sb("mv", [P, 4, 2])
            var = S.sb("var", [P, 4])
            tmp4 = S.sb("tmp4", [P, 4])
            rstd = S.sb("rstd", [P, 4])
            xl1 = S.sb("xl1", [P, 4, D + 1])
            xl1T = S.sb("xl1T", [P, KD, 4 * P])
            prob = S.sb("prob", [P, 4, HID])
            sw = S.sb("sw", [P, 4, HID])
            gmax = S.sb("gmax", [P, 4 * HEADS])
            gsum = S.sb("gsum", [P, 4 * HEADS])
            swT = S.sb("swT", [P, 4, HID])
            psA = [S.ps(f"psA{i}") for i in range(2)]
            psT = [S.ps(f"psT{i}") for i in range(2)]
            psM = [S.ps(f"psM{i}") for i in range(4)]

            s_w = S.sem("weights")
            s_dve = S.sem("dve_chain")
            s_self = S.sem("self_rows")
            s_x = S.sem("x_rows")
            s_evac = S.sem("sums_copied")
            s_tr = S.sem("sums_transposed")
            s_aggT = S.sem("transposes_copied")
            s_m1 = S.sem("first_product")
            s_h3T = S.sem("first_relu")
            s_m2 = S.sem("second_product")
            s_xl = S.sem("x1_normalised")
            s_t1 = S.sem("second_bank_transposed")
            s_t1c = S.sem("second_bank_copied")
            s_lg = S.sem("logits")
            s_sh = S.sem("logits_less_max")
            s_exp = S.sem("exponentials")
            s_sw = S.sem("slice_weights")
            s_tokp = S.sem("token_products")
            s_tok = S.sem("token_sums")
            s_x1s = S.sem("x1_stored")
            s_sws = S.sem("slice_weights_stored")
            block = stack.enter_context(nc.Block())

            @block.gpsimd
            def _(pool):
                edges.gather(pool)

            @block.sync
            def _(sp):
                edges.relay(sp)

            @block.scalar
            def _(act):
                ac = nc.scalar
                act.dma_start(w2a[:, :, :], a["L0_gnn_W2a"].rearrange("(k p) n -> p k n", p=P)).then_inc(s_w, 16)
                act.dma_start(w2b[:, :, :], a["L0_gnn_W2b"].rearrange("(k p) n -> p k n", p=P)).then_inc(s_w, 16)
                act.dma_start(b2a[:, :], a["L0_gnn_b2a"].rearrange("(m p) -> p m", p=P), allow_slow_non_contiguous=True).then_inc(s_w, 16)
                act.dma_start(b2b[:, :], row_bc(a["L0_gnn_b2b"], D)).then_inc(s_w, 16)
                act.dma_start(eps2[:, :], row_bc(a["L0_gnn_eps2"], 1)).then_inc(s_w, 16)
                act.sem_inc(s_aggT, 1)
                act.sem_inc(s_t1c, 1)
                act.sem_inc(s_x1s, 16)
                act.sem_inc(s_sws, 16)
                act.wait_ge(s_w, 80)

                def begin(sb, nb):
                    act.wait_ge(s_evac, sb * 4 + 2)
                    act.dma_start(self_h[:, 0:nb, :], rows_of(h_rows, sb, nb)).then_inc(s_self, 16)

                def close(sb, q):
                    act.wait_ge(s_tr, sb * 4 + (q + 1))
                    ac.activation(aggT[:, :, q * P:(q + 1) * P], psT[0][:, :].rearrange("p (k n) -> p k n", k=KH),
                                  ACT.Copy).then_inc(s_aggT, 1)

                def pieces(sb, nb, q):
                    if q == 0:
                        act.wait_ge(s_xl, sb * 4 + 4)
                        if nb == 4:
                            act.dma_start(xrow[:, :, :], rows_of(a["x"], sb, 4)).then_inc(s_x, 16)
                        else:
                            act.dma_start(xrow[:, 0, :], xtail).then_inc(s_x, 16)
                        for m in range(KH):
                            act.wait_ge(s_m1, sb * 4 + (m + 1))
                            ac.activation(h3T[:, m, 0:nb * P], psM[m][:, 0:nb * P], ACT.Relu, bias=b2a[:, m:m + 1]).then_inc(s_h3T, 1)
                    if q == 2:
                        act.wait_ge(s_xl, sb * 4 + (nb + 4))
                        act.dma_start(rows_of(x1_rows, sb, nb), x1[:, 0:nb, :]).then_inc(s_x1s, 16)
                        for j in range(nb):
                            act.wait_ge(s_t1, sb * 8 + (j + 1))
                            ac.activation(xl1T[:, :, j * P:(j + 1) * P], psT[1][:, 0:D].rearrange("p (k n) -> p k n", k=KD),
                                          ACT.Copy).then_inc(s_t1c, 1)
                        act.wait_ge(s_sh, sb + 1)
                        ac.activation(prob[:, 0:nb, :], prob[:, 0:nb, :], ACT.Exp).then_inc(s_exp, 1)
                    if q == 3:
                        act.wait_ge(s_sws, sb * 16 + 16)
                        for j in range(nb):
                            act.wait_ge(s_t1, sb * 8 + (nb + j + 1))
                            last = ac.activation(swT[:, j, :], psT[1][:, :], ACT.Copy)
                            last.then_inc(s_t1c, 1)
                        act.wait_ge(s_t1c, sb * 8 + (2 * nb + 1))
                        act.dma_start(swt_rows[bass.ds(sb * 4, nb), :, :].rearrange("q p d -> p q d"), swT[:, 0:nb, :]).then_inc(s_sws, 16)

                pipeline(act, lambda sb, q: None, close, pieces, begin)
                act.wait_ge(s_x1s, 16 * (SB + 2))
                act.wait_ge(s_sws, 16 * (SB + 2))

            @block.vector
            def _(dve):
                v = nc.vector
                ch = Chain(dve, s_dve)
                dve.sem_inc(s_evac, 2)
                dve.sem_inc(s_xl, 4)
                dve.sem_inc(s_tok, 4)
                edges.onehots(dve, 0)
                dve.wait_ge(s_w, 80)
                v.memset(xl1[:, :, D:D + 1], 1.0)
                ch.link(v.tensor_scalar(eps2[:, :], eps2[:, :], 1.0, None, ALU.add))
                ch.restart()

                def close(sb, q):
                    dve.wait_ge(edges.s_agg, sb * 4 + (q + 1))
                    dve.wait_ge(s_self, sb * 16 + 16)
                    v.scalar_tensor_tensor(agg[:, q, :], self_h[:, q, :], eps2[:, 0:1], psA[q % 2][:, :],
                                           ALU.mult, ALU.add).then_inc(s_evac, 1)

                def pieces(sb, nb, q):
                    groups = prob[:, 0:nb, :].rearrange("p q (h g) -> p (q h) g", g=G)
                    if q == 1:
                        dve.wait_ge(s_x, sb * 16 + 16)
                        dve.wait_ge(s_x1s, sb * 16 + 16)
                        for j in range(nb):
                            dve.wait_ge(s_m2, sb * 4 + (j + 1))
                            last = v.tensor_tensor(x1[:, j, :], psM[j][:, 0:D], b2b[:, :], ALU.add)
                        ch.link(last)
                        ch.link(v.tensor_tensor(x1[:, 0:nb, :], x1[:, 0:nb, :], xrow[:, 0:nb, :], ALU.add))
                        for j in range(nb):
                            last = v.bn_stats(stat[:, j, :], x1[:, j, :])
                        ch.link(last)
                        for j in range(nb):
                            last = v.bn_aggr(mv[:, j, :], stat[:, j, :])
                        ch.link(last)
                        ch.link(v.tensor_scalar(var[:, 0:nb], mv[:, 0:nb, 1], LN_EPS, None, ALU.add))
                        rsqrt(ch, rstd[:, 0:nb], var[:, 0:nb], tmp4[:, 0:nb])
                        for j in range(nb):
                            v.tensor_scalar(xl1[:, j, 0:D], x1[:, j, :], mv[:, j, 0:1], rstd[:, j:j + 1],
                                            ALU.subtract, ALU.mult).then_inc(s_xl, 1)
                        ch.restart()
                    if q == 2:
                        for j in range(nb):
                            dve.wait_ge(s_lg, sb * 4 + (j + 1))
                            last = v.tensor_tensor(prob[:, j, :], psM[j][:, :], slice_b[:, :], ALU.add)
                        ch.link(last)
                        ch.link(v.tensor_reduce(gmax[:, 0:nb * HEADS], groups, AX, ALU.max))
                        v.tensor_tensor(groups, groups, gmax[:, 0:nb * HEADS].unsqueeze(2).to_broadcast([P, nb * HEADS, G]),
                                        ALU.subtract).then_inc(s_sh, 1)
                        dve.wait_ge(s_exp, sb + 1)
                        ch.link(v.tensor_reduce(gsum[:, 0:nb * HEADS], groups, AX, ALU.add))
                        ch.link(v.reciprocal(gsum[:, 0:nb * HEADS], gsum[:, 0:nb * HEADS]))
                        v.tensor_tensor(sw[:, 0:nb, :].rearrange("p q (h g) -> p (q h) g", g=G), groups,
                                        gsum[:, 0:nb * HEADS].unsqueeze(2).to_broadcast([P, nb * HEADS, G]),
                                        ALU.mult).then_inc(s_sw, 1)
                        ch.restart()
                    if q == 3:
                        for c in range(KH):
                            dve.wait_ge(s_tokp, sb * 4 + (c + 1))
                            v.tensor_tensor(tok[:, c, :], tok[:, c, :], psM[c][:, 0:D + 1], ALU.add).then_inc(s_tok, 1)

                pipeline(dve, lambda sb, q: edges.next_onehots(dve, sb, q), close, pieces, close_first=True)

            @block.tensor
            def _(pe):
                mm = nc.tensor.matmul
                pe.sem_inc(edges.s_used, edges.AHEAD)
                pe.wait_ge(s_w, 80)

                def items(sb, q):
                    pe.wait_ge(s_evac, sb * 4 + (q + 1))
                    edges.sums(pe, sb * 4 + q, psA[q % 2])

                def close(sb, q):
                    pe.wait_ge(s_evac, sb * 4 + (q + 3))
                    pe.wait_ge(s_aggT, sb * 4 + (q + 1))
                    for k in range(KH):
                        last = nc.tensor.transpose(psT[0][:, k * P:(k + 1) * P], agg[:, q, k * P:(k + 1) * P], ident[:, :])
                    last.then_inc(s_tr, 1)

                def logits(sb, j):
                    pe.wait_ge(s_t1c, sb * 8 + (j + 2))
                    for k in range(KD):
                        last = mm(psM[j][:, :], xl1T[:, k, j * P:(j + 1) * P], slice_w[:, k, :], start=k == 0, stop=k == KD - 1)
                    last.then_inc(s_lg, 1)

                def pieces(sb, nb, q):
                    n = nb * P
                    if q == 0:
                        pe.wait_ge(s_aggT, sb * 4 + (nb + 1))
                        for m in range(KH):
                            pe.wait_ge(s_tok, sb * 4 + (m + 1))
                            for k in range(KH):
                                last = mm(psM[m][:, 0:n], w2a[:, k, m * P:(m + 1) * P], aggT[:, k, 0:n], start=k == 0, stop=k == KH - 1)
                            last.then_inc(s_m1, 1)
                    if q == 1:
                        pe.wait_ge(s_h3T, sb * 4 + 4)
                        for j in range(nb):
                            for k in range(KH):
                                last = mm(psM[j][:, 0:D], h3T[:, k, j * P:(j + 1) * P], w2b[:, k, :], start=k == 0, stop=k == KH - 1)
                            last.then_inc(s_m2, 1)
                    if q == 2:
                        for j in range(nb):
                            pe.wait_ge(s_xl, sb * 4 + (j + 5))
                            pe.wait_ge(s_t1c, sb * 8 + (j + 1))
                            for k in range(KD):
                                last = nc.tensor.transpose(psT[1][:, k * P:(k + 1) * P], xl1[:, j, k * P:(k + 1) * P], ident[:, :])
                            last.then_inc(s_t1, 1)
                            if j >= 1:
                                logits(sb, j - 1)
                        logits(sb, nb - 1)
                    if q == 3:
                        pe.wait_ge(s_sw, sb + 1)
                        for j in range(nb):
                            pe.wait_ge(s_t1c, sb * 8 + (nb + j + 1))
                            for c in range(KH):
                                last = nc.tensor.transpose(psT[1][:, c * P:(c + 1) * P], sw[:, j, c * P:(c + 1) * P], ident[:, :])
                            last.then_inc(s_t1, 1)
                            k = P if nb == 4 else TAIL
                            for c in range(KH):
                                last = mm(psM[c][:, 0:D + 1], sw[0:k, j, c * P:(c + 1) * P], xl1[0:k, j, :],
                                          start=j == 0, stop=j == nb - 1)
                                if j == nb - 1:
                                    last.then_inc(s_tokp, 1)

                pipeline(pe, items, close, pieces)

        with ExitStack() as stack:
            S = Scope(stack, "s3")
            wfx = S.sb("wfx", [P, KD, HID])
            bfx = S.sb("bfx", [P, HID])
            wqkv = S.sb("wqkv", [P, 3, HD])
            wbd = S.sb("wbd", [P, 3, P])
            wout = S.sb("wout", [P, KH, D])
            bout = S.sb("bout", [P, D])
            tokT = S.sb("tokT", [P, KD, HID])
            rnorm = S.sb("rnorm", [P, KH])
            stok = S.sb("stok", [P, KH, P])
            stokT = S.sb("stokT", [P, KH, P])
            qT = S.sb("qT", [P, KH, P])
            kT = S.sb("kT", [P, KH, P])
            val = S.sb("val", [P, KH, P])
            score = S.sb("score", [P, KH, HD])
            smax = S.sb("smax", [P, KH])
            ssum = S.sb("ssum", [P, KH])
            pbd = S.sb("pbd", [P, KH, P])
            pbdT = S.sb("pbdT", [P, KH, P])
            osT = S.sb("osT", [P, KH, P])
            mix = S.sb("mix", [P, KH, D])
            dtmp = S.sb("dtmp", [P, NB])
            swT = S.sb("swT", [P, 2, 4, HID])
            x1 = S.sb("x1", [P, 2, 4, D])
            x2 = S.sb("x2", [P, 2, 4, D])
            stat = S.sb("stat", [P, 4, 6])
            mv = S.sb("mv", [P, 4, 2])
            var = S.sb("var", [P, 4])
            tmp4 = S.sb("tmp4", [P, 4])
            rstd = S.sb("rstd", [P, 4])
            vrow = S.sb("vrow", [P, 2, 4, D])
            res = S.sb("res", [P, 4, D])
            trow = S.sb("trow", [P, 2, 4, T3_W], BF16)
            psM = [S.ps(f"psM{i}") for i in range(4)]
            psX = [S.ps(f"psX{i}") for i in range(3)]

            s_w = S.sem("weights")
            s_dve = S.sem("dve_chain")
            s_pe = S.sem("attention_products")
            s_at = S.sem("attention_operands")
            s_ex = S.sem("attention_exponentials")
            s_in = [S.sem(f"rows_loaded{i}") for i in range(2)]
            s_read = S.sem("loaded_rows_read")
            s_mm = S.sem("products")
            s_x2 = S.sem("x2_rows")
            s_v = S.sem("scaled_rows")
            s_hi = S.sem("high_part")
            s_res = S.sem("residual")
            s_mid = S.sem("middle_part")
            s_lo = S.sem("low_part")
            s_rows = [S.sem(f"rows_stored{i}") for i in range(2)]
            s_sto = [S.sem(f"table_stored{i}") for i in range(2)]
            block = stack.enter_context(nc.Block())

            @block.sync
            def _(sp):
                sp.dma_start(wfx[:, :, :], a["L0_ffn_W_fx"].rearrange("(k p) n -> p k n", p=P)).then_inc(s_w, 16)
                sp.dma_start(bfx[:, :], row_bc(a["L0_ffn_b_fx"], HID)).then_inc(s_w, 16)
                for i, name in enumerate(("L0_ffn_W_q", "L0_ffn_W_k", "L0_ffn_W_v")):
                    for h in range(2):
                        sp.dma_start(wqkv[h * HD:(h + 1) * HD, i, :], a[name]).then_inc(s_w, 16)
                sp.dma_start(wout[:, :, :], a["L0_ffn_W_out"].rearrange("(c p) n -> p c n", p=P)).then_inc(s_w, 16)
                sp.dma_start(bout[:, :], row_bc(a["L0_ffn_b_out"], D)).then_inc(s_w, 16)

                def load(sb, nb, par):
                    sp.wait_ge(s_read, sb + 1)
                    sp.dma_start(swT[:, par, 0:nb, :], swt_rows[bass.ds(sb * 4, nb), :, :].rearrange("q p d -> p q d")).then_inc(s_in[par], 16)
                    sp.dma_start(x1[:, par, 0:nb, :], rows_of(x1_rows, sb, nb)).then_inc(s_in[par], 16)

                with sp.Fori(0, SB // 2) as it:
                    for par in range(2):
                        load(it * 2 + par, 4, par)
                load(SB, 1, 0)
                sp.wait_ge(s_in[0], 32 * (SB // 2 + 1))
                sp.wait_ge(s_in[1], 32 * (SB // 2))

            @block.gpsimd
            def _(pool):
                pool.sem_inc(s_lo, 2)

                def residuals(sb, nb, par, it):
                    hi, mid, lo = (trow[:, par, 0:nb, i * D:(i + 1) * D] for i in range(3))
                    pool.wait_ge(s_hi, sb + 1)
                    pool.wait_ge(s_lo, sb + 2)
                    nc.gpsimd.tensor_tensor(res[:, 0:nb, :], vrow[:, par, 0:nb, :], hi, ALU.subtract).then_inc(s_res, 1)
                    pool.wait_ge(s_mid, sb + 1)
                    nc.gpsimd.tensor_tensor(lo, res[:, 0:nb, :], mid, ALU.subtract).then_inc(s_lo, 1)

                halves(pool, residuals)

            @block.vector
            def _(dve):
                v = nc.vector
                ch = Chain(dve, s_dve)
                dve.sem_inc(s_x2, 8)
                dve.sem_inc(s_read, 2)
                dve.sem_inc(s_v, 2)
                for t in (wbd, stok, pbd):
                    last = v.memset(t[:, :, :], 0.0)
                ch.link(last)
                dve.wait_ge(s_w, 16 * 10)
                for i in range(3):
                    for h in range(2):
                        rows = slice(h * HD, (h + 1) * HD)
                        last = v.tensor_copy(wbd[rows, i, rows], wqkv[rows, i, :])
                ch.link(v.tensor_scalar(rnorm[:, :], tok[:, :, D], 1e-5, None, ALU.add))
                ch.link(v.reciprocal(rnorm[:, :], rnorm[:, :]))
                for k in range(KD):
                    dve.wait_ge(s_pe, 1)
                    last = v.tensor_copy(tokT[:, k, :], psX[k][:, :])
                last.then_inc(s_at, 1)
                dve.wait_ge(s_pe, 2)
                for c in range(KH):
                    for h in range(2):
                        rows = slice(h * HD, (h + 1) * HD)
                        cols = slice(c * P + h * HD, c * P + (h + 1) * HD)
                        last = v.scalar_tensor_tensor(stok[rows, c, rows], bfx[rows, cols], tok[rows, c, D:D + 1], psX[2][rows, cols],
                                                      ALU.mult, ALU.add)
                ch.link(last)
                for c in range(KH):
                    last = v.tensor_scalar(stok[:, c, :], stok[:, c, :], rnorm[:, c:c + 1], None, ALU.mult)
                last.then_inc(s_at, 1)
                dve.wait_ge(s_pe, 3)
                v.tensor_copy(stokT[:, :, :], psX[0][:, :].rearrange("p (c j) -> p c j", c=KH)).then_inc(s_at, 1)
                dve.wait_ge(s_pe, 4)
                for t, ps in ((qT, psX[0]), (kT, psX[1]), (val, psX[2])):
                    last = v.tensor_copy(t[:, :, :], ps[:, :].rearrange("p (c j) -> p c j", c=KH))
                last.then_inc(s_at, 1)
                dve.wait_ge(s_pe, 5)
                for h in range(2):
                    rows = slice(h * HD, (h + 1) * HD)
                    last = v.tensor_scalar(score[rows, :, :], psX[0][rows, :].rearrange("p (c j) -> p c j", c=KH)[:, :, rows],
                                           float(HD) ** -0.5, None, ALU.mult)
                ch.link(last)
                ch.link(v.tensor_reduce(smax[:, :], score[:, :, :], AX, ALU.max))
                v.tensor_tensor(score[:, :, :], score[:, :, :], smax[:, :].unsqueeze(2).to_broadcast([P, KH, HD]),
                                ALU.subtract).then_inc(s_at, 1)
                dve.wait_ge(s_ex, 1)
                ch.link(v.tensor_reduce(ssum[:, :], score[:, :, :], AX, ALU.add))
                ch.link(v.reciprocal(ssum[:, :], ssum[:, :]))
                for h in range(2):
                    rows = slice(h * HD, (h + 1) * HD)
                    last = v.tensor_tensor(pbd[rows, :, rows], score[rows, :, :], ssum[rows, :].unsqueeze(2).to_broadcast([HD, KH, HD]), ALU.mult)
                last.then_inc(s_at, 1)
                dve.wait_ge(s_pe, 6)
                v.tensor_copy(pbdT[:, :, :], psX[1][:, :].rearrange("p (c j) -> p c j", c=KH)).then_inc(s_at, 1)
                dve.wait_ge(s_pe, 7)
                v.tensor_copy(osT[:, :, :], psX[0][:, :].rearrange("p (c j) -> p c j", c=KH)).then_inc(s_at, 1)
                dve.wait_ge(s_pe, 8)
                v.tensor_copy(mix[:, 0:2, :], psX[1][:, :].rearrange("p (c j) -> p c j", c=2))
                v.tensor_copy(mix[:, 2:4, :], psX[2][:, :].rearrange("p (c j) -> p c j", c=2)).then_inc(s_at, 1)
                rsqrt(ch, dinv[:, :], degree[:, :], dtmp[:, :])
                ch.restart()

                def norm(sb, nb, par, it):
                    dve.wait_ge(s_in[par], it * 32 + 32)
                    dve.wait_ge(s_rows[par], it * 32 + 32)
                    for j in range(nb):
                        dve.wait_ge(s_mm, sb * 4 + (j + 1))
                        last = v.tensor_tensor(x2[:, par, j, :], psM[j][:, 0:D], bout[:, :], ALU.add)
                        last.then_inc(s_x2, 1)
                    dve.wait_ge(s_x2, sb * 4 + (nb + 8))
                    ch.link(v.tensor_tensor(x2[:, par, 0:nb, :], x2[:, par, 0:nb, :], x1[:, par, 0:nb, :], ALU.add))
                    dve.sem_inc(s_read, 1)
                    for j in range(nb):
                        last = v.bn_stats(stat[:, j, :], x2[:, par, j, :])
                    ch.link(last)
                    for j in range(nb):
                        last = v.bn_aggr(mv[:, j, :], stat[:, j, :])
                    ch.link(last)
                    ch.link(v.tensor_scalar(var[:, 0:nb], mv[:, 0:nb, 1], LN_EPS, None, ALU.add))
                    rsqrt(ch, rstd[:, 0:nb], var[:, 0:nb], tmp4[:, 0:nb])
                    ch.link(v.tensor_tensor(rstd[:, 0:nb], rstd[:, 0:nb], dinv[:, bass.ds(sb * 4, nb)], ALU.mult))
                    dve.wait_ge(s_lo, sb + 1)
                    for j in range(nb):
                        last = v.tensor_scalar(vrow[:, par, j, :], x2[:, par, j, :], mv[:, j, 0:1], rstd[:, j:j + 1], ALU.subtract, ALU.mult)
                    last.then_inc(s_v, 1)
                    ch.restart()

                halves(dve, norm)

            @block.scalar
            def _(act):
                ac = nc.scalar
                act.sem_inc(s_rows[0], 32)
                act.sem_inc(s_rows[1], 32)
                act.sem_inc(s_sto[0], 16)
                act.sem_inc(s_sto[1], 16)
                act.wait_ge(s_at, 5)
                ac.activation(score[:, :, :], score[:, :, :], ACT.Exp).then_inc(s_ex, 1)

                def parts(sb, nb, par, it, later):
                    act.wait_ge(s_v, sb + 3)
                    act.dma_start(rows_of(x2_rows, sb, nb), x2[:, par, 0:nb, :]).then_inc(s_rows[par], 16)
                    act.dma_start(rows_of(v_rows, sb, nb), vrow[:, par, 0:nb, :]).then_inc(s_rows[par], 16)
                    act.wait_ge(s_sto[par], it * 16 + 16)
                    ac.activation(trow[:, par, 0:nb, 0:D], vrow[:, par, 0:nb, :], ACT.Copy).then_inc(s_hi, 1)
                    later()
                    act.wait_ge(s_res, sb + 1)
                    ac.activation(trow[:, par, 0:nb, D:2 * D], res[:, 0:nb, :], ACT.Copy).then_inc(s_mid, 1)

                def store(sb, nb, par):
                    act.wait_ge(s_lo, sb + 3)
                    act.dma_start(rows_of(table3, sb, nb), trow[:, par, 0:nb, :]).then_inc(s_sto[par], 16)

                delayed(parts, store, act)
                act.wait_ge(s_rows[0], 32 * (SB // 2 + 2))
                act.wait_ge(s_rows[1], 32 * (SB // 2 + 1))
                act.wait_ge(s_sto[0], 16 * (SB // 2 + 2))
                act.wait_ge(s_sto[1], 16 * (SB // 2 + 1))

            @block.tensor
            def _(pe):
                mm = nc.tensor.matmul
                pairs = [slice(c * P, (c + 1) * P) for c in range(KH)]
                for k in range(KD):
                    for c in range(KH):
                        last = nc.tensor.transpose(psX[k][:, pairs[c]], tok[:, c, k * P:(k + 1) * P], ident[:, :])
                last.then_inc(s_pe, 1)
                pe.wait_ge(s_at, 1)
                for c in range(KH):
                    for k in range(KD):
                        last = mm(psX[2][:, pairs[c]], tokT[:, k, pairs[c]], wfx[:, k, pairs[c]], start=k == 0, stop=k == KD - 1)
                last.then_inc(s_pe, 1)
                pe.wait_ge(s_at, 2)
                for c in range(KH):
                    last = nc.tensor.transpose(psX[0][:, pairs[c]], stok[:, c, :], ident[:, :])
                last.then_inc(s_pe, 1)
                pe.wait_ge(s_at, 3)
                for c in range(KH):
                    mm(psX[0][:, pairs[c]], wbd[:, 0, :], stokT[:, c, :], start=True, stop=True)
                    mm(psX[1][:, pairs[c]], wbd[:, 1, :], stokT[:, c, :], start=True, stop=True)
                    last = mm(psX[2][:, pairs[c]], stokT[:, c, :], wbd[:, 2, :], start=True, stop=True)
                last.then_inc(s_pe, 1)
                pe.wait_ge(s_at, 4)
                for c in range(KH):
                    last = mm(psX[0][:, pairs[c]], qT[:, c, :], kT[:, c, :], start=True, stop=True)
                last.then_inc(s_pe, 1)
                pe.wait_ge(s_at, 6)
                for c in range(KH):
                    last = nc.tensor.transpose(psX[1][:, pairs[c]], pbd[:, c, :], ident[:, :])
                last.then_inc(s_pe, 1)
                pe.wait_ge(s_at, 7)
                for c in range(KH):
                    last = mm(psX[0][:, pairs[c]], val[:, c, :], pbdT[:, c, :], start=True, stop=True)
                last.then_inc(s_pe, 1)
                pe.wait_ge(s_at, 8)
                for c in range(KH):
                    last = mm(psX[1 + c // 2][:, (c % 2) * D:(c % 2 + 1) * D], osT[:, c, :], wout[:, c, :], start=True, stop=True)
                last.then_inc(s_pe, 1)
                pe.wait_ge(s_at, 9)

                def body(sb, nb, par, it):
                    pe.wait_ge(s_in[par], it * 32 + 32)
                    for j in range(nb):
                        pe.wait_ge(s_x2, sb * 4 + (j + 5))
                        for c in range(KH):
                            last = mm(psM[j][:, 0:D], swT[:, par, j, pairs[c]], mix[:, c, :], start=c == 0, stop=c == KH - 1)
                        last.then_inc(s_mm, 1)

                with pe.Fori(0, SB // 2) as it:
                    for par in range(2):
                        body(it * 2 + par, 4, par, it)
                body(SB, 1, 0, SB // 2)

        with ExitStack() as stack:
            S = Scope(stack, "s4")
            edges = Edges(S, table3, T3_W, ((0, 2 * D, 0), (2 * D, D, D)), 2 * D)
            w = S.sb("w", [P, KD, D])
            bias = S.sb("bias", [P, D])
            bmean = S.sb("bmean", [P, D])
            bvar = S.sb("bvar", [P, D])
            gamma = S.sb("gamma", [P, D])
            beta = S.sb("beta", [P, D])
            factor = S.sb("factor", [P, D])
            wg = S.sb("wg", [P, KD, NE])
            bg = S.sb("bg", [P, NE])
            gbias = S.sb("gbias", [P, NE])
            erow = S.sb("erow", [P, 4, NE])
            self_v = S.sb("self_v", [P, 4, D])
            agg = S.sb("agg", [P, 4, D])
            aggT = S.sb("aggT", [P, KD, 4 * P])
            xrow = S.sb("xrow", [P, 4, D])
            acc = S.sb("acc", [P, 4, D])
            stat = S.sb("stat", [P, 4, 6])
            mv = S.sb("mv", [P, 4, 2])
            var = S.sb("var", [P, 4])
            tmp4 = S.sb("tmp4", [P, 4])
            rstd = S.sb("rstd", [P, 4])
            xl3 = S.sb("xl3", [P, 4, D])
            xl3T = S.sb("xl3T", [P, KD, 4 * P])
            gate = S.sb("gate", [P, 4, NE])
            equal = S.sb("equal", [P, 4, NE])
            top = [S.sb(f"top{i}", [P, 4]) for i in range(2)]
            first = S.sb("first", [P, 4])
            best = [S.sb(f"best{i}", [P, 4, NE]) for i in range(2)]
            part = [S.sb(f"part{i}", [P, 4]) for i in range(2)]
            ratio = S.sb("ratio", [P, 4])
            psA = [S.ps(f"psA{i}") for i in range(2)]
            psO = [S.ps(f"psO{i}") for i in range(2)]
            psT = [S.ps(f"psT{i}") for i in range(2)]

            s_wg = S.sem("graph_weights")
            s_we = S.sem("expert_weights")
            s_w = S.sem("scaled_weights")
            s_dve = S.sem("dve_chain")
            s_self = S.sem("self_rows")
            s_x = S.sem("x2_rows")
            s_evac = S.sem("sums_copied")
            s_tr = S.sem("sums_transposed")
            s_aggT = S.sem("transposes_copied")
            s_o = S.sem("graph_products")
            s_acc = S.sem("graph_products_used")
            s_xl = S.sem("x3_normalised")
            s_t1 = S.sem("second_bank_transposed")
            s_t1c = S.sem("second_bank_copied")
            s_gate = S.sem("gates")
            s_diff = S.sem("gate_differences")
            s_exp = S.sem("gate_exponentials")
            s_sto = S.sem("rows_stored")
            s_gread = S.sem("gates_read")
            block = stack.enter_context(nc.Block())

            @block.gpsimd
            def _(pool):
                edges.gather(pool)

            @block.sync
            def _(sp):
                edges.relay(sp)

            @block.scalar
            def _(act):
                ac = nc.scalar
                act.dma_start(w[:, :, :], a["L1_gnn_W"].rearrange("(k p) n -> p k n", p=P)).then_inc(s_wg, 16)
                for t, name in ((bias, "L1_gnn_b"), (bmean, "L1_gnn_running_mean"), (bvar, "L1_gnn_running_var"),
                                (gamma, "L1_gnn_gamma"), (beta, "L1_gnn_beta")):
                    act.dma_start(t[:, :], row_bc(a[name], D)).then_inc(s_wg, 16)
                act.dma_start(bg[:, :], row_bc(a["L1_ffn_bg"], NE)).then_inc(s_wg, 16)
                act.dma_start(gbias[:, :], row_bc(a["L1_ffn_bias"], NE)).then_inc(s_wg, 16)
                act.dma_start(wg[:, :, :], a["L1_ffn_Wg"].rearrange("(k p) n -> p k n", p=P)).then_inc(s_we, 16)
                act.sem_inc(s_aggT, 1)
                act.sem_inc(s_t1c, 1)
                act.sem_inc(s_sto, 32)

                def begin(sb, nb):
                    act.wait_ge(s_evac, sb * 4 + 2)
                    act.dma_start(self_v[:, 0:nb, :], rows_of(v_rows, sb, nb)).then_inc(s_self, 16)

                def close(sb, q):
                    act.wait_ge(s_tr, sb * 4 + (q + 1))
                    ac.activation(aggT[:, :, q * P:(q + 1) * P], psT[0][:, 0:D].rearrange("p (k n) -> p k n", k=KD),
                                  ACT.Copy).then_inc(s_aggT, 1)

                def pieces(sb, nb, q):
                    if q == 0:
                        act.wait_ge(s_xl, sb * 4 + 4)
                        act.dma_start(xrow[:, 0:nb, :], rows_of(x2_rows, sb, nb)).then_inc(s_x, 16)
                        act.wait_ge(s_o, sb * 4 + nb)
                    if q == 1:
                        act.wait_ge(s_xl, sb * 4 + (nb + 4))
                        act.dma_start(rows_of(x3_rows, sb, nb), acc[:, 0:nb, :]).then_inc(s_sto, 16)
                        act.dma_start(rows_of(xl3_rows, sb, nb), xl3[:, 0:nb, :]).then_inc(s_sto, 16)
                        for j in range(nb):
                            act.wait_ge(s_t1, sb * 4 + (j + 1))
                            ac.activation(xl3T[:, :, j * P:(j + 1) * P], psT[1][:, 0:D].rearrange("p (k n) -> p k n", k=KD),
                                          ACT.Copy).then_inc(s_t1c, 1)
                        act.wait_ge(s_diff, sb + 1)
                        ac.activation(ratio[:, 0:nb], ratio[:, 0:nb], ACT.Exp).then_inc(s_exp, 1)

                pipeline(act, lambda sb, q: None, close, pieces, begin)
                act.wait_ge(s_sto, 32 * (SB + 2))

            @block.vector
            def _(dve):
                v = nc.vector
                ch = Chain(dve, s_dve)
                dve.sem_inc(s_evac, 2)
                dve.sem_inc(s_acc, 2)
                dve.sem_inc(s_xl, 4)
                dve.sem_inc(s_gread, 1)
                edges.onehots(dve, 0)
                dve.wait_ge(s_wg, 16 * 8)
                for e in range(NE):
                    last = v.memset(erow[:, :, e:e + 1], float(e - NE))
                ch.link(v.tensor_scalar(bvar[:, :], bvar[:, :], LN_EPS, None, ALU.add))
                rsqrt(ch, factor[:, :], bvar[:, :], xrow[:, 0, :])
                v.tensor_tensor(gbias[:, :], gbias[:, :], bg[:, :], ALU.add)
                v.tensor_tensor(bias[:, :], bias[:, :], bmean[:, :], ALU.subtract)
                ch.link(v.tensor_tensor(factor[:, :], factor[:, :], gamma[:, :], ALU.mult))
                ch.link(v.tensor_tensor(bias[:, :], bias[:, :], factor[:, :], ALU.mult))
                v.tensor_tensor(bias[:, :], bias[:, :], beta[:, :], ALU.add)
                for k in range(KD):
                    last = v.tensor_tensor(w[:, k, :], w[:, k, :], factor[:, :], ALU.mult)
                ch.link(last)
                ch.restart()
                dve.sem_inc(s_w, 1)

                def close(sb, q):
                    dve.wait_ge(edges.s_agg, sb * 4 + (q + 1))
                    dve.wait_ge(s_self, sb * 16 + 16)
                    ch.link(v.tensor_tensor(agg[:, q, :], self_v[:, q, :], psA[q % 2][:, D:2 * D], ALU.add))
                    v.tensor_tensor(agg[:, q, :], agg[:, q, :], psA[q % 2][:, 0:D], ALU.add).then_inc(s_evac, 1)
                    ch.restart()

                def largest(nb, i):
                    ch.link(v.tensor_reduce(top[i][:, 0:nb], gate[:, 0:nb, :], AX, ALU.max))
                    ch.link(v.tensor_tensor(equal[:, 0:nb, :], gate[:, 0:nb, :],
                                            top[i][:, 0:nb].unsqueeze(2).to_broadcast([P, nb, NE]), ALU.is_equal))
                    ch.link(v.tensor_tensor(equal[:, 0:nb, :], equal[:, 0:nb, :], erow[:, 0:nb, :], ALU.mult))
                    ch.link(v.tensor_reduce(first[:, 0:nb], equal[:, 0:nb, :], AX, ALU.min))
                    ch.link(v.tensor_tensor(best[i][:, 0:nb, :], erow[:, 0:nb, :],
                                            first[:, 0:nb].unsqueeze(2).to_broadcast([P, nb, NE]), ALU.is_equal))

                def pieces(sb, nb, q):
                    if q == 0:
                        dve.wait_ge(s_sto, sb * 32 + 32)
                        dve.wait_ge(s_x, sb * 16 + 16)
                        for j in range(nb):
                            dve.wait_ge(s_o, sb * 4 + (j + 1))
                            v.scalar_tensor_tensor(acc[:, j, :], psO[j % 2][:, 0:D], dinv[:, bass.ds(sb * 4 + j, 1)], bias[:, :],
                                                   ALU.mult, ALU.add).then_inc(s_acc, 1)
                        dve.wait_ge(s_acc, sb * 4 + (nb + 2))
                        ch.link(v.scalar_tensor_tensor(acc[:, 0:nb, :], acc[:, 0:nb, :], 0.0, xrow[:, 0:nb, :], ALU.max, ALU.add))
                        for j in range(nb):
                            last = v.bn_stats(stat[:, j, :], acc[:, j, :])
                        ch.link(last)
                        for j in range(nb):
                            last = v.bn_aggr(mv[:, j, :], stat[:, j, :])
                        ch.link(last)
                        ch.link(v.tensor_scalar(var[:, 0:nb], mv[:, 0:nb, 1], LN_EPS, None, ALU.add))
                        rsqrt(ch, rstd[:, 0:nb], var[:, 0:nb], tmp4[:, 0:nb])
                        for j in range(nb):
                            v.tensor_scalar(xl3[:, j, :], acc[:, j, :], mv[:, j, 0:1], rstd[:, j:j + 1],
                                            ALU.subtract, ALU.mult).then_inc(s_xl, 1)
                        ch.restart()
                    if q == 1:
                        dve.wait_ge(s_gate, sb * 4 + nb)
                        for j in range(nb):
                            last = v.tensor_tensor(gate[:, j, :], psT[1][:, D + j * NE:D + (j + 1) * NE], gbias[:, :], ALU.add)
                        ch.link(last)
                        dve.sem_inc(s_gread, 1)
                        largest(nb, 0)
                        ch.link(v.scalar_tensor_tensor(gate[:, 0:nb, :], best[0][:, 0:nb, :], -3e38, gate[:, 0:nb, :], ALU.mult, ALU.add))
                        largest(nb, 1)
                        v.tensor_tensor(ratio[:, 0:nb], top[1][:, 0:nb], top[0][:, 0:nb], ALU.subtract).then_inc(s_diff, 1)
                        dve.wait_ge(s_exp, sb + 1)
                        ch.link(v.tensor_scalar(part[0][:, 0:nb], ratio[:, 0:nb], 1.0, None, ALU.add))
                        ch.link(v.reciprocal(part[0][:, 0:nb], part[0][:, 0:nb]))
                        ch.link(v.tensor_tensor(part[1][:, 0:nb], ratio[:, 0:nb], part[0][:, 0:nb], ALU.mult))
                        for i in range(2):
                            v.tensor_copy(pick[i][:, bass.ds(sb * 4, nb), :], best[i][:, 0:nb, :])
                            last = v.tensor_copy(share[i][:, bass.ds(sb * 4, nb)], part[i][:, 0:nb])
                        ch.link(last)
                        ch.restart()

                pipeline(dve, lambda sb, q: edges.next_onehots(dve, sb, q), close, pieces, close_first=True)

            @block.tensor
            def _(pe):
                mm = nc.tensor.matmul
                pe.sem_inc(edges.s_used, edges.AHEAD)

                def items(sb, q):
                    pe.wait_ge(s_evac, sb * 4 + (q + 1))
                    edges.sums(pe, sb * 4 + q, psA[q % 2])

                def close(sb, q):
                    pe.wait_ge(s_evac, sb * 4 + (q + 3))
                    pe.wait_ge(s_aggT, sb * 4 + (q + 1))
                    for k in range(KD):
                        last = nc.tensor.transpose(psT[0][:, k * P:(k + 1) * P], agg[:, q, k * P:(k + 1) * P], ident[:, :])
                    last.then_inc(s_tr, 1)

                def gates(sb, j):
                    for k in range(KD):
                        last = mm(psT[1][:, D + j * NE:D + (j + 1) * NE], xl3T[:, k, j * P:(j + 1) * P], wg[:, k, :],
                                  start=k == 0, stop=k == KD - 1)
                    last.then_inc(s_gate, 1)

                def pieces(sb, nb, q):
                    if q == 0:
                        pe.wait_ge(s_w, 1)
                        pe.wait_ge(s_we, 16)
                        pe.wait_ge(s_aggT, sb * 4 + (nb + 1))
                        for j in range(nb):
                            pe.wait_ge(s_acc, sb * 4 + (j + 1))
                            for k in range(KD):
                                last = mm(psO[j % 2][:, 0:D], aggT[:, k, j * P:(j + 1) * P], w[:, k, :], start=k == 0, stop=k == KD - 1)
                            last.then_inc(s_o, 1)
                    if q == 1:
                        pe.wait_ge(s_gread, sb + 1)
                        for j in range(nb):
                            pe.wait_ge(s_xl, sb * 4 + (j + 5))
                            pe.wait_ge(s_t1c, sb * 4 + (j + 1))
                            for k in range(KD):
                                last = nc.tensor.transpose(psT[1][:, k * P:(k + 1) * P], xl3[:, j, k * P:(k + 1) * P], ident[:, :])
                            last.then_inc(s_t1, 1)
                        pe.wait_ge(s_t1c, sb * 4 + (nb + 1))
                        for j in range(nb):
                            gates(sb, j)

                pipeline(pe, items, close, pieces)

        with ExitStack() as stack:
            S = Scope(stack, "s5")
            w1 = S.sb("w1", [P, NE, KD, HID])
            w2 = S.sb("w2", [P, NE, KH, D])
            b1 = S.sb("b1", [P, NE * HID])
            b2 = S.sb("b2", [P, NE * D])
            diff_i = S.sb("diff_i", [P, P], I32)
            tri = S.sb("tri", [P, P])
            ones = S.sb("ones", [P, P])
            tile_i = S.sb("tile_i", [1, TM], I32)
            tile_f = S.sb("tile_f", [1, TM])
            node_i = S.sb("node_i", [P, NB], I32)
            zrow = S.sb("zrow", [TM, P], I32)
            both = S.sb("both", [P, NB, NE])
            total = [S.sb(f"total{i}", [P, NB, NE]) for i in range(2)]
            pos = S.sb("pos", [P, NB, NE])
            chosen = S.sb("chosen", [P, NB, NE])
            ntile_i = S.sb("ntile_i", [P, NE], I32)
            ntile = S.sb("ntile", [P, NE])
            tend = S.sb("tend", [P, NE])
            tbase = S.sb("tbase", [P, NE])
            slot_f = S.sb("slot_f", [P, NB, 2])
            slot = S.sb("slot", [P, NB * 2], I32)
            slot_by = [S.sb(f"slot_by{i}", [P, NB], I32) for i in range(2)]
            after = S.sb("after", [1, TM, NE])
            expert_f = S.sb("expert_f", [1, TM])
            expert = S.sb("expert", [1, TM], I32)
            sidx = [S.sb(f"sidx{i}", [P, SCAT], I32) for i in range(2)]
            snode = [S.sb(f"snode{i}", [P, SCAT], I32) for i in range(2)]
            trow_i = S.sb("trow_i", [TM, P], I32)
            trow_f = S.sb("trow_f", [TM, P])
            tnode = S.sb("tnode", [P, TM], I32)
            tidx = S.sb("tidx", [P, 4], I32)
            xs = S.sb("xs", [P, 4, D])
            xT = S.sb("xT", [P, 2, KD, P])
            hrow = S.sb("hrow", [P, 2, HID])
            hT = S.sb("hT", [P, 2, KH, P])
            y = S.sb("y", [P, 4, D])
            cidx = [S.sb(f"cidx{i}", [P, 8], I32) for i in range(2)]
            yg = S.sb("yg", [P, 2, 8, D])
            x3 = S.sb("x3", [P, 2, 4, D])
            psX = [S.ps(f"psX{i}") for i in range(2)]
            psU = [S.ps(f"psU{i}") for i in range(2)]
            psH = [S.ps(f"psH{i}") for i in range(2)]
            psD = [S.ps(f"psD{i}") for i in range(2)]

            s_w = S.sem("weights")
            s_dve = S.sem("dve_chain")
            s_iota = S.sem("iotas")
            s_zero = S.sem("slots_zeroed")
            s_both = S.sem("choices")
            s_cnt = S.sem("choices_counted")
            s_slot = S.sem("slots")
            s_si = [S.sem(f"scatter_indices{i}") for i in range(2)]
            s_sc = [S.sem(f"scattered{i}") for i in range(2)]
            s_go = S.sem("rounds_begun")
            s_sgo = S.sem("loads_and_stores_begun")
            s_tok = S.sem("slot_nodes_loaded")
            s_tf = S.sem("slot_nodes_float")
            s_tp = S.sem("slot_nodes_transposed")
            s_tn = S.sem("slot_nodes")
            s_ti = S.sem("tile_indices")
            s_xs = [S.sem(f"rows_gathered{j}") for j in range(4)]
            s_T = S.sem("rows_transposed")
            s_xT = S.sem("transposes_copied")
            s_up = S.sem("up_products")
            s_hr = S.sem("hidden_rows")
            s_H = S.sem("hidden_rows_transposed")
            s_h = S.sem("hidden")
            s_dn = S.sem("down_products")
            s_y = S.sem("expert_outputs")
            s_ys = [S.sem(f"outputs_stored{j}") for j in range(4)]
            s_ci = [S.sem(f"combine_indices{i}") for i in range(2)]
            s_yg = [S.sem(f"outputs_gathered{i}") for i in range(2)]
            s_x3 = [S.sem(f"x3_loaded{i}") for i in range(2)]
            s_done = S.sem("combined")
            s_out = [S.sem(f"out_stored{i}") for i in range(2)]
            block = stack.enter_context(nc.Block())
            slot_table = slot_node.rearrange("(t p) a -> t (p a)", p=P)

            def rounds(eng, body):
                with eng.Fori(0, TM // 4 - 1) as c:
                    for j in range(4):
                        body(c, j, False)
                for j in range(4):
                    body(TM // 4 - 1, j, True)

            def expert_of(eng, t):
                return eng.value_load(expert[0:1, bass.ds(t, 1)], min_val=0, max_val=NE - 1)

            @block.gpsimd
            def _(pool):
                pool.iota(diff_i[:, :], [[1, P]], base=0, channel_multiplier=-1).then_inc(s_iota, 1)
                pool.iota(tile_i[:, :], [[1, TM]], base=0, channel_multiplier=0).then_inc(s_iota, 1)
                pool.iota(node_i[:, :], [[P, NB]], base=0, channel_multiplier=1).then_inc(s_iota, 1)
                pool.memset(zrow[:, :], 0).then_inc(s_iota, 1)
                with pool.Fori(0, NB // SCAT) as r:
                    for i in range(2):
                        pool.wait_ge(s_si[i], r * 32 + 32)
                        pool.sem_inc(s_go, 1)
                        for j in range(SCAT):
                            pool.indirect_dma_start(slot_node, bass.IndirectOffsetOnAxis(ap=sidx[i][:, j:j + 1], axis=0),
                                                    snode[i][:, j:j + 1], None).then_inc(s_sc[i], 16)
                pool.wait_ge(s_tn, 1)
                with pool.Fori(0, TM // 4) as c:
                    pool.dma_start(tidx[:, :], tnode[:, bass.ds(c * 4, 4)]).then_inc(s_ti, 16)
                    pool.wait_ge(s_ti, c * 16 + 16)
                    for j in range(4):
                        pool.wait_ge(s_T, c * 4 + (j + 1))
                        pool.sem_inc(s_go, 1)
                        pool.indirect_dma_start(xs[:, j, :], None, xl3_rows,
                                                bass.IndirectOffsetOnAxis(ap=tidx[:, j:j + 1], axis=0)).then_inc(s_xs[j], 16)
                    for j in range(4):
                        pool.wait_ge(s_xs[j], c * 16 + 16)
                for j in range(4):
                    pool.wait_ge(s_ys[j], 16 * (TM // 4 + 1))

                def gather(sb, nb, par, it):
                    pool.wait_ge(s_done, sb + 1)
                    pool.wait_ge(s_ci[par], it * 16 + 16)
                    pool.sem_inc(s_go, 1)
                    for j in range(2 * nb):
                        pool.indirect_dma_start(yg[:, par, j, :], None, y_slots,
                                                bass.IndirectOffsetOnAxis(ap=cidx[par][:, j:j + 1], axis=0)).then_inc(s_yg[par], 16)

                halves(pool, gather)

            @block.sync
            def _(sp):
                sp.wait_ge(s_iota, 4)
                sp.dma_start(slot_table, zrow[:, :]).then_inc(s_zero, 16)
                sp.wait_ge(s_zero, 16)
                sp.wait_ge(s_slot, 1)

                def load(i, r):
                    sp.dma_start(sidx[i][:, :], slot_by[i][:, bass.ds(r * SCAT, SCAT)]).then_inc(s_si[i], 16)
                    sp.dma_start(snode[i][:, :], node_i[:, bass.ds(r * SCAT, SCAT)]).then_inc(s_si[i], 16)

                for i in range(2):
                    load(i, 0)
                with sp.Fori(0, NB // SCAT - 1) as r:
                    for i in range(2):
                        sp.wait_ge(s_sc[i], r * (16 * SCAT) + 16 * SCAT)
                        sp.sem_inc(s_sgo, 1)
                        load(i, r + 1)
                for i in range(2):
                    sp.wait_ge(s_sc[i], 16 * NB)
                sp.dma_start(trow_i[:, :], slot_table).then_inc(s_tok, 16)

                def store(c, j, last):
                    sp.wait_ge(s_y, c * 4 + (j + 3))
                    sp.sem_inc(s_sgo, 1)
                    sp.dma_start(y_slots[bass.ds(c * (4 * P) + j * P, P), :], y[:, j, :]).then_inc(s_ys[j], 16)

                rounds(sp, store)

                def loads(sb, nb, par, it):
                    sp.wait_ge(s_done, sb + 1)
                    sp.sem_inc(s_sgo, 1)
                    sp.dma_start(cidx[par][:, 0:2 * nb], slot[:, bass.ds(sb * 8, 2 * nb)]).then_inc(s_ci[par], 16)
                    sp.wait_ge(s_out[par], it * 16 + 16)
                    sp.sem_inc(s_sgo, 1)
                    sp.dma_start(x3[:, par, 0:nb, :], rows_of(x3_rows, sb, nb)).then_inc(s_x3[par], 16)

                halves(sp, loads)

            @block.scalar
            def _(act):
                ac = nc.scalar
                act.dma_start(w1[:, :, :, :], a["L1_ffn_W1"].rearrange("e (k p) n -> p e k n", p=P)).then_inc(s_w, 16)
                act.dma_start(w2[:, :, :, :], a["L1_ffn_W2"].rearrange("e (k p) n -> p e k n", p=P)).then_inc(s_w, 16)
                act.dma_start(b1[:, :], row_bc(a["L1_ffn_b1"].rearrange("e n -> (e n)"), NE * HID)).then_inc(s_w, 16)
                act.dma_start(b2[:, :], row_bc(a["L1_ffn_b2"].rearrange("e n -> (e n)"), NE * D)).then_inc(s_w, 16)
                act.sem_inc(s_xT, 2)
                act.sem_inc(s_h, 2)
                for i in range(2):
                    act.sem_inc(s_out[i], 16)

                def copy(c, j):
                    act.wait_ge(s_T, c * 4 + (j + 5))
                    act.wait_ge(s_up, c * 4 + (j + 1))
                    ac.activation(xT[:, j % 2, :, :], psX[j % 2][:, 0:D].rearrange("p (k n) -> p k n", k=KD),
                                  ACT.Copy).then_inc(s_xT, 1)

                def relu(c, j):
                    act.wait_ge(s_H, c * 4 + (j + 3))
                    act.wait_ge(s_dn, c * 4 + (j + 1))
                    ac.activation(hT[:, j % 2, :, :], psH[j % 2][:, :].rearrange("p (m n) -> p m n", m=KH), ACT.Relu).then_inc(s_h, 1)

                for j in range(3):
                    copy(0, j)
                relu(0, 0)

                def step(c, j, last):
                    if not last or j + 3 < 4:
                        copy(c + (j + 3) // 4, (j + 3) % 4)
                    if not last or j + 1 < 4:
                        relu(c + (j + 1) // 4, (j + 1) % 4)

                rounds(act, step)

                def store(sb, nb, par, it):
                    act.wait_ge(s_done, sb + 3)
                    if nb == 4:
                        act.dma_start(rows_of(out, sb, 4), x3[:, par, :, :]).then_inc(s_out[par], 16)
                    else:
                        act.dma_start(out[N - TAIL:N, :], x3[0:TAIL, par, 0, :]).then_inc(s_out[par], 16)

                halves(act, store)
                act.wait_ge(s_out[0], 16 * (SB // 2 + 2))
                act.wait_ge(s_out[1], 16 * (SB // 2 + 1))

            @block.vector
            def _(dve):
                v = nc.vector
                ch = Chain(dve, s_dve)
                dve.sem_inc(s_y, 2)
                dve.sem_inc(s_hr, 2)
                dve.sem_inc(s_done, 2)
                for j in range(4):
                    dve.sem_inc(s_ys[j], 16)
                v.tensor_tensor(both[:, :, :], pick[0][:, :, :], pick[1][:, :, :], ALU.add)
                v.memset(ones[:, :], 1.0)
                dve.wait_ge(s_iota, 4)
                v.tensor_copy(tile_f[:, :], tile_i[:, :])
                v.tensor_scalar(tri[:, :], diff_i[:, :], 0.0, None, ALU.is_gt).then_inc(s_both, 1)
                dve.wait_ge(s_cnt, 1)
                counts = psX[1][:, 0:NB * NE].rearrange("p (b e) -> p b e", e=NE)
                ch.link(v.tensor_copy(total[0][:, :, :], counts))
                src, dst, step = total[0], total[1], 1
                while step < NB:
                    v.tensor_copy(dst[:, 0:step, :], src[:, 0:step, :])
                    ch.link(v.tensor_tensor(dst[:, step:NB, :], src[:, step:NB, :], src[:, 0:NB - step, :], ALU.add))
                    src, dst, step = dst, src, 2 * step
                ch.link(v.tensor_scalar(ntile_i[:, :], src[:, NB - 1, :], float(P - 1), None, ALU.add))
                ch.link(v.tensor_scalar(ntile_i[:, :], ntile_i[:, :], 7, None, ALU.arith_shift_right))
                v.tensor_copy(tend[:, :], ntile_i[:, :])
                ch.link(v.tensor_copy(ntile[:, :], ntile_i[:, :]))
                for e in range(1, NE):
                    ch.link(v.tensor_tensor(tend[:, e:e + 1], tend[:, e:e + 1], tend[:, e - 1:e], ALU.add))
                ch.link(v.tensor_tensor(tbase[:, :], tend[:, :], ntile[:, :], ALU.subtract))
                ch.link(v.tensor_scalar(tbase[:, :], tbase[:, :], float(P), None, ALU.mult))
                ch.link(v.tensor_tensor(pos[:, :, :], src[:, :, :], counts, ALU.subtract))
                ch.link(v.tensor_tensor(pos[:, :, :], pos[:, :, :], psX[0][:, 0:NB * NE].rearrange("p (b e) -> p b e", e=NE), ALU.add))
                ch.link(v.tensor_tensor(pos[:, :, :], pos[:, :, :], tbase[:, :].unsqueeze(1).to_broadcast([P, NB, NE]), ALU.add))
                for i in range(2):
                    ch.link(v.tensor_tensor(chosen[:, :, :], pick[i][:, :, :], pos[:, :, :], ALU.mult))
                    ch.link(v.tensor_reduce(slot_f[:, :, i], chosen[:, :, :], AX, ALU.add))
                    v.tensor_copy(slot_by[i][:, :], slot_f[:, :, i])
                v.tensor_copy(slot[:, :], slot_f[:, :, :].rearrange("p b i -> p (b i)"))
                ch.link(v.tensor_tensor(after[:, :, :], tile_f[:, :].unsqueeze(2).to_broadcast([1, TM, NE]),
                                        tend[0:1, :].unsqueeze(1).to_broadcast([1, TM, NE]), ALU.is_ge))
                ch.link(v.tensor_reduce(expert_f[:, :], after[:, :, :], AX, ALU.add))
                v.tensor_scalar(expert[:, :], expert_f[:, :], float(NE - 1), None, ALU.min).then_inc(s_slot, 1)
                dve.wait_ge(s_tok, 16)
                v.tensor_copy(trow_f[:, :], trow_i[:, :]).then_inc(s_tf, 1)
                dve.wait_ge(s_tp, 1)
                v.tensor_copy(tnode[:, :], psD[0][:, 0:TM]).then_inc(s_tn, 1)
                dve.wait_ge(s_w, 64)
                ch.restart()

                def add_bias(c, j):
                    e = expert_of(dve, c * 4 + j)
                    dve.wait_ge(s_up, c * 4 + (j + 3))
                    dve.wait_ge(s_H, c * 4 + (j + 1))
                    v.tensor_tensor(hrow[:, j % 2, :], psU[j % 2][:, :], b1[:, bass.ds(e * HID, HID)], ALU.add).then_inc(s_hr, 1)

                add_bias(0, 0)
                add_bias(0, 1)

                def output(c, j, last):
                    if not last or j + 2 < 4:
                        add_bias(c + (j + 2) // 4, (j + 2) % 4)
                    e = expert_of(dve, c * 4 + j)
                    dve.wait_ge(s_dn, c * 4 + (j + 3))
                    dve.wait_ge(s_ys[j], c * 16 + 16)
                    v.tensor_tensor(y[:, j, :], psD[j % 2][:, 0:D], b2[:, bass.ds(e * D, D)], ALU.add).then_inc(s_y, 1)

                rounds(dve, output)

                def combine(sb, nb, par, it):
                    dve.wait_ge(s_x3[par], it * 16 + 16)
                    dve.wait_ge(s_yg[par], it * 128 + 32 * nb)
                    for i in range(2):
                        for j in range(nb):
                            last = v.scalar_tensor_tensor(x3[:, par, j, :], yg[:, par, 2 * j + i, :], share[i][:, bass.ds(sb * 4 + j, 1)],
                                                          x3[:, par, j, :], ALU.mult, ALU.add)
                        if i == 0:
                            ch.link(last)
                    last.then_inc(s_done, 1)
                    ch.restart()

                halves(dve, combine)

            @block.tensor
            def _(pe):
                mm = nc.tensor.matmul
                pe.sem_inc(s_T, 4)
                pe.sem_inc(s_up, 2)
                pe.sem_inc(s_H, 2)
                pe.sem_inc(s_dn, 2)
                pe.wait_ge(s_both, 1)
                choices = both[:, :, :].rearrange("p b e -> p (b e)")
                mm(psX[0][:, 0:NB * NE], tri[:, :], choices, start=True, stop=True)
                mm(psX[1][:, 0:NB * NE], ones[:, :], choices, start=True, stop=True).then_inc(s_cnt, 1)
                pe.wait_ge(s_tf, 1)
                nc.tensor.transpose(psD[0][:, 0:TM], trow_f[:, :], ident[0:TM, 0:TM]).then_inc(s_tp, 1)
                pe.wait_ge(s_tn, 1)
                pe.wait_ge(s_w, 64)

                def rows_transposed(c, j):
                    pe.wait_ge(s_xs[j], c * 16 + 16)
                    pe.wait_ge(s_xT, c * 4 + (j + 1))
                    for k in range(KD):
                        last = nc.tensor.transpose(psX[j % 2][:, k * P:(k + 1) * P], xs[:, j, k * P:(k + 1) * P], ident[:, :])
                    last.then_inc(s_T, 1)

                def up(c, j):
                    e = expert_of(pe, c * 4 + j)
                    pe.wait_ge(s_xT, c * 4 + (j + 3))
                    pe.wait_ge(s_hr, c * 4 + (j + 1))
                    for k in range(KD):
                        last = mm(psU[j % 2][:, :], xT[:, j % 2, k, :], w1[:, bass.ds(e, 1), k, :], start=k == 0, stop=k == KD - 1)
                    last.then_inc(s_up, 1)

                def hidden_transposed(c, j):
                    pe.wait_ge(s_hr, c * 4 + (j + 3))
                    pe.wait_ge(s_h, c * 4 + (j + 1))
                    for m in range(KH):
                        last = nc.tensor.transpose(psH[j % 2][:, m * P:(m + 1) * P], hrow[:, j % 2, m * P:(m + 1) * P], ident[:, :])
                    last.then_inc(s_H, 1)

                def down(c, j):
                    e = expert_of(pe, c * 4 + j)
                    pe.wait_ge(s_h, c * 4 + (j + 3))
                    pe.wait_ge(s_y, c * 4 + (j + 1))
                    for k in range(KH):
                        last = mm(psD[j % 2][:, 0:D], hT[:, j % 2, k, :], w2[:, bass.ds(e, 1), k, :], start=k == 0, stop=k == KH - 1)
                    last.then_inc(s_dn, 1)

                for j in range(3):
                    rows_transposed(0, j)
                up(0, 0)
                up(0, 1)
                hidden_transposed(0, 0)

                def step(c, j, last):
                    if not last or j + 3 < 4:
                        rows_transposed(c + (j + 3) // 4, (j + 3) % 4)
                    if not last or j + 2 < 4:
                        up(c + (j + 2) // 4, (j + 2) % 4)
                    if not last or j + 1 < 4:
                        hidden_transposed(c + (j + 1) // 4, (j + 1) % 4)
                    down(c, j)

                rounds(pe, step)


def kernel(**inputs):
    import numpy as _np
    import concourse.bacc as _bacc
    from concourse import mybir as _mybir
    from concourse.bass_utils import run_bass_kernel_spmd as _run

    nc = _bacc.Bacc("TRN2", target_bir_lowering=False, num_devices=1)
    arrays, args = {}, {}
    for name, value in inputs.items():
        array = _np.ascontiguousarray(_np.atleast_1d(_np.asarray(value)))
        arrays[f"in_{name}_dram"] = array
        args[name] = nc.dram_tensor(f"in_{name}_dram", array.shape, _mybir.dt.from_np(array.dtype), kind="ExternalInput").ap()
    out = nc.dram_tensor("out_0_dram", (N, D), FP32, kind="ExternalOutput").ap()
    build(nc, args, out)
    result = _run(nc, [arrays], core_ids=[0])
    return result.results[0]["out_0_dram"]
```
